# Optimizing a Trainium2 kernel written in Bass

```python
import numpy as np
import jax
import jax.numpy as jnp

def _softmax(x, axis=-1):
    return jax.nn.softmax(x, axis=axis)

def _gelu(x):
    return jax.nn.gelu(x, approximate=True)

def _silu(x):
    return jax.nn.silu(x)

def _sigmoid(x):
    return jax.nn.sigmoid(x)

def _layernorm(x, axis=-1, eps=1e-05):
    m = jnp.mean(x, axis=axis, keepdims=True)
    v = jnp.var(x, axis=axis, keepdims=True)
    return (x - m) / jnp.sqrt(v + eps)

def _scatter_add(tgt, idx, src, axis=0):
    return tgt.at[idx].add(src)

def _segment_sum(src, seg, n):
    return jax.ops.segment_sum(src, seg, n)
kernel_name = 'mk_gnn_resnorm_d4_gnn_r8_3fb17f'

def setup_inputs(seed: int=0):
    np.random.seed(seed)
    _w = jnp.asarray

    def _rec_inputs():
        import jax
        import jax.numpy as jnp
        _gk = jax.random.key(seed)
        x = -0.0005121 + 1.001 * jax.random.normal(jax.random.fold_in(_gk, 1), (6250, 64), jnp.float32)
        _s = jax.random.randint(jax.random.fold_in(_gk, 2), (100000,), 0, 6250, jnp.int32)
        _d = jax.random.randint(jax.random.fold_in(_gk, 3), (100000,), 0, 6250, jnp.int32)
        _loop = jnp.arange(6250, dtype=jnp.int32)
        src = jnp.concatenate([_s, _d, _loop])
        dst = jnp.concatenate([_d, _s, _loop])
        _o = jnp.argsort(dst, stable=True)
        src = src[_o]
        dst = dst[_o]
        edge_attr_64 = -6.74381e-05 + 0.999835 * jax.random.normal(jax.random.fold_in(_gk, 12), (206250, 64), jnp.float32)
        return (x, src, dst, edge_attr_64)
    x, src, dst, edge_attr_64 = _rec_inputs()

    def _L0_gnn_setup():
        import jax, jax.numpy as jnp
        import numpy as np
        N_NODES = 6250
        N_EDGES = 156250
        D_NODE = 64
        D_EDGE = 64
        M_OUT = 64
        U_OUT = 64
        key = jax.random.key(seed)
        k1, k2, k3, k4, k5, k6 = jax.random.split(key, 6)
        H = jax.random.normal(k1, (N_NODES, D_NODE), dtype=jnp.float32)
        Xe = jax.random.normal(k2, (N_EDGES, D_EDGE), dtype=jnp.float32)
        id_Xe = jax.random.randint(k3, (2, N_EDGES), 0, N_NODES, dtype=jnp.int64)
        M_W = jax.random.normal(k4, (M_OUT, D_NODE + D_EDGE), dtype=jnp.float32) * 0.05
        M_b = jnp.zeros((M_OUT,), dtype=jnp.float32)
        U_W = jax.random.normal(k5, (U_OUT, D_NODE + M_OUT), dtype=jnp.float32) * 0.05
        U_b = jnp.zeros((U_OUT,), dtype=jnp.float32)
        return {'H': H, 'Xe': Xe, 'id_Xe': id_Xe, 'M_W': M_W, 'M_b': M_b, 'U_W': U_W, 'U_b': U_b}
    _L0_gnn_all = _L0_gnn_setup()
    _L0_gnn_in = {k: v for k, v in _L0_gnn_all.items() if k in ('M_W', 'M_b', 'U_W', 'U_b')}
    del _L0_gnn_all

    def _L1_gnn_setup():
        import jax, jax.numpy as jnp
        import numpy as np
        N_NODES = 12500
        N_EDGES = 125000
        F_IN = 64
        F_HID = 32

        def gcn_conv(x, W, b, src, dst, n):
            h = x @ W
            ones = jnp.ones(src.shape[0], dtype=h.dtype)
            deg = jax.ops.segment_sum(ones, dst, num_segments=n) + 1.0
            dis = jax.lax.rsqrt(deg)
            norm = dis[src] * dis[dst]
            agg = jax.ops.segment_sum(h[src] * norm[:, None], dst, num_segments=n)
            agg = agg + h * (dis * dis)[:, None]
            return agg + b
        key = jax.random.key(seed)
        k = jax.random.split(key, 6)
        x = jax.random.normal(k[0], (N_NODES, F_IN), dtype=jnp.float32)
        edge_index = jax.random.randint(k[1], (2, N_EDGES), 0, N_NODES, dtype=jnp.int32)
        W1 = jax.random.normal(k[2], (F_IN, F_HID), dtype=jnp.float32) / np.sqrt(F_IN)
        b1 = jax.random.normal(k[3], (F_HID,), dtype=jnp.float32) * 0.01
        W2 = jax.random.normal(k[4], (F_HID, F_IN), dtype=jnp.float32) / np.sqrt(F_HID)
        b2 = jax.random.normal(k[5], (F_IN,), dtype=jnp.float32) * 0.01
        return {'x': x, 'edge_index': edge_index, 'W1': W1, 'b1': b1, 'W2': W2, 'b2': b2}
    _L1_gnn_all = _L1_gnn_setup()
    _L1_gnn_in = {k: v for k, v in _L1_gnn_all.items() if k in ('W1', 'b1', 'W2', 'b2')}
    del _L1_gnn_all

    def _L2_gnn_setup():
        import jax, jax.numpy as jnp
        import numpy as np
        N_NODES = 12500
        N_EDGES = 200000
        H, D = (4, 16)
        DE = 16
        DIN_N = 64
        DIN_E = 64
        key = jax.random.key(seed)
        ks = jax.random.split(key, 9)
        return {'inputs_node': jax.random.normal(ks[0], (N_NODES, DIN_N), dtype=jnp.float32), 'inputs_edge': jax.random.normal(ks[1], (N_EDGES, DIN_E), dtype=jnp.float32), 'src': jax.random.randint(ks[2], (N_EDGES,), 0, N_NODES, dtype=jnp.int32), 'dst': jax.random.randint(ks[3], (N_EDGES,), 0, N_NODES, dtype=jnp.int32), 'W_node': jax.random.normal(ks[4], (DIN_N, H * D), dtype=jnp.float32) * (1.0 / np.sqrt(DIN_N)), 'W_edge': jax.random.normal(ks[5], (DIN_E, H * DE), dtype=jnp.float32) * (1.0 / np.sqrt(DIN_E)), 'attn_query': jax.random.normal(ks[6], (H, D), dtype=jnp.float32) * (1.0 / np.sqrt(D)), 'attn_key': jax.random.normal(ks[7], (H, D), dtype=jnp.float32) * (1.0 / np.sqrt(D)), 'attn_edge': jax.random.normal(ks[8], (H, DE), dtype=jnp.float32) * (1.0 / np.sqrt(DE)), 'bias': jnp.zeros((H * D,), dtype=jnp.float32)}
    _L2_gnn_all = _L2_gnn_setup()
    _L2_gnn_in = {k: v for k, v in _L2_gnn_all.items() if k in ('W_node', 'W_edge', 'attn_query', 'attn_key', 'attn_edge', 'bias')}
    del _L2_gnn_all

    def _L3_gnn_setup():
        import jax, jax.numpy as jnp
        import numpy as np
        N = 12500
        E = 150000
        D = 64
        EPS = 1e-05

        def gcn_conv(x, src, dst, W, b):
            xw = x @ W
            deg = jnp.zeros((x.shape[0],), x.dtype).at[dst].add(1.0) + 1.0
            dinv = jax.lax.rsqrt(deg)
            norm = dinv[src] * dinv[dst]
            agg = jnp.zeros_like(xw).at[dst].add(norm[:, None] * xw[src])
            agg = agg + (dinv * dinv)[:, None] * xw
            return agg + b

        def batchnorm(x, gamma, beta):
            mu = x.mean(axis=0)
            var = x.var(axis=0)
            return gamma * (x - mu) * jax.lax.rsqrt(var + EPS) + beta
        key = jax.random.key(seed)
        ks = jax.random.split(key, 5)
        x = jax.random.normal(ks[0], (N, D), dtype=jnp.float32)
        edge_index = jax.random.randint(ks[1], (2, E), 0, N, dtype=jnp.int32)
        W1 = jax.random.normal(ks[2], (D, D), dtype=jnp.float32) * (1.0 / np.sqrt(D))
        W2 = jax.random.normal(ks[3], (D, D), dtype=jnp.float32) * (1.0 / np.sqrt(D))
        return {'x': x, 'edge_index': edge_index, 'W1': W1, 'b1': jnp.zeros((D,), jnp.float32), 'gamma1': jnp.ones((D,), jnp.float32), 'beta1': jnp.zeros((D,), jnp.float32), 'W2': W2, 'b2': jnp.zeros((D,), jnp.float32), 'gamma2': jnp.ones((D,), jnp.float32), 'beta2': jnp.zeros((D,), jnp.float32)}
    _L3_gnn_all = _L3_gnn_setup()
    _L3_gnn_in = {k: v for k, v in _L3_gnn_all.items() if k in ('W1', 'b1', 'gamma1', 'beta1', 'W2', 'b2', 'gamma2', 'beta2')}
    del _L3_gnn_all
    return {'x': x, 'src': src, 'dst': dst, 'edge_attr_64': edge_attr_64, 'L0_gnn_M_W': _L0_gnn_in['M_W'], 'L0_gnn_M_b': _L0_gnn_in['M_b'], 'L0_gnn_U_W': _L0_gnn_in['U_W'], 'L0_gnn_U_b': _L0_gnn_in['U_b'], 'L1_gnn_W1': _L1_gnn_in['W1'], 'L1_gnn_b1': _L1_gnn_in['b1'], 'L1_gnn_W2': _L1_gnn_in['W2'], 'L1_gnn_b2': _L1_gnn_in['b2'], 'L2_gnn_W_node': _L2_gnn_in['W_node'], 'L2_gnn_W_edge': _L2_gnn_in['W_edge'], 'L2_gnn_attn_query': _L2_gnn_in['attn_query'], 'L2_gnn_attn_key': _L2_gnn_in['attn_key'], 'L2_gnn_attn_edge': _L2_gnn_in['attn_edge'], 'L2_gnn_bias': _L2_gnn_in['bias'], 'L3_gnn_W1': _L3_gnn_in['W1'], 'L3_gnn_b1': _L3_gnn_in['b1'], 'L3_gnn_gamma1': _L3_gnn_in['gamma1'], 'L3_gnn_beta1': _L3_gnn_in['beta1'], 'L3_gnn_W2': _L3_gnn_in['W2'], 'L3_gnn_b2': _L3_gnn_in['b2'], 'L3_gnn_gamma2': _L3_gnn_in['gamma2'], 'L3_gnn_beta2': _L3_gnn_in['beta2']}

def reference(x, src, dst, edge_attr_64, L0_gnn_M_W, L0_gnn_M_b, L0_gnn_U_W, L0_gnn_U_b, L1_gnn_W1, L1_gnn_b1, L1_gnn_W2, L1_gnn_b2, L2_gnn_W_node, L2_gnn_W_edge, L2_gnn_attn_query, L2_gnn_attn_key, L2_gnn_attn_edge, L2_gnn_bias, L3_gnn_W1, L3_gnn_b1, L3_gnn_gamma1, L3_gnn_beta1, L3_gnn_W2, L3_gnn_b2, L3_gnn_gamma2, L3_gnn_beta2):
    import jax
    import jax.numpy as jnp

    def _L0_gnn_ref(H, Xe, id_Xe, M_W, M_b, U_W, U_b):
        import jax, jax.numpy as jnp
        import numpy as np
        N_NODES = 6250
        N_EDGES = 156250
        D_NODE = 64
        D_EDGE = 64
        M_OUT = 64
        U_OUT = 64
        features = H[id_Xe[0]]
        M_in = jnp.concatenate([features, Xe], axis=1)
        Y = jax.nn.relu(M_in @ M_W.T + M_b)
        Z = jax.ops.segment_sum(Y, id_Xe[1], num_segments=H.shape[0])
        U_in = jnp.concatenate([H, Z], axis=1)
        H_next = jax.nn.relu(U_in @ U_W.T + U_b)
        return H_next

    def _L1_gnn_ref(x, edge_index, W1, b1, W2, b2):
        import jax, jax.numpy as jnp
        import numpy as np
        N_NODES = 12500
        N_EDGES = 125000
        F_IN = 64
        F_HID = 32

        def gcn_conv(x, W, b, src, dst, n):
            h = x @ W
            ones = jnp.ones(src.shape[0], dtype=h.dtype)
            deg = jax.ops.segment_sum(ones, dst, num_segments=n) + 1.0
            dis = jax.lax.rsqrt(deg)
            norm = dis[src] * dis[dst]
            agg = jax.ops.segment_sum(h[src] * norm[:, None], dst, num_segments=n)
            agg = agg + h * (dis * dis)[:, None]
            return agg + b
        src, dst = (edge_index[0], edge_index[1])
        n = x.shape[0]
        h = jax.nn.relu(gcn_conv(x, W1, b1, src, dst, n))
        return gcn_conv(h, W2, b2, src, dst, n)

    def _L2_gnn_ref(inputs_node, inputs_edge, src, dst, W_node, W_edge, attn_query, attn_key, attn_edge, bias):
        import jax, jax.numpy as jnp
        import numpy as np
        N_NODES = 12500
        N_EDGES = 200000
        H, D = (4, 16)
        DE = 16
        DIN_N = 64
        DIN_E = 64
        n = inputs_node.shape[0]
        hn = (inputs_node @ W_node).reshape(n, H, D)
        he = (inputs_edge @ W_edge).reshape(-1, H, DE)
        w_q = jnp.einsum('nhd,hd->nh', hn, attn_query)
        w_k = jnp.einsum('nhd,hd->nh', hn, attn_key)
        w_e = jnp.einsum('ehd,hd->eh', he, attn_edge)
        logits = jax.nn.leaky_relu(w_k[src] + w_q[dst] + w_e, negative_slope=0.01)
        seg_max = jax.ops.segment_max(logits, dst, num_segments=n)
        seg_max = jnp.where(jnp.isfinite(seg_max), seg_max, 0.0)
        ex = jnp.exp(logits - seg_max[dst])
        denom = jax.ops.segment_sum(ex, dst, num_segments=n)
        attn = ex / denom[dst]
        msg = hn[src] * attn[:, :, None]
        out = jax.ops.segment_sum(msg, dst, num_segments=n)
        out = out.reshape(n, H * D) + bias
        out = out + inputs_node
        return out

    def _L3_gnn_ref(x, edge_index, W1, b1, gamma1, beta1, W2, b2, gamma2, beta2):
        import jax, jax.numpy as jnp
        import numpy as np
        N = 12500
        E = 150000
        D = 64
        EPS = 1e-05

        def gcn_conv(x, src, dst, W, b):
            xw = x @ W
            deg = jnp.zeros((x.shape[0],), x.dtype).at[dst].add(1.0) + 1.0
            dinv = jax.lax.rsqrt(deg)
            norm = dinv[src] * dinv[dst]
            agg = jnp.zeros_like(xw).at[dst].add(norm[:, None] * xw[src])
            agg = agg + (dinv * dinv)[:, None] * xw
            return agg + b

        def batchnorm(x, gamma, beta):
            mu = x.mean(axis=0)
            var = x.var(axis=0)
            return gamma * (x - mu) * jax.lax.rsqrt(var + EPS) + beta
        src, dst = (edge_index[0], edge_index[1])
        h = gcn_conv(x, src, dst, W1, b1)
        h = jax.nn.leaky_relu(batchnorm(h, gamma1, beta1), 0.01)
        h = gcn_conv(h, src, dst, W2, b2)
        h = jax.nn.leaky_relu(batchnorm(h, gamma2, beta2), 0.01)
        return h
    edge_index = jnp.stack([src, dst])
    x = _layernorm(x + _L0_gnn_ref(x, edge_attr_64, edge_index, L0_gnn_M_W, L0_gnn_M_b, L0_gnn_U_W, L0_gnn_U_b), axis=-1)
    x = _layernorm(x + _L1_gnn_ref(x, edge_index, L1_gnn_W1, L1_gnn_b1, L1_gnn_W2, L1_gnn_b2), axis=-1)
    x = _layernorm(x + _L2_gnn_ref(x, edge_attr_64, src, dst, L2_gnn_W_node, L2_gnn_W_edge, L2_gnn_attn_query, L2_gnn_attn_key, L2_gnn_attn_edge, L2_gnn_bias), axis=-1)
    x = _layernorm(x + _L3_gnn_ref(x, edge_index, L3_gnn_W1, L3_gnn_b1, L3_gnn_gamma1, L3_gnn_beta1, L3_gnn_W2, L3_gnn_b2, L3_gnn_gamma2, L3_gnn_beta2), axis=-1)
    return x

_drawn_inputs = setup_inputs


def setup_inputs(seed=0):
    import zlib

    import numpy as np

    out = dict(_drawn_inputs(seed))
    spreads = {'L0_gnn_M_b': (0.0, 0.1),
     'L0_gnn_U_b': (0.0, 0.268),
     'L2_gnn_bias': (0.0, 0.1),
     'L3_gnn_b1': (0.0, 0.8),
     'L3_gnn_gamma1': (1.0, 0.2),
     'L3_gnn_beta1': (0.0, 0.1),
     'L3_gnn_b2': (0.0, 0.8),
     'L3_gnn_gamma2': (1.0, 0.2),
     'L3_gnn_beta2': (0.0, 0.1)}
    factors = {'L1_gnn_b1': 8.0, 'L1_gnn_b2': 5.483}
    for name, (base, spread) in spreads.items():
        noise = np.random.default_rng([zlib.crc32(name.encode()), seed]).standard_normal(out[name].shape)
        drawn = base * np.exp(spread * noise) if base else spread * noise
        out[name] = jnp.asarray(drawn.astype(out[name].dtype))
    for name, factor in factors.items():
        out[name] = (out[name] * factor).astype(out[name].dtype)
    return out
```

```python
import concourse.bass as bass
from concourse import mybir
from contextlib import ExitStack

F32 = mybir.dt.float32
BF16 = mybir.dt.bfloat16
I32 = mybir.dt.int32
ALU = mybir.AluOpType
ACT = mybir.ActivationFunctionType
AX = mybir.AxisListType.X

P = 125
D = 64
HEADS = 4
HD = D // HEADS
BIG = 1.0e30
GROUP = 3
BANK = 512
U = 22
BUFS = 3
PAIRS = U // 2
EPS = 1e-5
AW = HD + 1
ROW2 = HEADS * AW


def gnn_kernel(nc, a, out):
    N, E = a["x"].shape[0], a["src"].shape[0]
    B, J = N // P, E // P
    CHUNKS = J // U
    ITER = CHUNKS // BUFS
    assert B * P == N and J * P == E and CHUNKS * U == J and ITER * BUFS == CHUNKS

    ctx = ExitStack()
    with ctx:
        def sb(name, shape, dt=F32):
            return ctx.enter_context(nc.sbuf_tensor(name, shape, dt))

        sems = {}

        def S(name):
            if name not in sems:
                sems[name] = ctx.enter_context(nc.semaphore(name))
            return sems[name]

        def dram(name, shape):
            return nc.dram_tensor(name, shape, F32, kind="Internal").ap()

        tables = [dram(f"table{r}", [N, w]) for r, w in enumerate((D, 32, 32, ROW2, D, D))]
        sums = [dram(f"sums{r}", [E, w]) for r, w in enumerate((D, 32, 32, ROW2 + HEADS, D, D))]
        query_table = dram("query_table", [N, HEADS])
        query_start = dram("query_start", [E + N, HEADS])

        srcI = sb("srcI", [P, J + BUFS * U], I32)
        keep = sb("keep", [P, J])
        edge_logit = sb("edge_logit", [P, J, HEADS])
        big = sb("big", [P, J * HEADS])
        cross_sel = sb("cross_sel", [P, N])
        X = sb("X", [P, B, D])
        Tflat = sb("Tflat", [P, B * (D + 2 * HEADS)])
        Zflat = sb("Zflat", [P, B * (ROW2 + HEADS)])
        tmpf = sb("tmpf", [P, B * (ROW2 + HEADS + 1)])
        idx = [sb(f"idx{k}", [P, U], I32) for k in range(BUFS)]
        gath = [sb(f"gath{k}", [P, U * ROW2]) for k in range(BUFS)]
        keepc = sb("keepc", [P, U])
        gate = sb("gate", [1, 8])
        factor = sb("factor", [P, ROW2 * (U + 1)])
        values = sb("values", [P, ROW2 * (U + 1)])
        runs = sb("runs", [P, ROW2 * (U + 1)])
        rows = sb("rows", [P, U * (ROW2 + HEADS)])
        xT = sb("xT", [128, PAIRS, P])
        lin_in = [xT[:, 4 * i:4 * i + GROUP, :] for i in range(2)]
        ident = sb("ident", [128, 128])
        ones = sb("ones", [P, P])
        tri = sb("tri", [P, P])
        iotaP = sb("iotaP", [P, P], BF16)
        iotaB = sb("iotaB", [P, B], BF16)
        node_no = sb("node_no", [P, B])
        prep = xT[:, :, :].rearrange("p u n -> p (u n)")
        srcG, srcE, srcU = prep[:, 0:128], prep[:, 128:256], prep[0:D, 256:384]
        WG = sb("WG", [128, 128])
        WE = sb("WE", [128, 2 * (D + HEADS)])
        WU = sb("WU", [128, D])
        WN = sb("WN", [128, 2 * (D + 2 * HEADS)])
        W11 = sb("W11", [128, D])
        W12 = sb("W12", [128, 128])
        W31 = sb("W31", [128, 128])
        W32 = sb("W32", [128, 128])
        w_edge2, w_node2, wtmp = prep[:, 384:384 + D], prep[:, 448:448 + D], prep[:, 512:512 + D]
        attn = prep[:, 576:576 + 3 * D].rearrange("p (m n) -> p m n", m=3)
        bias = sb("bias", [P, 11, D])
        deg = sb("deg", [P, B])
        dis = sb("dis", [P, B])
        mask = sb("mask", [P, B])
        cum = sb("cum", [P, B])
        nt = sb("nt", [P, 4, D])
        endI = sb("endI", [P, B], I32)
        startI = sb("startI", [P, B], I32)
        firstI = sb("firstI", [P, 2], I32)
        nextI = sb("nextI", [P, 2], I32)
        edge_ends = sb("edge_ends", [P, 4])
        rs_in = sb("rs_in", [P, D])
        rs_out = sb("rs_out", [P, D])
        w0 = sb("w0", [P, HEADS])
        mrun = sb("mrun", [P, HEADS, U + 1])
        logit = sb("logit", [P, U, HEADS])
        logitT = sb("logitT", [P, HEADS, U])
        keepn = sb("keepn", [P, U])
        expo = sb("expo", [P, 2, HEADS, U])
        bnd = sb("bnd", [P, ROW2 + HEADS + 1])
        bmax = sb("bmax", [P, 3, HEADS])

        xe = [big[:, k * U * D:(k + 1) * U * D] for k in range(BUFS)]
        o = BUFS * U * D
        hotP = big[:, o:o + U * P // 2].bitcast(BF16).rearrange("p (j n) -> p j n", j=U)
        o += U * P // 2 + 1
        hotB = big[:, o:o + U * B // 2].bitcast(BF16).rearrange("p (j n) -> p j n", j=U)
        assert o + U * B // 2 <= J * HEADS
        XZ = big[:, 0:B * 2 * D].rearrange("p (b f) -> p b f", b=B)
        query = big[:, :].rearrange("p (j h) -> p j h", h=HEADS)
        dstI = Zflat[:, 0:J].bitcast(I32)
        dstF = Zflat[:, J:2 * J]
        node_half = Zflat[:, 0:J].bitcast(BF16)
        pnode, bnode = node_half[:, 0:J], node_half[:, J:2 * J]

        ps = ctx.enter_context(nc.psum_tensor("ps", [128, 8, BANK], F32))

        def v3(t, w, n=B):
            return t[:, 0:n * w].rearrange("p (b f) -> p b f", b=n)

        def chunk3(t, w):
            return t[:, 0:U * w].rearrange("p (j f) -> p j f", j=U)

        def run3(t, w):
            return t[:, 0:w * (U + 1)].rearrange("p (f j) -> p f j", f=w)

        def rowsof(r, i, k):
            v = sums[r].rearrange("(p j) f -> p j f", p=P)
            return v[:, bass.ds(i * (BUFS * U) + k * U, U), :]

        PASSW = (D, 32, 32, ROW2, D, D)
        GCN_NO = {1: 0, 2: 1, 4: 2, 5: 3}
        CORRW = (D, 32, 32, ROW2 + HEADS + 1, D, D)

        def units(src, kind):
            if kind == "pair":
                return [src[:, 2 * u:2 * u + 2, :].rearrange("p b f -> p (b f)") for u in range(B // 2)]
            return [src[:, u, :] for u in range(B)]

        T64, T32, T72 = v3(Tflat, D), v3(Tflat, 32), v3(Tflat, D + 2 * HEADS)
        tmp64 = v3(tmpf, D)
        LINEARS = {
            "message": (units(X, "pair"), WG, 128),
            "update": (units(XZ, "one"), WU, D),
            "gcn11": (units(X, "pair"), W11, D),
            "gcn12": (units(tmp64, "pair"), W12, 128),
            "attend": (units(X, "pair"), WN, 2 * (D + 2 * HEADS)),
            "gcn31": (units(tmp64, "pair"), W31, 128),
            "gcn32": (units(tmp64, "pair"), W32, 128),
        }
        ORDER = list(LINEARS)
        group_base, g0 = {}, 0
        for name in ORDER:
            group_base[name] = g0
            g0 += -(-len(LINEARS[name][0]) // GROUP)

        def groups(name):
            us = LINEARS[name][0]
            return [us[i:i + GROUP] for i in range(0, len(us), GROUP)]

        BIASES = ("L0_gnn_M_b", "L0_gnn_U_b", "L1_gnn_b1", "L1_gnn_b2", "L2_gnn_bias", "L3_gnn_b1", "L3_gnn_gamma1",
                  "L3_gnn_beta1", "L3_gnn_b2", "L3_gnn_gamma2", "L3_gnn_beta2")
        W_LOADS = 18 + 4 + len(BIASES)

        block = ctx.enter_context(nc.Block())

        @block.sync
        def _(sp):
            def load(dst, src, sem="loaded"):
                sp.dma_start(dst, src).then_inc(S(sem), 16)

            load(srcI[:, 0:J], a["src"].rearrange("(p j) -> p j", p=P), "loaded_idx")
            load(dstI, a["dst"].rearrange("(p j) -> p j", p=P), "loaded_idx")
            dst2 = a["dst"].rearrange("(p j) -> p j", p=P)
            load(firstI[:, :], dst2[:, 0:2], "loaded_idx")
            sp.wait_ge(S("zeroed"), 1)
            load(nextI[0:P - 1, :], dst2[1:P, 0:2], "loaded_idx")
            load(X[:, :, :], a["x"].rearrange("(p b) f -> p b f", p=P), "loaded_x")
            n = 0
            for h in range(2):
                lo, hi = D * h, D * h + D
                for dst, src in (
                    (srcG[lo:hi, lo:hi], a["L0_gnn_M_W"][:, 0:D]),
                    (srcE[lo:hi, lo:hi], a["L0_gnn_M_W"][:, D:2 * D]),
                    (W11[lo:hi, 32 * h:32 * h + 32], a["L1_gnn_W1"]),
                    (W12[lo:lo + 32, lo:hi], a["L1_gnn_W2"]),
                    (WN[lo:hi, 72 * h:72 * h + D], a["L2_gnn_W_node"]),
                    (W31[lo:hi, lo:hi], a["L3_gnn_W1"]),
                    (W32[lo:hi, lo:hi], a["L3_gnn_W2"]),
                    (w_edge2[lo:hi, :], a["L2_gnn_W_edge"]),
                    (w_node2[lo:hi, :], a["L2_gnn_W_node"]),
                ):
                    load(dst, src, "loaded_w")
                    n += 1
            load(srcU[:, :], a["L0_gnn_U_W"], "loaded_w")
            for m, name in enumerate(("edge", "key", "query")):
                row = a[f"L2_gnn_attn_{name}"].rearrange("(a h) d -> a (h d)", a=1)
                load(attn[:, m, :], row.to_broadcast([128, D]), "loaded_w")
            for m, name in enumerate(BIASES):
                v = a[name].rearrange("(a n) -> a n", a=1)
                w = v.shape[1]
                load(bias[:, m, 0:w], v.to_broadcast([P, w]), "loaded_w")
            assert n + 4 + len(BIASES) == W_LOADS

            def store_table(r, src):
                sp.wait_ge(S("table_ready"), r + 1)
                sp.dma_start(tables[r].rearrange("(p b) f -> p b f", p=P), src).then_inc(S("table"), 16)

            store_table(0, T64)
            edges = a["edge_attr_64"].rearrange("(p j) f -> p j f", p=P)
            with sp.Fori(0, ITER) as i:
                for k in range(BUFS):
                    sp.wait_ge(S("xe_used"), i * BUFS + (k + 1))
                    sp.dma_start(chunk3(xe[k], D), edges[:, bass.ds(i * (BUFS * U) + k * U, U), :]).then_inc(S(f"xe{k}"), 16)
            store_table(1, T32)
            store_table(2, T32)
            sp.wait_ge(S("table_ready"), 4)
            sp.dma_start(tables[3].rearrange("(p b) f -> p b f", p=P), T72[:, :, 0:ROW2]).then_inc(S("table"), 16)
            sp.dma_start(query_table.rearrange("(p b) f -> p b f", p=P), T72[:, :, ROW2:ROW2 + HEADS]).then_inc(S("query_table"), 16)
            sp.dma_start(query_start[0:E, :].rearrange("(p j) h -> p (j h)", p=P), big[:, :]).then_inc(S("query_zero"), 16)
            sp.wait_ge(S("query_put"), 16 * B)
            sp.dma_start(big[:, :], query_start[0:E, :].rearrange("(p j) h -> p (j h)", p=P)).then_inc(S("query_back"), 16)
            store_table(4, T64)
            store_table(5, T64)
            sp.wait_ge(S("result"), 1)
            sp.dma_start(out.rearrange("(p b) f -> p b f", p=P), X[:, :, :]).then_inc(S("out"), 16)
            sp.wait_ge(S("out"), 16)

        @block.gpsimd
        def _(g):
            g.memset(ident[:, :], 0.0).then_inc(S("pool_const"), 1)
            g.memset(ones[:, :], 1.0).then_inc(S("pool_const"), 1)
            g.memset(gate[:, :], 1.0).then_inc(S("pool_const"), 1)
            g.iota(iotaP[:, :], pattern=[[1, P]], base=0, channel_multiplier=0, allow_small_or_imprecise_dtypes=True).then_inc(S("pool_const"), 1)
            g.iota(iotaB[:, :], pattern=[[1, B]], base=0, channel_multiplier=0, allow_small_or_imprecise_dtypes=True).then_inc(S("pool_const"), 1)
            g.iota(node_no[:, :], pattern=[[1, B]], base=0, channel_multiplier=B, allow_small_or_imprecise_dtypes=True).then_inc(S("pool_const"), 1)
            g.iota(cross_sel[:, :], pattern=[[1, N]], base=0, channel_multiplier=0, allow_small_or_imprecise_dtypes=True).then_inc(S("pool_const"), 1)
            g.wait_ge(S("pool_const"), 7)
            g.affine_select(out=ident[:, :], in_=ident[:, :], compare_op=ALU.not_equal, fill=1.0, base=0,
                            pattern=[[-1, 128]], channel_multiplier=1).then_inc(S("pool_const"), 1)
            g.affine_select(out=tri[:, :], in_=ones[:, :], compare_op=ALU.is_gt, fill=0.0, base=0,
                            pattern=[[1, P]], channel_multiplier=-1).then_inc(S("pool_const"), 1)

            def gather(dst, table, index, sem):
                g.indirect_dma_start(out=dst, out_offset=None, in_=table,
                                     in_offset=bass.IndirectOffsetOnAxis(ap=index, axis=0)).then_inc(S(sem), 16)

            def edge_pass(r):
                w = PASSW[r]
                g.wait_ge(S("table"), 16 * (r + 1))
                with g.Fori(0, ITER) as i:
                    for k in range(BUFS):
                        g.wait_ge(S("gate_done"), i * BUFS + (r * CHUNKS + k + 1))
                        g.wait_ge(S("idx_ready"), i * BUFS + (r * CHUNKS + k + 1))
                        g.tensor_tensor(gate[:, 0:4], gate[:, 4:8], gate[:, 4:8], ALU.add).then_inc(S("gate_done"), 1)
                        for j in range(U):
                            gather(chunk3(gath[k], w)[:, j, :], tables[r], idx[k][:, j:j + 1], f"gathered{k}")

            def node_gather(r):
                w = sums[r].shape[1]
                g.wait_ge(S("stored"), 16 * (CHUNKS * (r + 1) + 1))
                g.wait_ge(S("ends_ready"), 1)
                g.wait_ge(S("z_free"), r + 1)
                for b in range(B):
                    gather(v3(Zflat, w)[:, b, :], sums[r], endI[:, b:b + 1], "nodes_gathered")

            g.sem_inc(S("gate_done"), 1)
            for r in range(6):
                if r == 3:
                    g.wait_ge(S("query_zero"), 16)
                    for b in range(B):
                        g.indirect_dma_start(out=query_start, out_offset=bass.IndirectOffsetOnAxis(ap=startI[:, b:b + 1], axis=0),
                                             in_=T72[:, b, ROW2:ROW2 + HEADS], in_offset=None).then_inc(S("query_put"), 16)
                    g.wait_ge(S("query_table"), 16)
                    gather(w0[:, :], query_table, firstI[:, 0:1], "query_first")
                edge_pass(r)
                node_gather(r)

        @block.tensor
        def _(pe):
            def linear(name):
                _, w, ncol = LINEARS[name]
                gs, base = groups(name), group_base[name]
                pe.wait_ge(S("in_" + name), 1)

                def turn(n):
                    q = base + n
                    if q >= 2:
                        pe.wait_ge(S("lin_copied"), q - 1)
                    for i, u in enumerate(gs[n]):
                        last = pe.transpose(ps[:, q % 2, i * P:(i + 1) * P], u, ident[0:P, 0:P])
                    last.then_inc(S("lin_turned"), 1)

                turn(0)
                for n in range(len(gs)):
                    if n + 1 < len(gs):
                        turn(n + 1)
                    q = base + n
                    pe.wait_ge(S("lin_copied"), q + 1)
                    if q >= 2:
                        pe.wait_ge(S("lin_taken"), q - 1)
                    for i in range(len(gs[n])):
                        last = pe.matmul(ps[0:P, 2 + q % 2, i * ncol:(i + 1) * ncol], lin_in[q % 2][:, i, :], w[:, 0:ncol],
                                         start=True, stop=True)
                    last.then_inc(S("lin_done"), 1)

            def crossing(r, rhs):
                w = CORRW[r]
                per = min(8, BANK // w)
                pe.wait_ge(S("cross_in"), r + 1)
                for b in range(B):
                    last = pe.matmul(ps[0:P, b // per, (b % per) * w:(b % per + 1) * w], cross_sel[:, b:N:B], rhs,
                                     start=True, stop=True)
                last.then_inc(S("cross_out"), 1)

            def column_sums(n):
                pe.wait_ge(S("colsum_in"), n + 1)
                pe.matmul(ps[0:P, 7, 0:D], ones[:, :], nt[:, 0, :], start=True, stop=True).then_inc(S("colsum_out"), 1)

            pe.wait_ge(S("loaded_w"), 16 * W_LOADS)
            pe.wait_ge(S("pool_const"), 9)
            pe.transpose(ps[:, 0, 0:128], srcG[:, :], ident[:, :])
            pe.transpose(ps[:, 1, 0:128], srcE[:, :], ident[:, :])
            pe.transpose(ps[:, 2, 0:D], srcU[:, :], ident[0:D, 0:D]).then_inc(S("w_turned"), 1)

            linear("message")

            pe.wait_ge(S("hist_zero"), 1)
            pe.matmul(ps[0:P, 7, 0:B], hotP[:, 0, :], hotB[:, 0, :], start=True, stop=False, skip_group_check=True).then_inc(S("hot_used"), 1)
            pe.sem_inc(S("xe_used"), BUFS)
            with pe.Fori(0, ITER) as i:
                for k in range(BUFS):
                    c = i * BUFS + k
                    pe.wait_ge(S(f"xe{k}"), i * 16 + 16)
                    pe.wait_ge(S("xt_copied"), c + 1)
                    for u in range(PAIRS):
                        last = pe.transpose(ps[:, u // 4, (u % 4) * P:(u % 4 + 1) * P],
                                            xe[k][:, u * 2 * D:(u + 1) * 2 * D], ident[0:P, 0:P])
                    last.then_inc(S("xe_used"), 1)
                    pe.wait_ge(S("xt_copied"), c + 2)
                    pe.wait_ge(S("edge_taken"), c + 1)
                    for u in range(PAIRS):
                        last = pe.matmul(ps[0:P, 3 + u // 3, (u % 3) * 136:(u % 3 + 1) * 136], xT[:, u, :], WE[:, :],
                                         start=True, stop=True)
                    last.then_inc(S("edge_done"), 1)
                    pe.wait_ge(S("hot_ready"), c + 1)
                    for j in range(U):
                        last = pe.matmul(ps[0:P, 7, 0:B], hotP[:, j, :], hotB[:, j, :], start=False, stop=False,
                                         skip_group_check=True)
                    last.then_inc(S("hot_used"), 1)
            pe.wait_ge(S("cum_in"), 1)
            pe.matmul(ps[0:P, 7, D:D + 1], tri[:, :], cum[:, B - 1:B], start=True, stop=True).then_inc(S("cum_out"), 1)
            crossing(0, chunk3(rows, D)[:, U - 1, :])
            linear("update")
            linear("gcn11")
            crossing(1, chunk3(rows, 32)[:, U - 1, :])
            crossing(2, chunk3(rows, 32)[:, U - 1, :])
            linear("gcn12")
            linear("attend")
            pe.wait_ge(S("diag_ready"), 1)
            for m in range(6):
                last = pe.matmul(ps[0:P, m // 4, (m % 4) * P:(m % 4 + 1) * P], ones[:, :], v3(tmpf, P, 6)[:, m, :],
                                 start=True, stop=True)
            last.then_inc(S("diag_out"), 1)
            crossing(3, bnd[:, :])
            crossing(4, chunk3(rows, D)[:, U - 1, :])
            linear("gcn31")
            column_sums(0)
            column_sums(1)
            crossing(5, chunk3(rows, D)[:, U - 1, :])
            linear("gcn32")
            column_sums(2)
            column_sums(3)

        @block.scalar
        def _(act):
            def linear(name):
                base = group_base[name]
                for n, us in enumerate(groups(name)):
                    q = base + n
                    act.wait_ge(S("lin_turned"), q + 1)
                    if q >= 2:
                        act.wait_ge(S("lin_done"), q - 1)
                    w = len(us)
                    act.copy(lin_in[q % 2][:, 0:w, :], ps[:, q % 2, 0:w * P].rearrange("p (u n) -> p u n", u=w)).then_inc(S("lin_copied"), 1)

            root_n = [0]

            def root(w=B):
                root_n[0] += 1
                act.wait_ge(S("root_in"), root_n[0])
                act.activation(rs_out[:, 0:w], rs_in[:, 0:w], ACT.Sqrt).then_inc(S("root_out"), 1)

            def expand(r, c, w):
                act.wait_ge(S("keepc_ready"), c + (r * CHUNKS + 1))
                act.copy(run3(factor, w)[:, :, 1:U + 1],
                         keepc[:, :].unsqueeze(1).to_broadcast([P, w, U])).then_inc(S("factor_ready"), 1)

            def store_rows(r, i, k, w):
                c = i * BUFS + k
                act.wait_ge(S("scanned"), c + (r * CHUNKS + 1))
                act.wait_ge(S("stored"), (c + (r * CHUNKS + 1)) * 16)
                full = sums[r].shape[1]
                if full == w:
                    act.copy(chunk3(rows, w), run3(runs, w)[:, :, 1:U + 1].rearrange("p f j -> p j f")).then_inc(S("rows_ready"), 1)
                    act.wait_ge(S("rows_ready"), c + (r * CHUNKS + 2))
                else:
                    v = chunk3(rows, full)
                    act.copy(v[:, :, w:full], mrun[:, :, 1:U + 1].rearrange("p h j -> p j h")).then_inc(S("rows_max"), 1)
                    act.copy(v[:, :, 0:w], run3(runs, w)[:, :, 1:U + 1].rearrange("p f j -> p j f")).then_inc(S("rows_ready"), 1)
                    act.wait_ge(S("rows_max"), c + 1)
                    act.wait_ge(S("rows_ready"), c + (r * CHUNKS + 2))
                act.dma_start(rowsof(r, i, k), chunk3(rows, full)).then_inc(S("stored"), 16)

            act.sem_inc(S("stored"), 16)
            act.sem_inc(S("rows_ready"), 1)
            act.sem_inc(S("xt_copied"), 1)
            linear("message")
            with act.Fori(0, ITER) as i:
                for k in range(BUFS):
                    c = i * BUFS + k
                    expand(0, c, D)
                    act.wait_ge(S("xe_used"), c + (BUFS + 1))
                    act.wait_ge(S("edge_done"), c + 1)
                    for b in range(3):
                        n = min(4, PAIRS - 4 * b)
                        last = act.copy(xT[:, 4 * b:4 * b + n, :], ps[:, b, 0:n * P].rearrange("p (u n) -> p u n", u=n))
                    last.then_inc(S("xt_copied"), 1)
                    v = run3(values, D)[:, :, 1:U + 1]
                    act.wait_ge(S("values_ready"), c + 1)
                    act.activation(v, v, ACT.Relu).then_inc(S("messages_ready"), 1)
                    store_rows(0, i, k, D)
            root()
            act.wait_ge(S("x_fixed"), 1)
            act.copy(XZ[:, :, 0:D], X[:, :, :]).then_inc(S("xz_x"), 1)
            linear("update")
            root()
            linear("gcn11")
            for r in (1, 2):
                with act.Fori(0, ITER) as i:
                    for k in range(BUFS):
                        expand(r, i * BUFS + k, 32)
                        store_rows(r, i, k, 32)
            linear("gcn12")
            root()
            linear("attend")
            with act.Fori(0, ITER) as i:
                for k in range(BUFS):
                    c = i * BUFS + k
                    act.wait_ge(S("expo_in"), c + 1)
                    act.activation(expo[:, :, :, :], expo[:, :, :, :], ACT.Exp).then_inc(S("expo_out"), 1)
                    act.wait_ge(S("expo_out"), c + 1)
                    act.copy(run3(factor, ROW2).rearrange("p (h e) j -> p h e j", h=HEADS)[:, :, :, 1:U + 1],
                             expo[:, 0, :, :].unsqueeze(2).to_broadcast([P, HEADS, AW, U])).then_inc(S("factor_ready"), 1)
                    store_rows(3, i, k, ROW2)
            act.wait_ge(S("bexp_in"), 1)
            act.activation(bmax[:, 2, :], bmax[:, 2, :], ACT.Exp).then_inc(S("bexp_out"), 1)
            act.wait_ge(S("nexp_in"), 1)
            act.activation(Tflat[:, 0:2 * B * HEADS], Tflat[:, 0:2 * B * HEADS], ACT.Exp).then_inc(S("nexp_out"), 1)
            root()
            for r in (4, 5):
                with act.Fori(0, ITER) as i:
                    for k in range(BUFS):
                        expand(r, i * BUFS + k, D)
                        store_rows(r, i, k, D)
                linear("gcn31" if r == 4 else "gcn32")
                root(D)
            root()

        @block.vector
        def _(dve):
            done = [0]

            def do(ins):
                done[0] += 1
                ins.then_inc(S("dve"), 1)
                dve.wait_ge(S("dve"), done[0])

            def tell(name, n=1):
                dve.sem_inc(S(name), n)

            TT, TS, STT, CP = dve.tensor_tensor, dve.tensor_scalar, dve.scalar_tensor_tensor, dve.tensor_copy

            def over(t, w):
                return t.unsqueeze(2).to_broadcast([P, t.shape[1], w])

            def row(t, n):
                return t.unsqueeze(1).to_broadcast([P, n, t.shape[1]])

            for t in (srcG, srcE, W11, W12, W31, W32, WE, WN):
                do(dve.memset(t[:, :], 0.0))
            do(dve.memset(nextI[:, :], -1))
            tell("zeroed")
            do(dve.memset(keep[:, 0:1], 0.0))
            do(dve.memset(factor[:, :], 0.0))
            do(dve.memset(hotP, 0.0))
            do(dve.memset(hotB, 0.0))
            tell("hist_zero")
            dve.wait_ge(S("loaded_idx"), 64)
            do(CP(srcI[:, J:J + BUFS * U], srcI[:, 0:BUFS * U]))
            do(CP(dstF, dstI))
            do(TT(keep[:, 1:J], dstF[:, 1:J], dstF[:, 0:J - 1], ALU.is_equal))
            q, rest, off, qI = tmpf[:, 0:J], tmpf[:, J:2 * J], Tflat[:, 0:J], Tflat[:, J:2 * J].bitcast(I32)
            do(TS(qI, dstF, 1.0 / B, -0.49, ALU.mult, ALU.add))
            do(CP(q, qI))
            do(STT(rest, q, -float(B), dstF, ALU.mult, ALU.add))
            do(TS(off, rest, 0.0, None, ALU.is_lt))
            do(TT(q, q, off, ALU.subtract))
            do(STT(rest, off, float(B), rest, ALU.mult, ALU.add))
            do(TS(off, rest, float(B), None, ALU.is_ge))
            do(TT(pnode[:, :], q, off, ALU.add))
            do(STT(bnode[:, :], off, -float(B), rest, ALU.mult, ALU.add))
            do(CP(edge_ends[:, 0:1], dstF[:, J - 1:J]))
            do(CP(edge_ends[:, 1:2], nextI[:, 0:1]))
            do(TT(edge_ends[:, 2:3], edge_ends[:, 0:1], edge_ends[:, 1:2], ALU.is_equal))
            dve.wait_ge(S("pool_const"), 9)
            do(TS(cross_sel[:, :], cross_sel[:, :], edge_ends[:, 0:1], edge_ends[:, 2:3], ALU.is_equal, ALU.mult))
            dve.wait_ge(S("w_turned"), 1)
            do(CP(WG[:, :], ps[:, 0, 0:128]))
            for h in range(2):
                lo, hi = D * h, D * h + D
                do(CP(WE[lo:hi, 68 * h:68 * h + D], ps[lo:hi, 1, lo:hi]))
            do(CP(WU[:, :], ps[:, 2, 0:D]))
            for m, (w, t, at, step) in enumerate(((w_edge2, WE, D, 68), (w_node2, WN, D, 72), (w_node2, WN, D + HEADS, 72))):
                do(TT(wtmp[:, :], w[:, :], attn[:, m, :], ALU.mult))
                for h in range(2):
                    lo, hi = D * h, D * h + D
                    do(dve.tensor_reduce(t[lo:hi, step * h + at:step * h + at + HEADS],
                                         wtmp[lo:hi, :].rearrange("p (h d) -> p h d", h=HEADS), AX, ALU.add))
            dve.wait_ge(S("loaded_x"), 16)
            tell("in_message")
            tell("z_free")

            def take(name, n, us, ins):
                dve.wait_ge(S("lin_done"), group_base[name] + n + 1)
                ins(n, us).then_inc(S("lin_taken"), 1)
                dve.wait_ge(S("lin_taken"), group_base[name] + n + 1)

            def product(name, op):
                ncol = LINEARS[name][2]
                per = 2 if len(LINEARS[name][0]) < B else 1
                for n, us in enumerate(groups(name)):
                    nb = len(us) * per
                    b0 = n * GROUP * per
                    v = ps[0:P, 2 + (group_base[name] + n) % 2, 0:len(us) * ncol].rearrange("p (b f) -> p b f", b=nb)
                    take(name, n, us, lambda n, us: op(v, b0, nb))

            def rsqrt(t, w=B):
                do(CP(rs_in[:, 0:w], t))
                tell("root_in")
                roots[0] += 1
                dve.wait_ge(S("root_out"), roots[0])
                y, z = nt[:, 2, 0:w], nt[:, 3, 0:w]
                do(dve.reciprocal(y, rs_out[:, 0:w]))
                do(TT(z, y, y, ALU.mult))
                do(TT(z, z, rs_in[:, 0:w], ALU.mult))
                do(TS(z, z, -0.5, 1.5, ALU.mult, ALU.add))
                do(TT(t, y, z, ALU.mult))

            roots = [0]

            def layer_norm():
                m, v = nt[:, 0, 0:B], nt[:, 1, 0:B]
                do(dve.tensor_reduce(m, X[:, :, :], AX, ALU.add))
                do(TS(m, m, 1.0 / D, None, ALU.mult))
                do(TT(X[:, :, :], X[:, :, :], over(m, D), ALU.subtract))
                do(TT(tmp64, X[:, :, :], X[:, :, :], ALU.mult))
                do(dve.tensor_reduce(v, tmp64, AX, ALU.add))
                do(TS(v, v, 1.0 / D, EPS, ALU.mult, ALU.add))
                rsqrt(v)
                do(TT(X[:, :, :], X[:, :, :], over(v, D), ALU.mult))

            def first_indices():
                for k in range(BUFS):
                    CP(idx[k][:, :], srcI[:, k * U:(k + 1) * U]).then_inc(S("idx_ready"), 1)
                dve.wait_ge(S("idx_ready"), BUFS)

            def next_indices(r, i, k):
                TS(idx[k][:, :], srcI[:, bass.ds(i * (BUFS * U) + (BUFS + k) * U, U)], 1, None, ALU.mult).then_inc(S("idx_ready"), 1)

            def copy_keep(r, i, k):
                c = i * BUFS + k
                TS(keepc[:, :], keep[:, bass.ds(i * (BUFS * U) + k * U, U)], 1.0, None, ALU.mult).then_inc(S("keepc_ready"), 1)

            def scan(r, c, w):
                gc = c + (r * CHUNKS + 1)
                dve.wait_ge(S("factor_ready"), gc)
                dve.wait_ge(S("rows_ready"), gc)
                dve.tensor_tensor_scan(runs[:, 0:w * (U + 1)], factor[:, 0:w * (U + 1)], values[:, 0:w * (U + 1)], 0.0,
                                       ALU.mult, ALU.add).then_inc(S("scanned"), 1)
                dve.wait_ge(S("scanned"), gc)
                CP(run3(values, w)[:, :, 0:1], run3(runs, w)[:, :, U:U + 1]).then_inc(S("carried"), 1)
                dve.wait_ge(S("carried"), gc)

            def gcn_pass(r):
                w = PASSW[r]
                do(dve.memset(values[:, :], 0.0))
                do(dve.memset(factor[:, :], 0.0))
                with dve.Fori(0, ITER) as i:
                    for k in range(BUFS):
                        c = i * BUFS + k
                        copy_keep(r, i, k)
                        dve.wait_ge(S(f"gathered{k}"), (i + (r * ITER + 1)) * (16 * U))
                        CP(run3(values, w)[:, :, 1:U + 1], chunk3(gath[k], w).rearrange("p j f -> p f j")).then_inc(S("values_ready"), 1)
                        dve.wait_ge(S("values_ready"), c + (r * CHUNKS + 1))
                        next_indices(r, i, k)
                        scan(r, c, w)

            def finish_sums(r):
                w = PASSW[r]
                dve.wait_ge(S("rows_ready"), (r + 1) * CHUNKS + 1)
                tell("cross_in")
                dve.wait_ge(S("nodes_gathered"), 16 * B * (r + 1))
                z = v3(Zflat, w)
                do(TT(z, z, over(mask[:, :], w), ALU.mult))
                dve.wait_ge(S("cross_out"), r + 1)
                for n in range(0, B, 8):
                    m = min(8, B - n)
                    do(TT(z[:, n:n + m, :], z[:, n:n + m, :], ps[0:P, n // 8, 0:m * w].rearrange("p (b f) -> p b f", b=m), ALU.add))
                return z

            product("message", lambda v, b0, nb: TT(T64[:, b0:b0 + nb, :], v, row(bias[:, 0, :], nb), ALU.add))
            tell("table_ready")
            do(dve.memset(values[:, :], 0.0))
            first_indices()
            tell("edge_taken")
            tell("edge_done")
            with dve.Fori(0, ITER) as i:
                for k in range(BUFS):
                    c = i * BUFS + k
                    cols = i * (BUFS * U) + k * U
                    copy_keep(0, i, k)
                    dve.wait_ge(S("hot_used"), c + 1)
                    TT(hotP, pnode[:, bass.ds(cols, U)].unsqueeze(2).to_broadcast([P, U, P]),
                       iotaP[:, :].unsqueeze(1).to_broadcast([P, U, P]), ALU.is_equal)
                    TT(hotB, bnode[:, bass.ds(cols, U)].unsqueeze(2).to_broadcast([P, U, B]),
                       iotaB[:, :].unsqueeze(1).to_broadcast([P, U, B]), ALU.is_equal).then_inc(S("hot_ready"), 1)
                    dve.wait_ge(S("edge_done"), c + 2)
                    for b in range(4):
                        n = 2 * min(3, PAIRS - 3 * b)
                        v = ps[0:P, 3 + b, 0:n * 68].rearrange("p (j f) -> p j f", j=n)
                        last = TS(edge_logit[:, bass.ds(cols + 6 * b, n), :], v[:, :, D:D + HEADS], 1.0, None, ALU.mult)
                    dve.wait_ge(S(f"gathered{k}"), (i + 1) * (16 * U))
                    g3 = chunk3(gath[k], D)
                    for b in range(4):
                        n = 2 * min(3, PAIRS - 3 * b)
                        v = ps[0:P, 3 + b, 0:n * 68].rearrange("p (j f) -> p f j", j=n)
                        last = TT(run3(values, D)[:, :, 1 + 6 * b:1 + 6 * b + n],
                                  g3[:, 6 * b:6 * b + n, :].rearrange("p j f -> p f j"), v[:, 0:D, :], ALU.add)
                    last.then_inc(S("values_ready"), 1)
                    dve.wait_ge(S("values_ready"), c + 1)
                    dve.sem_inc(S("edge_taken"), 1)
                    next_indices(0, i, k)
                    dve.wait_ge(S("messages_ready"), c + 1)
                    scan(0, c, D)

            dve.wait_ge(S("hot_used"), CHUNKS + 1)
            do(CP(deg[:, :], ps[0:P, 7, 0:B]))
            do(dve.tensor_tensor_scan(cum[:, :], ones[:, 0:B], deg[:, :], 0.0, ALU.mult, ALU.add))
            tell("cum_in")
            dve.wait_ge(S("cum_out"), 1)
            do(CP(nt[:, 0, 0:1], ps[0:P, 7, D:D + 1]))
            do(TS(cum[:, :], cum[:, :], nt[:, 0, 0:1], None, ALU.add))
            do(TS(endI[:, :], cum[:, :], -1.0, 0.0, ALU.add, ALU.max))
            tell("ends_ready")
            do(TS(mask[:, :], deg[:, :], 1.0, None, ALU.min))
            do(TT(cum[:, :], cum[:, :], deg[:, :], ALU.subtract))
            do(TT(cum[:, :], cum[:, :], mask[:, :], ALU.mult))
            do(TS(nt[:, 0, 0:B], mask[:, :], -1.0, 1.0, ALU.mult, ALU.add))
            do(TS(nt[:, 1, 0:B], node_no[:, :], float(E), None, ALU.add))
            do(TT(nt[:, 0, 0:B], nt[:, 0, 0:B], nt[:, 1, 0:B], ALU.mult))
            do(TT(startI[:, :], cum[:, :], nt[:, 0, 0:B], ALU.add))
            do(TS(dis[:, :], deg[:, :], 1.0, None, ALU.add))
            rsqrt(dis[:, :])
            tell("x_fixed")

            z = finish_sums(0)
            dve.wait_ge(S("xz_x"), 1)
            do(CP(XZ[:, :, D:2 * D], z))
            tell("z_free")
            tell("in_update")
            product("update", lambda v, b0, nb: TT(tmp64[:, b0:b0 + nb, :], v, row(bias[:, 1, :], nb), ALU.add))
            do(STT(X[:, :, :], tmp64, 0.0, X[:, :, :], ALU.max, ALU.add))
            layer_norm()

            tell("in_gcn11")
            product("gcn11", lambda v, b0, nb: TT(T32[:, b0:b0 + nb, :], v, over(dis[:, b0:b0 + nb], 32), ALU.mult))
            tell("table_ready")
            gcn_pass(1)
            z = finish_sums(1)
            do(TT(z, z, T32, ALU.add))
            do(TT(z, z, over(dis[:, :], 32), ALU.mult))
            do(TT(z, z, row(bias[:, 2, 0:32], B), ALU.add))
            do(STT(T32, z, 0.0, over(dis[:, :], 32), ALU.max, ALU.mult))
            tell("z_free")
            tell("table_ready")
            gcn_pass(2)
            do(dve.memset(tmp64, 0.0))
            z = finish_sums(2)
            do(TT(z, z, T32, ALU.add))
            do(TT(tmp64[:, :, 0:32], z, over(dis[:, :], 32), ALU.mult))
            tell("z_free")
            tell("in_gcn12")
            product("gcn12", lambda v, b0, nb: TT(X[:, b0:b0 + nb, :], X[:, b0:b0 + nb, :], v, ALU.add))
            do(TT(X[:, :, :], X[:, :, :], row(bias[:, 3, :], B), ALU.add))
            layer_norm()

            do(dve.memset(big[:, :], 0.0))
            tell("in_attend")
            product("attend", lambda v, b0, nb: CP(T72[:, b0:b0 + nb, :], v))
            tell("table_ready")
            dve.wait_ge(S("query_back"), 16)
            dve.wait_ge(S("query_first"), 16)
            do(CP(query[:, 0, :], w0[:, :]))
            for h in range(HEADS):
                do(dve.tensor_tensor_scan(query[:, :, h], keep[:, :], query[:, :, h], 0.0, ALU.mult, ALU.add))
            do(TT(edge_logit[:, :, :], edge_logit[:, :, :], query, ALU.add))
            do(dve.memset(values[:, :], 0.0))
            do(dve.memset(factor[:, :], 0.0))
            do(dve.memset(mrun[:, :, :], -BIG))
            loop_base, STEPS = done[0], 14
            with dve.Fori(0, ITER) as i:
                for k in range(BUFS):
                    c = i * BUFS + k
                    n = [0]

                    def ldo(ins):
                        n[0] += 1
                        ins.then_inc(S("dve"), 1)
                        dve.wait_ge(S("dve"), c * STEPS + (loop_base + n[0]))

                    cols = bass.ds(i * (BUFS * U) + k * U, U)
                    dve.wait_ge(S(f"gathered{k}"), (i + (3 * ITER + 1)) * (16 * U))
                    g3 = chunk3(gath[k], ROW2)
                    ldo(TT(logit[:, :, :], edge_logit[:, cols, :], g3[:, :, D:ROW2], ALU.add))
                    ldo(STT(logitT[:, :, :].rearrange("p h j -> p j h"), logit[:, :, :], 0.01, logit[:, :, :], ALU.mult, ALU.max))
                    ldo(TS(keepn[:, :], keep[:, cols], -1.0, BIG, ALU.add, ALU.mult))
                    dve.wait_ge(S("rows_ready"), c + (3 * CHUNKS + 1))
                    for h in range(HEADS):
                        ldo(dve.tensor_tensor_scan(mrun[:, h, 1:U + 1], keepn[:, :], logitT[:, h, :], mrun[:, h, 0:1], ALU.add, ALU.max))
                    ldo(TT(expo[:, 0, :, :], mrun[:, :, 0:U], keepn[:, :].unsqueeze(1).to_broadcast([P, HEADS, U]), ALU.add))
                    ldo(TT(expo[:, 0, :, :], expo[:, 0, :, :], mrun[:, :, 1:U + 1], ALU.subtract))
                    TT(expo[:, 1, :, :], logitT[:, :, :], mrun[:, :, 1:U + 1], ALU.subtract).then_inc(S("expo_in"), 1)
                    dve.wait_ge(S("expo_in"), c + 1)
                    dve.wait_ge(S("expo_out"), c + 1)
                    v4 = run3(values, ROW2).rearrange("p (h e) j -> p h e j", h=HEADS)
                    for h in range(HEADS):
                        ins = TT(v4[:, h, 0:HD, 1:U + 1], g3[:, :, h * HD:(h + 1) * HD].rearrange("p j d -> p d j"),
                                 expo[:, 1, h, :].unsqueeze(1).to_broadcast([P, HD, U]), ALU.mult)
                        if h < HEADS - 1:
                            ldo(ins)
                        else:
                            ins.then_inc(S("values_ready"), 1)
                            dve.wait_ge(S("values_ready"), c + (3 * CHUNKS + 1))
                    ldo(CP(v4[:, :, HD, 1:U + 1], expo[:, 1, :, :]))
                    next_indices(3, i, k)
                    scan(3, c, ROW2)
                    dve.wait_ge(S("rows_ready"), c + (3 * CHUNKS + 2))
                    ldo(CP(mrun[:, :, 0:1], mrun[:, :, U:U + 1]))
                    assert n[0] == STEPS
            done[0] = loop_base + CHUNKS * STEPS
            tell("keepc_ready", CHUNKS)
            last_row = chunk3(rows, ROW2 + HEADS)[:, U - 1, :]
            dm = v3(tmpf, P, 6)
            for m in range(6):
                col = last_row[:, ROW2 + m:ROW2 + m + 1] if m < HEADS else edge_ends[:, (0, 2)[m - HEADS]:(0, 2)[m - HEADS] + 1]
                do(TS(dm[:, m, :], ident[0:P, 0:P], col, None, ALU.mult))
            tell("diag_ready")
            dve.wait_ge(S("diag_out"), 1)
            same, t2 = dm[:, 0, :], dm[:, 1, :]
            do(TS(same, ps[0:P, 1, 0:P], edge_ends[:, 0:1], None, ALU.is_equal))
            do(TT(same, same, ps[0:P, 1, P:2 * P], ALU.mult))
            for h in range(HEADS):
                do(TT(t2, same, ps[0:P, 0, h * P:(h + 1) * P], ALU.mult))
                do(TS(dm[:, 2, :], same, -1.0, BIG, ALU.add, ALU.mult))
                do(TT(t2, t2, dm[:, 2, :], ALU.add))
                do(dve.tensor_reduce(bmax[:, 0, h:h + 1], t2, AX, ALU.max))
            do(TT(t2, same, tri[:, :], ALU.mult))
            do(dve.tensor_reduce(edge_ends[:, 3:4], t2, AX, ALU.max))
            do(TS(edge_ends[:, 3:4], edge_ends[:, 3:4], -1.0, 1.0, ALU.mult, ALU.add))
            do(TT(edge_ends[:, 3:4], edge_ends[:, 3:4], edge_ends[:, 2:3], ALU.mult))
            do(TT(bmax[:, 2, :], last_row[:, ROW2:ROW2 + HEADS], bmax[:, 0, :], ALU.subtract))
            do(TS(bmax[:, 2, :], bmax[:, 2, :], 0.0, None, ALU.min))
            tell("bexp_in")
            dve.wait_ge(S("bexp_out"), 1)
            do(TT(bnd[:, 0:ROW2].rearrange("p (h e) -> p h e", h=HEADS), last_row[:, 0:ROW2].rearrange("p (h e) -> p h e", h=HEADS),
                  bmax[:, 2, :].unsqueeze(2).to_broadcast([P, HEADS, AW]), ALU.mult))
            do(TS(bnd[:, ROW2:ROW2 + HEADS], bmax[:, 0, :], edge_ends[:, 3:4], None, ALU.mult))
            do(CP(bnd[:, ROW2 + HEADS:ROW2 + HEADS + 1], edge_ends[:, 3:4]))
            tell("cross_in")
            dve.wait_ge(S("cross_out"), 4)
            CW = CORRW[3]
            cr = v3(tmpf, CW)
            per = BANK // CW
            for n in range(0, B, per):
                m = min(per, B - n)
                do(CP(cr[:, n:n + m, :], ps[0:P, n // per, 0:m * CW].rearrange("p (b f) -> p b f", b=m)))
            dve.wait_ge(S("nodes_gathered"), 16 * B * 4)
            z = v3(Zflat, ROW2 + HEADS)
            e1, e2 = v3(Tflat, HEADS), Tflat[:, B * HEADS:2 * B * HEADS].rearrange("p (b h) -> p b h", b=B)
            mx = Tflat[:, 2 * B * HEADS:3 * B * HEADS].rearrange("p (b h) -> p b h", b=B)
            has = nt[:, 0, 0:B]
            do(TS(has, cr[:, :, ROW2 + HEADS], -1.0, BIG, ALU.add, ALU.mult))
            do(TT(e2, cr[:, :, ROW2:ROW2 + HEADS], over(has, HEADS), ALU.add))
            do(TT(mx, z[:, :, ROW2:ROW2 + HEADS], e2, ALU.max))
            do(TT(e1, z[:, :, ROW2:ROW2 + HEADS], mx, ALU.subtract))
            do(TT(e2, e2, mx, ALU.subtract))
            tell("nexp_in")
            dve.wait_ge(S("nexp_out"), 1)
            for h in range(HEADS):
                zh, ch = z[:, :, h * AW:(h + 1) * AW], cr[:, :, h * AW:(h + 1) * AW]
                do(TT(zh, zh, over(e1[:, :, h], AW), ALU.mult))
                do(TT(ch, ch, over(e2[:, :, h], AW), ALU.mult))
                do(TT(zh, zh, ch, ALU.add))
                rd = nt[:, 1, 0:B]
                do(dve.reciprocal(rd, zh[:, :, HD]))
                do(TT(rd, rd, mask[:, :], ALU.mult))
                do(TT(zh[:, :, 0:HD], zh[:, :, 0:HD], over(rd, HD), ALU.mult))
                xh = X[:, :, h * HD:(h + 1) * HD]
                do(STT(xh, xh, 2.0, zh[:, :, 0:HD], ALU.mult, ALU.add))
            do(TT(X[:, :, :], X[:, :, :], row(bias[:, 4, :], B), ALU.add))
            tell("z_free")
            layer_norm()

            for n in range(2):
                r = 4 + n
                b_, gamma, beta = bias[:, 5 + 3 * n, :], bias[:, 6 + 3 * n, :], bias[:, 7 + 3 * n, :]
                do(TT(T64, X[:, :, :] if n == 0 else T64, over(dis[:, :], D), ALU.mult))
                tell("table_ready")
                gcn_pass(r)
                z = finish_sums(r)
                do(TT(z, z, T64, ALU.add))
                do(TT(tmp64, z, over(dis[:, :], D), ALU.mult))
                tell("z_free")
                name = ("gcn31", "gcn32")[n]
                tell("in_" + name)
                product(name, lambda v, b0, nb: TT(T64[:, b0:b0 + nb, :], v, row(b_, nb), ALU.add))
                s0, s1 = nt[:, 0, :], nt[:, 1, :]
                for m in range(2):
                    if m == 0:
                        do(dve.tensor_reduce(s0, T64.rearrange("p b f -> p f b"), AX, ALU.add))
                    else:
                        do(TT(tmp64, T64, T64, ALU.mult))
                        do(dve.tensor_reduce(s0, tmp64.rearrange("p b f -> p f b"), AX, ALU.add))
                    tell("colsum_in")
                    dve.wait_ge(S("colsum_out"), 2 * n + m + 1)
                    do(TS(s1, ps[0:P, 7, 0:D], 1.0 / N, EPS * m, ALU.mult, ALU.add))
                    if m == 0:
                        do(TT(T64, T64, row(s1, B), ALU.subtract))
                rsqrt(s1, D)
                do(TT(s1, s1, gamma, ALU.mult))
                do(TT(T64, T64, row(s1, B), ALU.mult))
                do(TT(T64, T64, row(beta, B), ALU.add))
                do(STT(T64, T64, 0.01, T64, ALU.mult, ALU.max))
            do(TT(X[:, :, :], X[:, :, :], T64, ALU.add))
            layer_norm()
            tell("result")


def kernel(**inputs):
    import numpy as np
    import concourse.bacc as bacc
    from concourse.bass_utils import run_bass_kernel_spmd as run

    nc = bacc.Bacc("TRN2", target_bir_lowering=False, num_devices=1)
    arrays, args = {}, {}
    for name, value in inputs.items():
        v = np.ascontiguousarray(value)
        arrays[name] = v
        args[name] = nc.dram_tensor(name, v.shape, mybir.dt.from_np(v.dtype), kind="ExternalInput").ap()
    out = nc.dram_tensor("out", inputs["x"].shape, F32, kind="ExternalOutput").ap()
    gnn_kernel(nc, args, out)
    r = run(nc, [arrays], core_ids=[0])
    return r.results[0]["out"]
```

```python
import concourse.bass as bass
from concourse import mybir
from contextlib import ExitStack

F32 = mybir.dt.float32
BF16 = mybir.dt.bfloat16
F8 = mybir.dt.float8e4
I32 = mybir.dt.int32
ALU = mybir.AluOpType
ACT = mybir.ActivationFunctionType
AX = mybir.AxisListType.X

P = 125
D = 64
HEADS = 4
HD = D // HEADS
BIG = 1.0e30
GROUP = 3
BANK = 512
U = 22
BUFS = 3
PAIRS = U // 2
EPS = 1e-5
WIN = 5
WIN_EDGES = 256
WINS = P // WIN
MAX_COUNT = 15
ABUFS = 5
HIST_CHUNKS = 24
FLAG_AT = 0.5
HC = 23
AW = HD + 1
ROW2 = HEADS * AW


def gnn_kernel(nc, a, out):
    N, E = a["x"].shape[0], a["src"].shape[0]
    B, J = N // P, E // P
    CHUNKS = J // U
    ITER = CHUNKS // BUFS
    ABLOCKS = CHUNKS - HIST_CHUNKS
    assert ABLOCKS >= B and HIST_CHUNKS % BUFS == 0 and HIST_CHUNKS * 3 * HC >= J and WINS * WIN == P
    assert B * P == N and J * P == E and CHUNKS * U == J and ITER * BUFS == CHUNKS

    ctx = ExitStack()
    with ctx:
        def sb(name, shape, dt=F32):
            return ctx.enter_context(nc.sbuf_tensor(name, shape, dt))

        sems = {}

        def S(name):
            if name not in sems:
                sems[name] = ctx.enter_context(nc.semaphore(name))
            return sems[name]

        def dram(name, shape):
            return nc.dram_tensor(name, shape, F32, kind="Internal").ap()

        adjacency = nc.dram_tensor("adjacency", [ABLOCKS, P, B * P // 2], BF16, kind="Internal").ap()
        records = dram("records", [E + WIN_EDGES, 2])
        start_node = nc.dram_tensor("start_node", [N, 1], I32, kind="Internal").ap()
        tables = [dram(f"table{r}", [N, w]) for r, w in enumerate((D, 32, 32, ROW2, D, D))]
        sums = [dram(f"sums{r}", [E, w]) for r, w in enumerate((D, 32, 32, ROW2 + HEADS, D, D))]
        query_table = dram("query_table", [N, HEADS])
        query_start = dram("query_start", [E + N, HEADS])

        srcI = sb("srcI", [P, J + BUFS * U], I32)
        keep = sb("keep", [P, J])
        edge_logit = sb("edge_logit", [P, J, HEADS])
        big = sb("big", [P, J * HEADS])
        spare = sb("spare", [128, N])
        cross_sel = spare[0:P, :]
        X = sb("X", [P, B, D])
        Tflat = sb("Tflat", [P, B * (D + 2 * HEADS)])
        Zflat = sb("Zflat", [P, B * (ROW2 + HEADS)])
        tmpf = sb("tmpf", [P, B * (ROW2 + HEADS + 1)])
        idx = [sb(f"idx{k}", [P, U], I32) for k in range(BUFS)]
        gath_all = sb("gath_all", [P, BUFS * U * ROW2])
        gath = [gath_all[:, k * U * ROW2:(k + 1) * U * ROW2] for k in range(BUFS)]
        keepc = sb("keepc", [P, U])
        factor = sb("factor", [P, ROW2 * (U + 1)])
        values = sb("values", [P, ROW2 * (U + 1)])
        runs = sb("runs", [P, ROW2 * (U + 1)])
        rows = sb("rows", [P, U * (ROW2 + HEADS)])
        xT = sb("xT", [128, PAIRS, P])
        lin_in = [xT[:, 4 * i:4 * i + GROUP, :] for i in range(2)]
        ident = sb("ident", [128, 128])
        ones = sb("ones", [P, P])
        tri = sb("tri", [P, P])
        iotaP = sb("iotaP", [P, P], BF16)
        iotaB = sb("iotaB", [P, B], BF16)
        node_no = sb("node_no", [P, B])
        prep = xT[:, :, :].rearrange("p u n -> p (u n)")
        srcG, srcE, srcU = prep[:, 0:128], prep[:, 128:256], prep[0:D, 256:384]
        WG = sb("WG", [128, 128])
        WE = sb("WE", [128, 2 * (D + HEADS)])
        WU = sb("WU", [128, D])
        WN = sb("WN", [128, 2 * (D + 2 * HEADS)])
        W11 = sb("W11", [128, D])
        W12 = sb("W12", [128, 128])
        W31 = sb("W31", [128, 128])
        W32 = sb("W32", [128, 128])
        w_edge2, w_node2, wtmp = prep[:, 384:384 + D], prep[:, 448:448 + D], prep[:, 512:512 + D]
        attn = prep[:, 576:576 + 3 * D].rearrange("p (m n) -> p m n", m=3)
        bias = sb("bias", [P, 11, D])
        deg = sb("deg", [P, B])
        dis = sb("dis", [P, B])
        mask = sb("mask", [P, B])
        cum = sb("cum", [P, B])
        nt = sb("nt", [P, 4, D])
        endI = sb("endI", [P, B], I32)
        startnI = sb("startnI", [P, B], I32)
        startI = sb("startI", [P, B], I32)
        firstI = sb("firstI", [P, 2], I32)
        nextI = sb("nextI", [P, 2], I32)
        edge_ends = sb("edge_ends", [P, 4])
        tri_incl = sb("tri_incl", [P, P])
        shift4 = sb("shift4", [P, P])
        iotaW = sb("iotaW", [128, WIN * B], BF16)
        iotaP128 = sb("iotaP128", [128, P], BF16)
        win_off = sb("win_off", [128, WINS])
        rec_all = sb("rec_all", [128, BUFS * WINS * 4])
        rec = [rec_all[:, k * WINS * 4:(k + 1) * WINS * 4].rearrange("p (w c v) -> p w c v", w=WINS, c=2) for k in range(BUFS)]
        key = sb("key", [128, WINS, 2])
        checks = sb("checks", [P, 8])
        flagI = sb("flagI", [P, 1], I32)
        rs_in = sb("rs_in", [P, D])
        rs_out = sb("rs_out", [P, D])
        w0 = sb("w0", [P, HEADS])
        mrun = sb("mrun", [P, HEADS, U + 1])
        logit = tri_incl[:, 0:U * HEADS].rearrange("p (j h) -> p j h", h=HEADS)
        keepn = tri_incl[:, U * HEADS:U * HEADS + U]
        logitT = shift4[:, 0:U * HEADS].rearrange("p (h j) -> p h j", h=HEADS)
        expo = rec_all[0:P, 0:2 * HEADS * U].rearrange("p (t h j) -> p t h j", t=2, h=HEADS)
        bnd = rec_all[0:P, 2 * HEADS * U:2 * HEADS * U + ROW2 + HEADS + 1]
        bmax = sb("bmax", [P, 3, HEADS])

        xe = [big[:, k * U * D:(k + 1) * U * D] for k in range(BUFS)]
        o = BUFS * U * D
        hotP = big[:, o:o + (HC * P + 1) // 2].bitcast(BF16)[:, 0:HC * P].rearrange("p (j n) -> p j n", j=HC)
        o += (HC * P + 1) // 2
        hotB = big[:, o:o + HC * B // 2].bitcast(BF16).rearrange("p (j n) -> p j n", j=HC)
        assert o + HC * B // 2 <= J * HEADS and HC * B % 2 == 0
        XZ = big[:, 0:B * 2 * D].rearrange("p (b f) -> p b f", b=B)
        query = big[:, :].rearrange("p (j h) -> p j h", h=HEADS)
        dstI = Zflat[:, 0:J].bitcast(I32)
        JH = HIST_CHUNKS * 3 * HC
        dstF = Zflat[:, JH:JH + J]
        node_half = Zflat[:, 0:JH].bitcast(BF16)
        pnode, bnode = node_half[:, 0:JH], node_half[:, JH:2 * JH]
        starts = Zflat[0:1, 0:ABLOCKS * WINS].bitcast(I32)
        edge_rec = Tflat[:, 0:2 * J].rearrange("p (j v) -> p j v", v=2)
        AB4 = B * P // 4 + 1
        ablock_space = [spare[0:P, n * AB4:(n + 1) * AB4] for n in range(BUFS)]
        ablock = [t.bitcast(F8)[:, 0:B * P].rearrange("p (b d) -> p b d", b=B) for t in ablock_space]
        junk = tmpf[:, 0:AB4].bitcast(F8)[:, 0:B * P].rearrange("p (b d) -> p b d", b=B)
        WK = WIN * B + P
        winhot = [spare[:, 3 * AB4 + n * WK:3 * AB4 + (n + 1) * WK].bitcast(BF16) for n in range(4)]
        assert BUFS * AB4 + 4 * WK <= N
        abuf_space = [values[:, 0:AB4], factor[:, 0:AB4], runs[:, 0:AB4], gath_all[:, 0:AB4], gath_all[:, AB4:2 * AB4]]
        abuf = [t.bitcast(F8)[:, 0:B * P].rearrange("p (b d) -> p b d", b=B) for t in abuf_space]

        def pairs_of_bytes(t):
            return t.bitcast(BF16)[:, 0:B * P // 2]

        def parts3(w):
            return big[:, 0:B * 3 * w // 2].bitcast(BF16).rearrange("p (b t f) -> p b t f", b=B, t=3)

        ps = ctx.enter_context(nc.psum_tensor("ps", [128, 8, BANK], F32))

        def v3(t, w, n=B):
            return t[:, 0:n * w].rearrange("p (b f) -> p b f", b=n)

        def chunk3(t, w):
            return t[:, 0:U * w].rearrange("p (j f) -> p j f", j=U)

        def run3(t, w):
            return t[:, 0:w * (U + 1)].rearrange("p (f j) -> p f j", f=w)

        def rowsof(r, i, k):
            v = sums[r].rearrange("(p j) f -> p j f", p=P)
            return v[:, bass.ds(i * (BUFS * U) + k * U, U), :]

        PASSW = (D, 32, 32, ROW2, D, D)
        GCN_NO = {1: 0, 2: 1, 4: 2, 5: 3}

        def seq(r):
            return GCN_NO[r] if r in GCN_NO else r // 3

        def PS(name, r):
            return S(name + "_gcn") if r in GCN_NO else S(name)
        CORRW = (D, 32, 32, ROW2 + HEADS + 1, D, D)

        def units(src, kind):
            if kind == "pair":
                return [src[:, 2 * u:2 * u + 2, :].rearrange("p b f -> p (b f)") for u in range(B // 2)]
            return [src[:, u, :] for u in range(B)]

        T64, T32, T72 = v3(Tflat, D), v3(Tflat, 32), v3(Tflat, D + 2 * HEADS)
        tmp64 = v3(tmpf, D)
        LINEARS = {
            "message": (units(X, "pair"), WG, 128),
            "update": (units(XZ, "one"), WU, D),
            "gcn11": (units(X, "pair"), W11, D),
            "gcn12": (units(tmp64, "pair"), W12, 128),
            "attend": (units(X, "pair"), WN, 2 * (D + 2 * HEADS)),
            "gcn31": (units(tmp64, "pair"), W31, 128),
            "gcn32": (units(tmp64, "pair"), W32, 128),
        }
        ORDER = list(LINEARS)
        group_base, g0 = {}, 0
        for name in ORDER:
            group_base[name] = g0
            g0 += -(-len(LINEARS[name][0]) // GROUP)

        def groups(name):
            us = LINEARS[name][0]
            return [us[i:i + GROUP] for i in range(0, len(us), GROUP)]

        BIASES = ("L0_gnn_M_b", "L0_gnn_U_b", "L1_gnn_b1", "L1_gnn_b2", "L2_gnn_bias", "L3_gnn_b1", "L3_gnn_gamma1",
                  "L3_gnn_beta1", "L3_gnn_b2", "L3_gnn_gamma2", "L3_gnn_beta2")
        W_LOADS = 18 + 4 + len(BIASES)

        HALVES = (range(0, 6), range(6, PAIRS))
        SIDE = ((0, 1, 2), (range(0, 8), range(8, 16), range(16, WINS)))
        PAIRS_W = (WINS + 1) // 2

        def pair_bank(p):
            return 7 if p == PAIRS_W - 1 else 4 + p % 3
        block = ctx.enter_context(nc.Block())

        @block.sync
        def _(sp):
            dense = [None]

            def load(dst, src, sem="loaded"):
                sp.dma_start(dst, src).then_inc(S(sem), 16)

            load(srcI[:, 0:J], a["src"].rearrange("(p j) -> p j", p=P), "loaded_idx")
            load(dstI, a["dst"].rearrange("(p j) -> p j", p=P), "loaded_idx")
            dst2 = a["dst"].rearrange("(p j) -> p j", p=P)
            load(firstI[:, :], dst2[:, 0:2], "loaded_idx")
            sp.wait_ge(S("zeroed"), 1)
            load(nextI[0:P - 1, :], dst2[1:P, 0:2], "loaded_idx")
            load(X[:, :, :], a["x"].rearrange("(b p) f -> p b f", p=P), "loaded_x")
            n = 0
            for h in range(2):
                lo, hi = D * h, D * h + D
                for dst, src in (
                    (srcG[lo:hi, lo:hi], a["L0_gnn_M_W"][:, 0:D]),
                    (srcE[lo:hi, lo:hi], a["L0_gnn_M_W"][:, D:2 * D]),
                    (W11[lo:hi, 32 * h:32 * h + 32], a["L1_gnn_W1"]),
                    (W12[lo:lo + 32, lo:hi], a["L1_gnn_W2"]),
                    (WN[lo:hi, 72 * h:72 * h + D], a["L2_gnn_W_node"]),
                    (W31[lo:hi, lo:hi], a["L3_gnn_W1"]),
                    (W32[lo:hi, lo:hi], a["L3_gnn_W2"]),
                    (w_edge2[lo:hi, :], a["L2_gnn_W_edge"]),
                    (w_node2[lo:hi, :], a["L2_gnn_W_node"]),
                ):
                    load(dst, src, "loaded_w")
                    n += 1
            load(srcU[:, :], a["L0_gnn_U_W"], "loaded_w")
            for m, name in enumerate(("edge", "key", "query")):
                row = a[f"L2_gnn_attn_{name}"].rearrange("(a h) d -> a (h d)", a=1)
                load(attn[:, m, :], row.to_broadcast([128, D]), "loaded_w")
            for m, name in enumerate(BIASES):
                v = a[name].rearrange("(a n) -> a n", a=1)
                w = v.shape[1]
                load(bias[:, m, 0:w], v.to_broadcast([P, w]), "loaded_w")
            assert n + 4 + len(BIASES) == W_LOADS

            sp.wait_ge(S("records_ready"), 1)
            load(records[0:E, :].rearrange("(p j) v -> p j v", p=P), edge_rec, "records")
            load(records[E:E + WIN_EDGES, :].rearrange("(p c) v -> p c v", c=2), key[:, 0:2, :], "records")

            def store_table(r, src):
                sp.wait_ge(PS("table_ready", r), seq(r) + 1)
                sp.dma_start(tables[r].rearrange("(b p) f -> p b f", p=P), src).then_inc(PS("table", r), 16)

            def gcn_loads(r, src):
                with sp.If(dense[0] == 1):
                    sp.wait_ge(S("parts_ready"), seq(r) + 1)
                    with sp.Fori(0, B // ABUFS) as i:
                        for k in range(ABUFS):
                            sp.wait_ge(S("a_used"), i * ABUFS + (seq(r) * B + k + 1))
                            sp.dma_start(pairs_of_bytes(abuf_space[k]),
                                         adjacency[bass.ds(i * ABUFS + k, 1), :, :].rearrange("a p n -> (a p) n")).then_inc(S(f"a{k}"), 16)
                with sp.Else():
                    store_table(r, src)

            store_table(0, T64)
            edges = a["edge_attr_64"].rearrange("(p j) f -> p j f", p=P)
            def load_edges(i, k):
                sp.wait_ge(S("xt_turned"), (i * BUFS + k) * 2 + 2)
                sp.dma_start(chunk3(xe[k], D), edges[:, bass.ds(i * (BUFS * U) + k * U, U), :]).then_inc(S(f"xe{k}"), 16)

            with sp.Fori(0, HIST_CHUNKS // BUFS) as i:
                for k in range(BUFS):
                    load_edges(i, k)
            sp.wait_ge(S("starts_ready"), 1)
            sp.dma_start(start_node.rearrange("(b p) a -> p b a", p=P), startnI[:, :].unsqueeze(2), allow_slow_non_contiguous=True).then_inc(S("starts_put"), 16)
            sp.wait_ge(S("starts_put"), 16)
            sp.dma_start(starts[:, 0:N // WIN].unsqueeze(2), start_node.rearrange("(w d) a -> a w d", d=WIN)[:, :, 0:1],
                         allow_slow_non_contiguous=True).then_inc(S("starts_back"), 16)
            sp.wait_ge(S("starts_back"), 16)
            with sp.Fori(HIST_CHUNKS // BUFS, ITER) as i:
                for k in range(BUFS):
                    load_edges(i, k)
                    sp.wait_ge(S("rec_used"), i * BUFS + (k + 1 - HIST_CHUNKS))
                    for w in range(WINS):
                        at = (i * BUFS - (HIST_CHUNKS - k)) * WINS + w
                        first = sp.value_load(starts[0:1, bass.ds(at, 1)], min_val=0, max_val=E)
                        sp.dma_start(rec[k][:, w, :, :].rearrange("p c v -> p (c v)"),
                                     records[bass.ds(first, WIN_EDGES), :].rearrange("(p c) v -> p (c v)", c=2)).then_inc(S(f"rec{k}"), 16)
            sp.wait_ge(S("flag_ready"), 1)
            dense[0] = sp.value_load(flagI[0:1, 0:1], min_val=0, max_val=1)
            gcn_loads(1, T32)
            gcn_loads(2, T32)
            sp.wait_ge(S("table_ready"), 2)
            sp.dma_start(tables[3].rearrange("(b p) f -> p b f", p=P), T72[:, :, 0:ROW2]).then_inc(S("table"), 16)
            sp.dma_start(query_table.rearrange("(b p) f -> p b f", p=P), T72[:, :, ROW2:ROW2 + HEADS]).then_inc(S("query_table"), 16)
            sp.dma_start(query_start[0:E, :].rearrange("(p j) h -> p (j h)", p=P), big[:, :]).then_inc(S("query_zero"), 16)
            sp.wait_ge(S("query_put"), 16 * B)
            sp.dma_start(big[:, :], query_start[0:E, :].rearrange("(p j) h -> p (j h)", p=P)).then_inc(S("query_back"), 16)
            gcn_loads(4, T64)
            gcn_loads(5, T64)
            sp.wait_ge(S("result"), 1)
            sp.dma_start(out.rearrange("(b p) f -> p b f", p=P), X[:, :, :]).then_inc(S("out"), 16)
            sp.wait_ge(S("out"), 16)

        @block.gpsimd
        def _(g):
            g.memset(ident[:, :], 0.0).then_inc(S("pool_const"), 1)
            g.memset(ones[:, :], 1.0).then_inc(S("pool_const"), 1)
            g.iota(iotaP[:, :], pattern=[[1, P]], base=0, channel_multiplier=0, allow_small_or_imprecise_dtypes=True).then_inc(S("pool_const"), 1)
            g.iota(iotaB[:, :], pattern=[[1, B]], base=0, channel_multiplier=0, allow_small_or_imprecise_dtypes=True).then_inc(S("pool_const"), 1)
            g.iota(node_no[:, :], pattern=[[P, B]], base=0, channel_multiplier=1, allow_small_or_imprecise_dtypes=True).then_inc(S("pool_const"), 1)
            g.iota(iotaW[:, :], pattern=[[1, WIN * B]], base=0, channel_multiplier=0, allow_small_or_imprecise_dtypes=True).then_inc(S("pool_const"), 1)
            g.iota(iotaP128[:, :], pattern=[[1, P]], base=0, channel_multiplier=0, allow_small_or_imprecise_dtypes=True).then_inc(S("pool_const"), 1)
            g.iota(win_off[:, :], pattern=[[WIN * B, WINS]], base=0, channel_multiplier=0, allow_small_or_imprecise_dtypes=True).then_inc(S("pool_const"), 1)
            g.memset(shift4[:, :], 0.0).then_inc(S("pool_const"), 1)
            g.wait_ge(S("pool_const"), 9)
            g.affine_select(out=ident[:, :], in_=ident[:, :], compare_op=ALU.not_equal, fill=1.0, base=0,
                            pattern=[[-1, 128]], channel_multiplier=1).then_inc(S("pool_const"), 1)
            g.affine_select(out=tri[:, :], in_=ones[:, :], compare_op=ALU.is_gt, fill=0.0, base=0,
                            pattern=[[1, P]], channel_multiplier=-1).then_inc(S("pool_const"), 1)
            g.affine_select(out=tri_incl[:, :], in_=ones[:, :], compare_op=ALU.is_ge, fill=0.0, base=0,
                            pattern=[[1, P]], channel_multiplier=-1).then_inc(S("pool_const"), 1)
            g.affine_select(out=shift4[:, :], in_=shift4[:, :], compare_op=ALU.not_equal, fill=1.0, base=1 - WIN,
                            pattern=[[-1, P]], channel_multiplier=1).then_inc(S("pool_const"), 1)

            def gather(dst, table, index, sem):
                g.indirect_dma_start(out=dst, out_offset=None, in_=table,
                                     in_offset=bass.IndirectOffsetOnAxis(ap=index, axis=0)).then_inc(sem, 16)

            def edge_pass(r):
                w = PASSW[r]
                r0 = seq(r) * CHUNKS
                g.wait_ge(PS("table", r), 16 * (seq(r) + 1))
                with g.Fori(0, ITER) as i:
                    for k in range(BUFS):
                        g.wait_ge(PS("idx_ready", r), i * BUFS + (r0 + k + 1))
                        g.sem_inc(S("gather_begun"), 1)
                        for j in range(U):
                            gather(chunk3(gath[k], w)[:, j, :], tables[r], idx[k][:, j:j + 1], PS(f"gathered{k}", r))

            def node_gather(r):
                w = sums[r].shape[1]
                g.wait_ge(PS("stored", r), 16 * (CHUNKS * (seq(r) + 1) + 1))
                g.wait_ge(S("ends_ready"), 1)
                g.wait_ge(PS("z_free", r), seq(r) + 1)
                for b in range(B):
                    gather(v3(Zflat, w)[:, b, :], sums[r], endI[:, b:b + 1], PS("nodes_gathered", r))

            for r in range(6):
                if r == 3:
                    g.wait_ge(S("query_zero"), 16)
                    for b in range(B):
                        g.indirect_dma_start(out=query_start, out_offset=bass.IndirectOffsetOnAxis(ap=startI[:, b:b + 1], axis=0),
                                             in_=T72[:, b, ROW2:ROW2 + HEADS], in_offset=None).then_inc(S("query_put"), 16)
                    g.wait_ge(S("query_table"), 16)
                    gather(w0[:, :], query_table, firstI[:, 0:1], S("query_first"))
                if r in GCN_NO:
                    with g.If(dense == 0):
                        edge_pass(r)
                        node_gather(r)
                else:
                    edge_pass(r)
                    node_gather(r)
                if r == 0:
                    g.wait_ge(S("spare_free"), 1)
                    g.iota(cross_sel[:, :], pattern=[[1, N]], base=0, channel_multiplier=0,
                           allow_small_or_imprecise_dtypes=True).then_inc(S("cross_iota"), 1)
                    g.wait_ge(S("flag_ready"), 1)
                    dense = g.value_load(flagI[0:1, 0:1], min_val=0, max_val=1)

        @block.tensor
        def _(pe):
            def linear(name):
                _, w, ncol = LINEARS[name]
                gs, base = groups(name), group_base[name]
                pe.wait_ge(S("in_" + name), 1)

                def turn(n):
                    q = base + n
                    if q >= 2:
                        pe.wait_ge(S("lin_copied"), q - 1)
                    for i, u in enumerate(gs[n]):
                        last = pe.transpose(ps[:, q % 2, i * P:(i + 1) * P], u, ident[0:P, 0:P])
                    last.then_inc(S("lin_turned"), 1)

                turn(0)
                for n in range(len(gs)):
                    if n + 1 < len(gs):
                        turn(n + 1)
                    q = base + n
                    pe.wait_ge(S("lin_copied"), q + 1)
                    if q >= 2:
                        pe.wait_ge(S("lin_taken"), q - 1)
                    for i in range(len(gs[n])):
                        last = pe.matmul(ps[0:P, 2 + q % 2, i * ncol:(i + 1) * ncol], lin_in[q % 2][:, i, :], w[:, 0:ncol],
                                         start=True, stop=True)
                    last.then_inc(S("lin_done"), 1)

            def crossing(r, rhs):
                w = CORRW[r]
                per = min(8, BANK // w)
                pe.wait_ge(PS("cross_in", r), seq(r) + 1)
                for b in range(B):
                    last = pe.matmul(ps[0:P, b // per, (b % per) * w:(b % per + 1) * w], cross_sel[:, b * P:(b + 1) * P], rhs,
                                     start=True, stop=True)
                last.then_inc(PS("cross_out", r), 1)

            def gcn_products(r, rhs):
                w = PASSW[r]
                with pe.If(dense == 1):
                    pe.wait_ge(S("parts_ready"), seq(r) + 1)
                    with pe.Fori(0, B // ABUFS) as i:
                        for k in range(ABUFS):
                            pe.wait_ge(S(f"a{k}"), (i + (seq(r) * (B // ABUFS) + 1)) * 16)
                            pe.wait_ge(S("a_taken"), i * ABUFS + (seq(r) * B + k + 1))
                            pe.sem_inc(S("a_begun"), 1)
                            for b in range(B):
                                last = pe.matmul(ps[0:P, k, 0:3 * w], abuf[k][:, b, :],
                                                 parts3(w)[:, b, :, :].rearrange("p t f -> p (t f)"), start=(b == 0), stop=(b == B - 1))
                            last.then_inc(S("a_used"), 1)
                with pe.Else():
                    crossing(r, rhs)

            def column_sums(n):
                pe.wait_ge(S("colsum_in"), n + 1)
                pe.matmul(ps[0:P, 7, 0:D], ones[:, :], nt[:, 0, :], start=True, stop=True).then_inc(S("colsum_out"), 1)

            pe.wait_ge(S("loaded_w"), 16 * W_LOADS)
            pe.wait_ge(S("pool_const"), 13)
            pe.transpose(ps[:, 0, 0:128], srcG[:, :], ident[:, :])
            pe.transpose(ps[:, 1, 0:128], srcE[:, :], ident[:, :])
            pe.transpose(ps[:, 2, 0:D], srcU[:, :], ident[0:D, 0:D]).then_inc(S("w_turned"), 1)

            linear("message")

            pe.wait_ge(S("hist_zero"), 1)
            pe.matmul(ps[0:P, 7, 0:B], hotP[:, 0, :], hotB[:, 0, :], start=True, stop=False, skip_group_check=True).then_inc(S("hot_used"), 1)
            pe.sem_inc(S("xt_turned"), 2 * BUFS)
            pe.sem_inc(S("a_used"), ABUFS)

            def turn_edges(i, k, h):
                q = (i * BUFS + k) * 2 + h
                if h == 0:
                    pe.wait_ge(S(f"xe{k}"), i * 16 + 16)
                pe.wait_ge(S("xt_copied"), q + 1)
                for u in HALVES[h]:
                    v = u - HALVES[h][0]
                    last = pe.transpose(ps[:, v // 4, (v % 4) * P:(v % 4 + 1) * P], xe[k][:, u * 2 * D:(u + 1) * 2 * D], ident[0:P, 0:P])
                last.then_inc(S("xt_turned"), 1)

            def edge_products(i, k, h):
                q = (i * BUFS + k) * 2 + h
                pe.wait_ge(S("xt_copied"), q + 2)
                pe.wait_ge(S("edge_taken"), q + 1)
                for u in HALVES[h]:
                    v = u - HALVES[h][0]
                    last = pe.matmul(ps[0:P, 2 + v // 3, (v % 3) * 136:(v % 3 + 1) * 136], xT[:, u, :], WE[:, :], start=True, stop=True)
                last.then_inc(S("edge_done"), 1)

            def hist(i, k, part):
                n = (i * BUFS + k) * 3 + part
                pe.wait_ge(S("hot_ready"), n + 1)
                for j in range(HC):
                    last = pe.matmul(ps[0:P, 7, 0:B], hotP[:, j, :], hotB[:, j, :], start=False, stop=False, skip_group_check=True)
                last.then_inc(S("hot_used"), 1)

            def windows(i, k, ws):
                for w in ws:
                    at = (i * BUFS - (HIST_CHUNKS - k)) * WINS + w
                    pair = (i * BUFS - (HIST_CHUNKS - k)) * PAIRS_W + w // 2
                    pe.wait_ge(S("winhot"), at + 1)
                    if w % 2 == 0:
                        pe.wait_ge(S("win_copied"), pair + 1)
                    bank = pair_bank(w // 2)
                    hb = winhot[w % 4]
                    for c in range(2):
                        last = pe.matmul(ps[0:P, bank, WIN * B * (w % 2):WIN * B * (w % 2 + 1)],
                                         hb[:, 2 * WIN * B + c * P:2 * WIN * B + (c + 1) * P],
                                         hb[:, c * WIN * B:(c + 1) * WIN * B], start=(c == 0), stop=(c == 1))
                    last.then_inc(S("win_done"), 1)

            for lo, hi, side in ((0, HIST_CHUNKS // BUFS, hist), (HIST_CHUNKS // BUFS, ITER, windows)):
                with pe.Fori(lo, hi) as i:
                    for k in range(BUFS):
                        turn_edges(i, k, 0)
                        side(i, k, SIDE[side is windows][0])
                        edge_products(i, k, 0)
                        turn_edges(i, k, 1)
                        side(i, k, SIDE[side is windows][1])
                        edge_products(i, k, 1)
                        side(i, k, SIDE[side is windows][2])
                if side is hist:
                    pe.wait_ge(S("cum_in"), 1)
                    pe.matmul(ps[0:P, 7, 64:64 + B], tri_incl[:, :], deg[:, :], start=True, stop=True)
                    pe.matmul(ps[0:P, 7, 128:128 + B], ones[:, :], deg[:, :], start=True, stop=True).then_inc(S("cum_out"), 1)
                    pe.wait_ge(S("cum_in"), 2)
                    pe.matmul(ps[0:P, 7, 192:192 + B], shift4[:, :], cum[:, :], start=True, stop=True).then_inc(S("cum_out"), 1)
            pe.wait_ge(S("checks_in"), 1)
            pe.matmul(ps[0:P, 7, 256:257], ones[:, :], checks[:, 0:1], start=True, stop=True).then_inc(S("checks_out"), 1)
            pe.wait_ge(S("flag_ready"), 1)
            dense = pe.value_load(flagI[0:1, 0:1], min_val=0, max_val=1)
            crossing(0, chunk3(rows, D)[:, U - 1, :])
            linear("update")
            linear("gcn11")
            gcn_products(1, chunk3(rows, 32)[:, U - 1, :])
            gcn_products(2, chunk3(rows, 32)[:, U - 1, :])
            linear("gcn12")
            linear("attend")
            pe.wait_ge(S("diag_ready"), 1)
            for m in range(6):
                last = pe.matmul(ps[0:P, m // 4, (m % 4) * P:(m % 4 + 1) * P], ones[:, :], v3(tmpf, P, 6)[:, m, :],
                                 start=True, stop=True)
            last.then_inc(S("diag_out"), 1)
            crossing(3, bnd[:, :])
            gcn_products(4, chunk3(rows, D)[:, U - 1, :])
            linear("gcn31")
            column_sums(0)
            column_sums(1)
            gcn_products(5, chunk3(rows, D)[:, U - 1, :])
            linear("gcn32")
            column_sums(2)
            column_sums(3)

        @block.scalar
        def _(act):
            def linear(name):
                base = group_base[name]
                for n, us in enumerate(groups(name)):
                    q = base + n
                    act.wait_ge(S("lin_turned"), q + 1)
                    if q >= 2:
                        act.wait_ge(S("lin_done"), q - 1)
                    w = len(us)
                    act.copy(lin_in[q % 2][:, 0:w, :], ps[:, q % 2, 0:w * P].rearrange("p (u n) -> p u n", u=w)).then_inc(S("lin_copied"), 1)

            root_n = [0]

            def root(w=B):
                root_n[0] += 1
                act.wait_ge(S("root_in"), root_n[0])
                act.activation(rs_out[:, 0:w], rs_in[:, 0:w], ACT.Sqrt).then_inc(S("root_out"), 1)

            def expand(r, c, w):
                act.wait_ge(PS("keepc_ready", r), c + (seq(r) * CHUNKS + 1))
                act.copy(run3(factor, w)[:, :, 1:U + 1],
                         keepc[:, :].unsqueeze(1).to_broadcast([P, w, U])).then_inc(PS("factor_ready", r), 1)

            def store_rows(r, i, k, w):
                c = i * BUFS + k
                c1 = c + (seq(r) * CHUNKS + 1)
                act.wait_ge(PS("scanned", r), c1)
                act.wait_ge(PS("stored", r), c1 * 16)
                full = sums[r].shape[1]
                v = chunk3(rows, full)
                if full > w:
                    act.copy(v[:, :, w:full], mrun[:, :, 1:U + 1].rearrange("p h j -> p j h")).then_inc(S("rows_max"), 1)
                    act.wait_ge(S("rows_max"), c + 1)
                act.copy(v[:, :, 0:w], run3(runs, w)[:, :, 1:U + 1].rearrange("p f j -> p j f")).then_inc(PS("rows_ready", r), 1)
                act.wait_ge(PS("rows_ready", r), c + (seq(r) * CHUNKS + 2))
                act.dma_start(rowsof(r, i, k), v).then_inc(PS("stored", r), 16)

            for suffix in ("", "_gcn"):
                act.sem_inc(S("stored" + suffix), 16)
                act.sem_inc(S("rows_ready" + suffix), 1)
            for k in range(BUFS):
                act.sem_inc(S(f"block_stored{k}"), 16)
            act.sem_inc(S("win_copied"), 3)
            act.sem_inc(S("xt_copied"), 1)
            linear("message")

            def copy_turned(i, k, h):
                q = (i * BUFS + k) * 2 + h
                act.wait_ge(S("xt_turned"), q + (2 * BUFS + 1))
                act.wait_ge(S("edge_done"), q + 1)
                n, at = len(HALVES[h]), HALVES[h][0]
                act.copy(xT[:, at:at + 4, :], ps[:, 0, 0:4 * P].rearrange("p (u n) -> p u n", n=P))
                act.copy(xT[:, at + 4:at + n, :], ps[:, 1, 0:(n - 4) * P].rearrange("p (u n) -> p u n", n=P)).then_inc(S("xt_copied"), 1)

            def relu(i, k):
                v = run3(values, D)[:, :, 1:U + 1]
                act.wait_ge(S("edge_taken"), (i * BUFS + k) * 2 + 3)
                act.activation(v, v, ACT.Relu).then_inc(S("messages_ready"), 1)

            def copy_windows(i, k, pairs):
                at = (i * BUFS - (HIST_CHUNKS - k)) * WINS
                if 0 in pairs:
                    act.wait_ge(S(f"block_stored{k}"), (i - (HIST_CHUNKS // BUFS - 1)) * 16)
                for p in pairs:
                    n = min(2, WINS - 2 * p)
                    act.wait_ge(S("win_done"), at + (2 * p + n + 4))
                    act.sem_inc(S("copy_begun"), 1)
                    act.copy(ablock[k][:, :, 2 * p * WIN:(2 * p + n) * WIN].rearrange("p b (w d) -> p w d b", w=n),
                             ps[0:P, pair_bank(p), 0:n * WIN * B].rearrange("p (w d b) -> p w d b", w=n, d=WIN),
                             saturate=False).then_inc(S("win_copied"), 1)

            def finish_block(i, k):
                n = i * BUFS - (HIST_CHUNKS - k)
                act.wait_ge(S("win_copied"), n * PAIRS_W + (PAIRS_W + 3))
                act.wait_ge(S("carried"), n + (HIST_CHUNKS - BUFS + 1))
                act.sem_inc(S("copy_begun"), 1)
                act.activation(junk, ablock[k], ACT.Relu, bias=checks[:, 7:8], accum_out=checks[:, 1 + k:2 + k],
                               saturate=False).then_inc(S("checked"), 1)
                act.dma_start(adjacency[bass.ds(n, 1), :, :].rearrange("a p n -> (a p) n"),
                              pairs_of_bytes(ablock_space[k])).then_inc(S(f"block_stored{k}"), 16)

            with act.Fori(0, HIST_CHUNKS // BUFS) as i:
                for k in range(BUFS):
                    expand(0, i * BUFS + k, D)
                    copy_turned(i, k, 0)
                    copy_turned(i, k, 1)
                    relu(i, k)
                    store_rows(0, i, k, D)
            root()
            with act.Fori(HIST_CHUNKS // BUFS, ITER) as i:
                for k in range(BUFS):
                    expand(0, i * BUFS + k, D)
                    copy_turned(i, k, 0)
                    copy_windows(i, k, range(0, 4))
                    copy_turned(i, k, 1)
                    copy_windows(i, k, range(4, 8))
                    relu(i, k)
                    copy_windows(i, k, range(8, PAIRS_W))
                    finish_block(i, k)
                    store_rows(0, i, k, D)
            act.wait_ge(S("flag_ready"), 1)
            dense = act.value_load(flagI[0:1, 0:1], min_val=0, max_val=1)
            act.wait_ge(S("x_fixed"), 1)
            act.copy(XZ[:, :, 0:D], X[:, :, :]).then_inc(S("xz_x"), 1)
            linear("update")
            root()
            linear("gcn11")
            for r in (1, 2):
                with act.If(dense == 0):
                    with act.Fori(0, ITER) as i:
                        for k in range(BUFS):
                            expand(r, i * BUFS + k, 32)
                            store_rows(r, i, k, 32)
            linear("gcn12")
            root()
            linear("attend")
            with act.Fori(0, ITER) as i:
                for k in range(BUFS):
                    c = i * BUFS + k
                    act.wait_ge(S("expo_in"), c + 1)
                    act.activation(expo[:, :, :, :], expo[:, :, :, :], ACT.Exp).then_inc(S("expo_out"), 1)
                    act.wait_ge(S("expo_out"), c + 1)
                    act.copy(run3(factor, ROW2).rearrange("p (h e) j -> p h e j", h=HEADS)[:, :, :, 1:U + 1],
                             expo[:, 0, :, :].unsqueeze(2).to_broadcast([P, HEADS, AW, U])).then_inc(S("factor_ready"), 1)
                    store_rows(3, i, k, ROW2)
            act.wait_ge(S("bexp_in"), 1)
            act.activation(bmax[:, 2, :], bmax[:, 2, :], ACT.Exp).then_inc(S("bexp_out"), 1)
            act.wait_ge(S("nexp_in"), 1)
            act.activation(Tflat[:, 0:2 * B * HEADS], Tflat[:, 0:2 * B * HEADS], ACT.Exp).then_inc(S("nexp_out"), 1)
            root()
            for r in (4, 5):
                with act.If(dense == 0):
                    with act.Fori(0, ITER) as i:
                        for k in range(BUFS):
                            expand(r, i * BUFS + k, D)
                            store_rows(r, i, k, D)
                linear("gcn31" if r == 4 else "gcn32")
                root(D)
            root()

        @block.vector
        def _(dve):
            done = [0]

            def do(ins):
                done[0] += 1
                ins.then_inc(S("dve"), 1)
                dve.wait_ge(S("dve"), done[0])

            def tell(name, n=1):
                dve.sem_inc(S(name), n)

            TT, TS, STT, CP = dve.tensor_tensor, dve.tensor_scalar, dve.scalar_tensor_tensor, dve.tensor_copy

            def over(t, w):
                return t.unsqueeze(2).to_broadcast([P, t.shape[1], w])

            def row(t, n):
                return t.unsqueeze(1).to_broadcast([P, n, t.shape[1]])

            for t in (srcG, srcE, W11, W12, W31, W32, WE, WN):
                do(dve.memset(t[:, :], 0.0))
            do(dve.memset(nextI[:, :], -1))
            tell("zeroed")
            do(dve.memset(keep[:, 0:1], 0.0))
            do(dve.memset(factor[:, :], 0.0))
            do(dve.memset(hotP, 0.0))
            do(dve.memset(hotB, 0.0))
            tell("hist_zero")
            dve.wait_ge(S("loaded_idx"), 64)
            do(CP(srcI[:, J:J + BUFS * U], srcI[:, 0:BUFS * U]))
            do(CP(dstF, dstI))
            do(TT(keep[:, 1:J], dstF[:, 1:J], dstF[:, 0:J - 1], ALU.is_equal))
            q, rest, off = (spare[0:P, n * J:(n + 1) * J] for n in range(3))
            qI, srcF = tmpf[:, 0:J].bitcast(I32), tmpf[:, J:2 * J]

            def divide(t, quotient, remainder):
                do(TS(qI, t, 1.0 / P, -0.496, ALU.mult, ALU.add))
                do(CP(q, qI))
                do(STT(rest, q, -float(P), t, ALU.mult, ALU.add))
                do(TS(off, rest, 0.0, None, ALU.is_lt))
                do(TT(q, q, off, ALU.subtract))
                do(STT(rest, off, float(P), rest, ALU.mult, ALU.add))
                do(TS(off, rest, float(P), None, ALU.is_ge))
                do(TT(quotient, q, off, ALU.add))
                do(STT(remainder, off, -float(P), rest, ALU.mult, ALU.add))

            do(CP(srcF, srcI[:, 0:J]))
            divide(srcF, srcF, edge_rec[:, :, 1])
            do(STT(edge_rec[:, :, 0], dstF, float(B), srcF, ALU.mult, ALU.add))
            do(dve.memset(key[:, 0:2, :], -1.0))
            tell("records_ready")
            do(dve.memset(pnode[:, J:JH], -1.0))
            do(dve.memset(bnode[:, J:JH], -1.0))
            divide(dstF, bnode[:, 0:J], pnode[:, 0:J])
            do(CP(edge_ends[:, 0:1], dstF[:, J - 1:J]))
            do(CP(edge_ends[:, 1:2], nextI[:, 0:1]))
            do(TT(edge_ends[:, 2:3], edge_ends[:, 0:1], edge_ends[:, 1:2], ALU.is_equal))
            dve.wait_ge(S("pool_const"), 13)
            dve.wait_ge(S("w_turned"), 1)
            do(CP(WG[:, :], ps[:, 0, 0:128]))
            for h in range(2):
                lo, hi = D * h, D * h + D
                do(CP(WE[lo:hi, 68 * h:68 * h + D], ps[lo:hi, 1, lo:hi]))
            do(CP(WU[:, :], ps[:, 2, 0:D]))
            for m, (w, t, at, step) in enumerate(((w_edge2, WE, D, 68), (w_node2, WN, D, 72), (w_node2, WN, D + HEADS, 72))):
                do(TT(wtmp[:, :], w[:, :], attn[:, m, :], ALU.mult))
                for h in range(2):
                    lo, hi = D * h, D * h + D
                    do(dve.tensor_reduce(t[lo:hi, step * h + at:step * h + at + HEADS],
                                         wtmp[lo:hi, :].rearrange("p (h d) -> p h d", h=HEADS), AX, ALU.add))
            dve.wait_ge(S("loaded_x"), 16)
            tell("in_message")
            tell("z_free")
            dve.wait_ge(S("records"), 32)

            def take(name, n, us, ins):
                dve.wait_ge(S("lin_done"), group_base[name] + n + 1)
                ins(n, us).then_inc(S("lin_taken"), 1)
                dve.wait_ge(S("lin_taken"), group_base[name] + n + 1)

            def product(name, op):
                ncol = LINEARS[name][2]
                per = 2 if len(LINEARS[name][0]) < B else 1
                for n, us in enumerate(groups(name)):
                    nb = len(us) * per
                    b0 = n * GROUP * per
                    v = ps[0:P, 2 + (group_base[name] + n) % 2, 0:len(us) * ncol].rearrange("p (b f) -> p b f", b=nb)
                    take(name, n, us, lambda n, us: op(v, b0, nb))

            def rsqrt(t, w=B):
                do(CP(rs_in[:, 0:w], t))
                tell("root_in")
                roots[0] += 1
                dve.wait_ge(S("root_out"), roots[0])
                y, z = nt[:, 2, 0:w], nt[:, 3, 0:w]
                do(dve.reciprocal(y, rs_out[:, 0:w]))
                do(TT(z, y, y, ALU.mult))
                do(TT(z, z, rs_in[:, 0:w], ALU.mult))
                do(TS(z, z, -0.5, 1.5, ALU.mult, ALU.add))
                do(TT(t, y, z, ALU.mult))

            roots = [0]

            def layer_norm():
                m, v = nt[:, 0, 0:B], nt[:, 1, 0:B]
                do(dve.tensor_reduce(m, X[:, :, :], AX, ALU.add))
                do(TS(m, m, 1.0 / D, None, ALU.mult))
                do(TT(X[:, :, :], X[:, :, :], over(m, D), ALU.subtract))
                do(TT(tmp64, X[:, :, :], X[:, :, :], ALU.mult))
                do(dve.tensor_reduce(v, tmp64, AX, ALU.add))
                do(TS(v, v, 1.0 / D, EPS, ALU.mult, ALU.add))
                rsqrt(v)
                do(TT(X[:, :, :], X[:, :, :], over(v, D), ALU.mult))

            def copy_keep(r, i, k):
                TS(keepc[:, :], keep[:, bass.ds(i * (BUFS * U) + k * U, U)], 1.0, None, ALU.mult).then_inc(PS("keepc_ready", r), 1)

            def first_indices():
                for k in range(BUFS):
                    CP(idx[k][:, :], srcI[:, k * U:(k + 1) * U]).then_inc(S("idx_ready"), 1)
                dve.wait_ge(S("idx_ready"), BUFS)

            def next_indices(r, i, k):
                TS(idx[k][:, :], srcI[:, bass.ds(i * (BUFS * U) + (BUFS + k) * U, U)], 1, None, ALU.mult).then_inc(PS("idx_ready", r), 1)

            def scan(r, c, w):
                gc = c + (seq(r) * CHUNKS + 1)
                dve.wait_ge(PS("factor_ready", r), gc)
                dve.wait_ge(PS("rows_ready", r), gc)
                dve.tensor_tensor_scan(runs[:, 0:w * (U + 1)], factor[:, 0:w * (U + 1)], values[:, 0:w * (U + 1)], 0.0,
                                       ALU.mult, ALU.add).then_inc(PS("scanned", r), 1)
                dve.wait_ge(PS("scanned", r), gc)
                CP(run3(values, w)[:, :, 0:1], run3(runs, w)[:, :, U:U + 1]).then_inc(PS("carried", r), 1)
                dve.wait_ge(PS("carried", r), gc)

            def finish_sums(r):
                w, n0 = PASSW[r], seq(r) + 1
                dve.wait_ge(PS("rows_ready", r), n0 * CHUNKS + 1)
                tell(("cross_in_gcn" if r in GCN_NO else "cross_in"))
                dve.wait_ge(PS("nodes_gathered", r), 16 * B * n0)
                z = v3(Zflat, w)
                do(TT(z, z, over(mask[:, :], w), ALU.mult))
                dve.wait_ge(PS("cross_out", r), n0)
                for n in range(0, B, 8):
                    m = min(8, B - n)
                    do(TT(z[:, n:n + m, :], z[:, n:n + m, :], ps[0:P, n // 8, 0:m * w].rearrange("p (b f) -> p b f", b=m), ALU.add))
                return z

            def gcn_sums(r, table):
                w, z, n0 = PASSW[r], v3(Zflat, PASSW[r]), seq(r)
                tell("z_free_gcn")
                before = done[0]
                with dve.If(dense[0] == 1):
                    t3, left = parts3(w), v3(tmpf, w)
                    do(CP(t3[:, :, 0, :], table))
                    do(TT(left, table, t3[:, :, 0, :], ALU.subtract))
                    do(CP(t3[:, :, 1, :], left))
                    do(TT(t3[:, :, 2, :], left, t3[:, :, 1, :], ALU.subtract))
                    tell("parts_ready")
                    with dve.Fori(0, B // ABUFS) as i:
                        for k in range(ABUFS):
                            n = i * ABUFS + (n0 * B + k)
                            dve.wait_ge(S("a_used"), n + (ABUFS + 1))
                            dve.wait_ge(S("z_summed"), n + 1)
                            part = rows[:, k * D:k * D + w]
                            dve.tensor_reduce(part, ps[0:P, k, 0:3 * w].rearrange("p (t f) -> p f t", t=3), AX, ALU.add).then_inc(S("a_taken"), 1)
                            dve.wait_ge(S("a_taken"), n + (ABUFS + 1))
                            at = bass.ds(i * ABUFS + k, 1)
                            TT(z[:, at, :].rearrange("p a f -> p (a f)"), part, table[:, at, :].rearrange("p a f -> p (a f)"), ALU.add).then_inc(S("z_summed"), 1)
                    dve.wait_ge(S("z_summed"), (n0 + 1) * B + ABUFS)
                    dve.sem_inc(S("dve"), BRANCH - (done[0] - before))
                done[0] = before
                with dve.Else():
                    tell("table_ready_gcn")
                    do(dve.memset(values[:, :], 0.0))
                    do(dve.memset(factor[:, :], 0.0))
                    with dve.Fori(0, ITER) as i:
                        for k in range(BUFS):
                            c = i * BUFS + k
                            copy_keep(r, i, k)
                            dve.wait_ge(PS(f"gathered{k}", r), (i + (n0 * ITER + 1)) * (16 * U))
                            CP(run3(values, w)[:, :, 1:U + 1], chunk3(gath[k], w).rearrange("p j f -> p f j")).then_inc(PS("values_ready", r), 1)
                            dve.wait_ge(PS("values_ready", r), c + (n0 * CHUNKS + 1))
                            next_indices(r, i, k)
                            scan(r, c, w)
                    finish_sums(r)
                    do(TT(z, z, table, ALU.add))
                    dve.sem_inc(S("dve"), BRANCH - (done[0] - before))
                done[0] = before + BRANCH
                return z

            BRANCH = 32
            dense = [None]

            product("message", lambda v, b0, nb: TT(T64[:, b0:b0 + nb, :], v, row(bias[:, 0, :], nb), ALU.add))
            tell("table_ready")
            do(dve.memset(values[:, :], 0.0))
            do(dve.memset(checks[:, :], 0.0))
            do(dve.memset(checks[:, 7:8], -float(MAX_COUNT)))
            first_indices()
            tell("edge_taken")
            tell("edge_done", 2)
            tell("win_done", 4)
            tell("rec_used", BUFS)
            tell("idx_ready_gcn", BUFS)
            tell("a_taken", ABUFS)
            tell("z_summed", ABUFS)

            def take_edges(i, k, h):
                q = (i * BUFS + k) * 2 + h
                cols = i * (BUFS * U) + k * U
                dve.wait_ge(S("edge_done"), q + 3)
                g3 = chunk3(gath[k], D)
                banks = [(2 + b, HALVES[h][0] * 2 + 6 * b, 2 * min(3, len(HALVES[h]) - 3 * b)) for b in range(2)]
                for bank, at, n in banks:
                    v = ps[0:P, bank, 0:n * 68].rearrange("p (j f) -> p j f", j=n)
                    TS(edge_logit[:, bass.ds(cols + at, n), :], v[:, :, D:D + HEADS], 1.0, None, ALU.mult)
                if h == 0:
                    dve.wait_ge(S(f"gathered{k}"), (i + 1) * (16 * U))
                for bank, at, n in banks:
                    v = ps[0:P, bank, 0:n * 68].rearrange("p (j f) -> p f j", j=n)
                    last = TT(run3(values, D)[:, :, 1 + at:1 + at + n], g3[:, at:at + n, :].rearrange("p j f -> p f j"), v[:, 0:D, :], ALU.add)
                last.then_inc(S("edge_taken"), 1)
                dve.wait_ge(S("edge_taken"), q + 2)

            def hist(i, k, part):
                n = (i * BUFS + k) * 3 + part
                dve.wait_ge(S("hot_used"), n + 1)
                at = bass.ds((i * BUFS + k) * (3 * HC) + part * HC, HC)
                TT(hotP, pnode[:, at].unsqueeze(2).to_broadcast([P, HC, P]), iotaP[:, :].unsqueeze(1).to_broadcast([P, HC, P]), ALU.is_equal)
                TT(hotB, bnode[:, at].unsqueeze(2).to_broadcast([P, HC, B]),
                   iotaB[:, :].unsqueeze(1).to_broadcast([P, HC, B]), ALU.is_equal).then_inc(S("hot_ready"), 1)

            def window_keys(i, k):
                n = i * BUFS - (HIST_CHUNKS - k)
                dve.wait_ge(S(f"rec{k}"), (i - (HIST_CHUNKS // BUFS - 1)) * (16 * WINS))
                TT(key[:, :, :], rec[k][:, :, :, 0], win_off[:, :].unsqueeze(2).to_broadcast([128, WINS, 2]), ALU.subtract).then_inc(S("keys_ready"), 1)
                dve.wait_ge(S("keys_ready"), n * 2 + 1)
                TS(win_off[:, :], win_off[:, :], float(P * B), None, ALU.add).then_inc(S("keys_ready"), 1)
                dve.wait_ge(S("keys_ready"), n * 2 + 2)

            def windows(i, k, ws):
                for w in ws:
                    at = (i * BUFS - (HIST_CHUNKS - k)) * WINS + w
                    dve.wait_ge(S("win_done"), at + (4 if w == 0 else 1))
                    hb = winhot[w % 4]
                    for c in range(2):
                        TS(hb[:, c * WIN * B:(c + 1) * WIN * B], iotaW[:, :], key[:, w, c:c + 1], None, ALU.is_equal)
                        last = TS(hb[:, 2 * WIN * B + c * P:2 * WIN * B + (c + 1) * P], iotaP128[:, :], rec[k][:, w, c, 1:2], None, ALU.is_equal)
                    last.then_inc(S("winhot"), 1)

            for lo, hi, side in ((0, HIST_CHUNKS // BUFS, hist), (HIST_CHUNKS // BUFS, ITER, windows)):
                with dve.Fori(lo, hi) as i:
                    for k in range(BUFS):
                        c = i * BUFS + k
                        steps = SIDE[side is windows]
                        if side is windows:
                            window_keys(i, k)
                        copy_keep(0, i, k)
                        side(i, k, steps[0])
                        take_edges(i, k, 0)
                        side(i, k, steps[1])
                        take_edges(i, k, 1)
                        next_indices(0, i, k)
                        side(i, k, steps[2])
                        if side is windows:
                            n = c - HIST_CHUNKS
                            dve.wait_ge(S("winhot"), n * WINS + WINS)
                            dve.sem_inc(S("rec_used"), 1)
                        dve.wait_ge(S("messages_ready"), c + 1)
                        if side is windows:
                            dve.wait_ge(S("checked"), n + 1)
                            TT(checks[:, 0:1], checks[:, 0:1], checks[:, 1 + k:2 + k], ALU.max).then_inc(S("check_kept"), 1)
                            dve.wait_ge(S("check_kept"), n + 1)
                        scan(0, c, D)
                if side is windows:
                    break
                dve.wait_ge(S("hot_used"), HIST_CHUNKS * 3 + 1)
                do(CP(deg[:, :], ps[0:P, 7, 0:B]))
                tell("cum_in")
                dve.wait_ge(S("cum_out"), 1)
                tot, before_block, first = nt[:, 0, 0:B], nt[:, 1, 0:B], nt[:, 2, 0:B]
                do(CP(tot, ps[0:P, 7, 128:128 + B]))
                do(dve.tensor_tensor_scan(before_block, ones[:, 0:B], tot, 0.0, ALU.mult, ALU.add))
                do(TT(before_block, before_block, tot, ALU.subtract))
                do(TT(cum[:, :], ps[0:P, 7, 64:64 + B], before_block, ALU.add))
                tell("cum_in")
                do(TT(first, cum[:, :], deg[:, :], ALU.subtract))
                do(CP(startnI[:, :], first))
                do(dve.memset(starts, E))
                tell("starts_ready")
                dve.wait_ge(S("cum_out"), 2)
                do(TT(tot, ps[0:P, 7, 192:192 + B], first, ALU.subtract))
                do(TS(tot, tot, float(WIN_EDGES), None, ALU.is_gt))
                do(dve.tensor_reduce(checks[:, 0:1], tot, AX, ALU.max))
                do(TS(endI[:, :], cum[:, :], -1.0, 0.0, ALU.add, ALU.max))
                tell("ends_ready")
                do(TS(mask[:, :], deg[:, :], 1.0, None, ALU.min))
                do(TT(first, first, mask[:, :], ALU.mult))
                do(TS(tot, mask[:, :], -1.0, 1.0, ALU.mult, ALU.add))
                do(TS(before_block, node_no[:, :], float(E), None, ALU.add))
                do(TT(tot, tot, before_block, ALU.mult))
                do(TT(startI[:, :], first, tot, ALU.add))
                do(TS(dis[:, :], deg[:, :], 1.0, None, ALU.add))
                rsqrt(dis[:, :])
            tell("x_fixed")
            dve.wait_ge(S("win_copied"), ABLOCKS * PAIRS_W + 3)
            for k in range(BUFS):
                dve.wait_ge(S(f"block_stored{k}"), 16 * (ABLOCKS // BUFS + 1))
            dve.wait_ge(S("win_done"), ABLOCKS * WINS + 4)
            tell("spare_free")
            tell("checks_in")
            dve.wait_ge(S("checks_out"), 1)
            do(TS(flagI[:, :], ps[0:P, 7, 256:257], FLAG_AT, None, ALU.is_le))
            tell("flag_ready")
            dense[0] = dve.value_load(flagI[0:1, 0:1], min_val=0, max_val=1)
            dve.wait_ge(S("cross_iota"), 1)
            do(TS(cross_sel[:, :], cross_sel[:, :], edge_ends[:, 0:1], edge_ends[:, 2:3], ALU.is_equal, ALU.mult))

            finish_sums(0)
            z = v3(Zflat, D)
            dve.wait_ge(S("xz_x"), 1)
            do(CP(XZ[:, :, D:2 * D], z))
            tell("z_free")
            tell("in_update")
            product("update", lambda v, b0, nb: TT(tmp64[:, b0:b0 + nb, :], v, row(bias[:, 1, :], nb), ALU.add))
            do(STT(X[:, :, :], tmp64, 0.0, X[:, :, :], ALU.max, ALU.add))
            layer_norm()

            tell("in_gcn11")
            product("gcn11", lambda v, b0, nb: TT(T32[:, b0:b0 + nb, :], v, over(dis[:, b0:b0 + nb], 32), ALU.mult))
            z = gcn_sums(1, T32)
            do(TT(z, z, over(dis[:, :], 32), ALU.mult))
            do(TT(z, z, row(bias[:, 2, 0:32], B), ALU.add))
            do(STT(T32, z, 0.0, over(dis[:, :], 32), ALU.max, ALU.mult))
            z = gcn_sums(2, T32)
            do(dve.memset(tmp64, 0.0))
            do(TT(tmp64[:, :, 0:32], z, over(dis[:, :], 32), ALU.mult))
            tell("in_gcn12")
            product("gcn12", lambda v, b0, nb: TT(X[:, b0:b0 + nb, :], X[:, b0:b0 + nb, :], v, ALU.add))
            do(TT(X[:, :, :], X[:, :, :], row(bias[:, 3, :], B), ALU.add))
            layer_norm()

            do(dve.memset(big[:, :], 0.0))
            tell("in_attend")
            product("attend", lambda v, b0, nb: CP(T72[:, b0:b0 + nb, :], v))
            tell("table_ready")
            dve.wait_ge(S("query_back"), 16)
            dve.wait_ge(S("query_first"), 16)
            do(CP(query[:, 0, :], w0[:, :]))
            for h in range(HEADS):
                do(dve.tensor_tensor_scan(query[:, :, h], keep[:, :], query[:, :, h], 0.0, ALU.mult, ALU.add))
            do(TT(edge_logit[:, :, :], edge_logit[:, :, :], query, ALU.add))
            do(dve.memset(values[:, :], 0.0))
            do(dve.memset(factor[:, :], 0.0))
            do(dve.memset(mrun[:, :, :], -BIG))
            loop_base, STEPS = done[0], 14
            with dve.Fori(0, ITER) as i:
                for k in range(BUFS):
                    c = i * BUFS + k
                    n = [0]

                    def ldo(ins):
                        n[0] += 1
                        ins.then_inc(S("dve"), 1)
                        dve.wait_ge(S("dve"), c * STEPS + (loop_base + n[0]))

                    cols = bass.ds(i * (BUFS * U) + k * U, U)
                    dve.wait_ge(S(f"gathered{k}"), (i + (ITER + 1)) * (16 * U))
                    g3 = chunk3(gath[k], ROW2)
                    ldo(TT(logit[:, :, :], edge_logit[:, cols, :], g3[:, :, D:ROW2], ALU.add))
                    ldo(STT(logitT[:, :, :].rearrange("p h j -> p j h"), logit[:, :, :], 0.01, logit[:, :, :], ALU.mult, ALU.max))
                    ldo(TS(keepn[:, :], keep[:, cols], -1.0, BIG, ALU.add, ALU.mult))
                    dve.wait_ge(S("rows_ready"), c + (CHUNKS + 1))
                    for h in range(HEADS):
                        ldo(dve.tensor_tensor_scan(mrun[:, h, 1:U + 1], keepn[:, :], logitT[:, h, :], mrun[:, h, 0:1], ALU.add, ALU.max))
                    ldo(TT(expo[:, 0, :, :], mrun[:, :, 0:U], keepn[:, :].unsqueeze(1).to_broadcast([P, HEADS, U]), ALU.add))
                    ldo(TT(expo[:, 0, :, :], expo[:, 0, :, :], mrun[:, :, 1:U + 1], ALU.subtract))
                    TT(expo[:, 1, :, :], logitT[:, :, :], mrun[:, :, 1:U + 1], ALU.subtract).then_inc(S("expo_in"), 1)
                    dve.wait_ge(S("expo_in"), c + 1)
                    dve.wait_ge(S("expo_out"), c + 1)
                    v4 = run3(values, ROW2).rearrange("p (h e) j -> p h e j", h=HEADS)
                    for h in range(HEADS):
                        ins = TT(v4[:, h, 0:HD, 1:U + 1], g3[:, :, h * HD:(h + 1) * HD].rearrange("p j d -> p d j"),
                                 expo[:, 1, h, :].unsqueeze(1).to_broadcast([P, HD, U]), ALU.mult)
                        if h < HEADS - 1:
                            ldo(ins)
                        else:
                            ins.then_inc(S("values_ready"), 1)
                            dve.wait_ge(S("values_ready"), c + 1)
                    ldo(CP(v4[:, :, HD, 1:U + 1], expo[:, 1, :, :]))
                    next_indices(3, i, k)
                    scan(3, c, ROW2)
                    dve.wait_ge(S("rows_ready"), c + (CHUNKS + 2))
                    ldo(CP(mrun[:, :, 0:1], mrun[:, :, U:U + 1]))
                    assert n[0] == STEPS
            done[0] = loop_base + CHUNKS * STEPS
            last_row = chunk3(rows, ROW2 + HEADS)[:, U - 1, :]
            dm = v3(tmpf, P, 6)
            for m in range(6):
                col = last_row[:, ROW2 + m:ROW2 + m + 1] if m < HEADS else edge_ends[:, (0, 2)[m - HEADS]:(0, 2)[m - HEADS] + 1]
                do(TS(dm[:, m, :], ident[0:P, 0:P], col, None, ALU.mult))
            tell("diag_ready")
            dve.wait_ge(S("diag_out"), 1)
            same, t2 = dm[:, 0, :], dm[:, 1, :]
            do(TS(same, ps[0:P, 1, 0:P], edge_ends[:, 0:1], None, ALU.is_equal))
            do(TT(same, same, ps[0:P, 1, P:2 * P], ALU.mult))
            for h in range(HEADS):
                do(TT(t2, same, ps[0:P, 0, h * P:(h + 1) * P], ALU.mult))
                do(TS(dm[:, 2, :], same, -1.0, BIG, ALU.add, ALU.mult))
                do(TT(t2, t2, dm[:, 2, :], ALU.add))
                do(dve.tensor_reduce(bmax[:, 0, h:h + 1], t2, AX, ALU.max))
            do(TT(t2, same, tri[:, :], ALU.mult))
            do(dve.tensor_reduce(edge_ends[:, 3:4], t2, AX, ALU.max))
            do(TS(edge_ends[:, 3:4], edge_ends[:, 3:4], -1.0, 1.0, ALU.mult, ALU.add))
            do(TT(edge_ends[:, 3:4], edge_ends[:, 3:4], edge_ends[:, 2:3], ALU.mult))
            do(TT(bmax[:, 2, :], last_row[:, ROW2:ROW2 + HEADS], bmax[:, 0, :], ALU.subtract))
            do(TS(bmax[:, 2, :], bmax[:, 2, :], 0.0, None, ALU.min))
            tell("bexp_in")
            dve.wait_ge(S("bexp_out"), 1)
            do(TT(bnd[:, 0:ROW2].rearrange("p (h e) -> p h e", h=HEADS), last_row[:, 0:ROW2].rearrange("p (h e) -> p h e", h=HEADS),
                  bmax[:, 2, :].unsqueeze(2).to_broadcast([P, HEADS, AW]), ALU.mult))
            do(TS(bnd[:, ROW2:ROW2 + HEADS], bmax[:, 0, :], edge_ends[:, 3:4], None, ALU.mult))
            do(CP(bnd[:, ROW2 + HEADS:ROW2 + HEADS + 1], edge_ends[:, 3:4]))
            tell("cross_in")
            dve.wait_ge(S("cross_out"), 2)
            CW = CORRW[3]
            cr = v3(tmpf, CW)
            per = BANK // CW
            for n in range(0, B, per):
                m = min(per, B - n)
                do(CP(cr[:, n:n + m, :], ps[0:P, n // per, 0:m * CW].rearrange("p (b f) -> p b f", b=m)))
            dve.wait_ge(S("nodes_gathered"), 16 * B * 2)
            z = v3(Zflat, ROW2 + HEADS)
            e1, e2 = v3(Tflat, HEADS), Tflat[:, B * HEADS:2 * B * HEADS].rearrange("p (b h) -> p b h", b=B)
            mx = Tflat[:, 2 * B * HEADS:3 * B * HEADS].rearrange("p (b h) -> p b h", b=B)
            has = nt[:, 0, 0:B]
            do(TS(has, cr[:, :, ROW2 + HEADS], -1.0, BIG, ALU.add, ALU.mult))
            do(TT(e2, cr[:, :, ROW2:ROW2 + HEADS], over(has, HEADS), ALU.add))
            do(TT(mx, z[:, :, ROW2:ROW2 + HEADS], e2, ALU.max))
            do(TT(e1, z[:, :, ROW2:ROW2 + HEADS], mx, ALU.subtract))
            do(TT(e2, e2, mx, ALU.subtract))
            tell("nexp_in")
            dve.wait_ge(S("nexp_out"), 1)
            for h in range(HEADS):
                zh, ch = z[:, :, h * AW:(h + 1) * AW], cr[:, :, h * AW:(h + 1) * AW]
                do(TT(zh, zh, over(e1[:, :, h], AW), ALU.mult))
                do(TT(ch, ch, over(e2[:, :, h], AW), ALU.mult))
                do(TT(zh, zh, ch, ALU.add))
                rd = nt[:, 1, 0:B]
                do(dve.reciprocal(rd, zh[:, :, HD]))
                do(TT(rd, rd, mask[:, :], ALU.mult))
                do(TT(zh[:, :, 0:HD], zh[:, :, 0:HD], over(rd, HD), ALU.mult))
                xh = X[:, :, h * HD:(h + 1) * HD]
                do(STT(xh, xh, 2.0, zh[:, :, 0:HD], ALU.mult, ALU.add))
            do(TT(X[:, :, :], X[:, :, :], row(bias[:, 4, :], B), ALU.add))
            layer_norm()

            for n in range(2):
                r = 4 + n
                b_, gamma, beta = bias[:, 5 + 3 * n, :], bias[:, 6 + 3 * n, :], bias[:, 7 + 3 * n, :]
                do(TT(T64, X[:, :, :] if n == 0 else T64, over(dis[:, :], D), ALU.mult))
                z = gcn_sums(r, T64)
                do(TT(tmp64, z, over(dis[:, :], D), ALU.mult))
                name = ("gcn31", "gcn32")[n]
                tell("in_" + name)
                product(name, lambda v, b0, nb: TT(T64[:, b0:b0 + nb, :], v, row(b_, nb), ALU.add))
                s0, s1 = nt[:, 0, :], nt[:, 1, :]
                for m in range(2):
                    if m == 0:
                        do(dve.tensor_reduce(s0, T64.rearrange("p b f -> p f b"), AX, ALU.add))
                    else:
                        do(TT(tmp64, T64, T64, ALU.mult))
                        do(dve.tensor_reduce(s0, tmp64.rearrange("p b f -> p f b"), AX, ALU.add))
                    tell("colsum_in")
                    dve.wait_ge(S("colsum_out"), 2 * n + m + 1)
                    do(TS(s1, ps[0:P, 7, 0:D], 1.0 / N, EPS * m, ALU.mult, ALU.add))
                    if m == 0:
                        do(TT(T64, T64, row(s1, B), ALU.subtract))
                rsqrt(s1, D)
                do(TT(s1, s1, gamma, ALU.mult))
                do(TT(T64, T64, row(s1, B), ALU.mult))
                do(TT(T64, T64, row(beta, B), ALU.add))
                do(STT(T64, T64, 0.01, T64, ALU.mult, ALU.max))
            do(TT(X[:, :, :], X[:, :, :], T64, ALU.add))
            layer_norm()
            tell("result")


def kernel(**inputs):
    import numpy as np
    import concourse.bacc as bacc
    from concourse.bass_utils import run_bass_kernel_spmd as run

    nc = bacc.Bacc("TRN2", target_bir_lowering=False, num_devices=1)
    arrays, args = {}, {}
    for name, value in inputs.items():
        v = np.ascontiguousarray(value)
        arrays[name] = v
        args[name] = nc.dram_tensor(name, v.shape, mybir.dt.from_np(v.dtype), kind="ExternalInput").ap()
    out = nc.dram_tensor("out", inputs["x"].shape, F32, kind="ExternalOutput").ap()
    gnn_kernel(nc, args, out)
    r = run(nc, [arrays], core_ids=[0])
    return r.results[0]["out"]
```

```python
import concourse.bass as bass
from concourse import mybir
from contextlib import ExitStack

F32 = mybir.dt.float32
BF16 = mybir.dt.bfloat16
F16 = mybir.dt.float16
F8 = mybir.dt.float8e4
I32 = mybir.dt.int32
ALU = mybir.AluOpType
ACT = mybir.ActivationFunctionType
AX = mybir.AxisListType.X

P = 125
D = 64
HEADS = 4
HD = D // HEADS
BIG = 1.0e30
GROUP = 3
LIN = 3
BANK = 512
U = 22
BUFS = 3
PAIRS = U // 2
EPS = 1e-5
WIN = 5
STEP = 25
WIN_EDGES = 2 * P
WINS = P // WIN
PEAK = 16384.0
MAX_COUNT = 15
ABUFS = 5
HIST_CHUNKS = 21
FIRST_BLOCK = 24
FLAG_AT = 0.5
HC = 10
HSTEPS = 8
AW = HD + 1
ROW2 = HEADS * AW


def gnn_kernel(nc, a, out):
    N, E = a["x"].shape[0], a["src"].shape[0]
    B, J = N // P, E // P
    CHUNKS = J // U
    WGROUPS = N // (WIN * P)
    ITER = CHUNKS // BUFS
    assert CHUNKS - FIRST_BLOCK == B + 1 and B % BUFS == BUFS - 1
    assert HIST_CHUNKS % BUFS == 0 and FIRST_BLOCK % BUFS == 0 and HIST_CHUNKS * HSTEPS * HC >= J and WINS * WIN == P
    assert B * P == N and J * P == E and CHUNKS * U == J and ITER * BUFS == CHUNKS

    ctx = ExitStack()
    with ctx:
        def sb(name, shape, dt=F32):
            return ctx.enter_context(nc.sbuf_tensor(name, shape, dt))

        sems = {}

        def S(name):
            if name not in sems:
                sems[name] = ctx.enter_context(nc.semaphore(name))
            return sems[name]

        def dram(name, shape):
            return nc.dram_tensor(name, shape, F32, kind="Internal").ap()

        adjacency = nc.dram_tensor("adjacency", [B, P, B * P // 2], BF16, kind="Internal").ap()
        SEGS = P // STEP
        WROWS = E // P * SEGS + 2 * SEGS
        FILLERS = (WROWS // SEGS + 1) * P - STEP - E
        assert SEGS * STEP == P and FILLERS % SEGS == 0
        records = dram("records", [E + FILLERS, 2])
        wide_records = dram("wide_records", [WROWS, 2 * P])
        start_node = nc.dram_tensor("start_node", [N, 1], I32, kind="Internal").ap()
        tables = [dram(f"table{r}", [N, w]) for r, w in enumerate((D, 32, 32, ROW2, D, D))]
        sums = [dram(f"sums{r}", [E, w]) for r, w in enumerate((D, 32, 32, ROW2 + HEADS, D, D))]
        query_table = dram("query_table", [N, HEADS])
        query_start = dram("query_start", [E + N, HEADS])

        srcI = sb("srcI", [P, J + BUFS * U], I32)
        keep = sb("keep", [P, J])
        edge_logit = sb("edge_logit", [P, J, HEADS])
        big = sb("big", [P, J * HEADS])
        spare = sb("spare", [128, N])
        cross_sel = spare[0:P, :]
        X = sb("X", [P, B, D])
        Tflat = sb("Tflat", [P, B * (D + 2 * HEADS)])
        Zflat = sb("Zflat", [P, B * (ROW2 + HEADS)])
        tmpf = sb("tmpf", [P, B * (ROW2 + HEADS + 1)])
        idx = [sb(f"idx{k}", [P, U], I32) for k in range(BUFS)]
        gath_all = sb("gath_all", [P, BUFS * U * ROW2])
        gath = [gath_all[:, k * U * ROW2:(k + 1) * U * ROW2] for k in range(BUFS)]
        keepc = sb("keepc", [P, U])
        factor = sb("factor", [P, ROW2 * (U + 1)])
        values = sb("values", [P, ROW2 * (U + 1)])
        runs = sb("runs", [P, ROW2 * (U + 1)])
        rows = sb("rows", [P, U * (ROW2 + HEADS)])
        xT = sb("xT", [128, PAIRS, P])
        lin_in = [xT[:, 4 * i:4 * i + GROUP, :] for i in range(LIN)]
        ident = sb("ident", [128, 128])
        ones = sb("ones", [P, P])
        tri = sb("tri", [P, P])
        iotaP = sb("iotaP", [P, P], BF16)
        iotaB = sb("iotaB", [P, B], BF16)
        node_no = sb("node_no", [P, B])
        prep = spare[:, 3 * J:]
        srcG, srcE, srcU = prep[:, 0:128], prep[:, 128:256], prep[0:D, 256:384]
        WG = sb("WG", [128, 128])
        WE = sb("WE", [128, 2 * (D + HEADS)])
        WU = sb("WU", [128, D])
        WN = sb("WN", [128, 2 * (D + 2 * HEADS)])
        W11 = sb("W11", [128, D])
        W12 = sb("W12", [128, 128])
        W31 = sb("W31", [128, 128])
        W32 = sb("W32", [128, 128])
        w_edge2, w_node2, wtmp = prep[:, 384:384 + D], prep[:, 448:448 + D], prep[:, 512:512 + D]
        attn = prep[:, 576:576 + 3 * D].rearrange("p (m n) -> p m n", m=3)
        bias = sb("bias", [P, 11, D])
        deg = sb("deg", [P, B])
        dis = sb("dis", [P, B])
        mask = sb("mask", [P, B])
        cum = sb("cum", [P, B])
        nt = sb("nt", [P, 4, D])
        endI = sb("endI", [P, B], I32)
        startnI = sb("startnI", [P, B], I32)
        startI = sb("startI", [P, B], I32)
        firstI = sb("firstI", [P, 2], I32)
        nextI = sb("nextI", [P, 2], I32)
        edge_ends = sb("edge_ends", [P, 4])
        tri_incl = sb("tri_incl", [P, P])
        shift4 = sb("shift4", [P, P])
        iotaW = sb("iotaW", [P, WIN * B], BF16)
        win_off = sb("win_off", [P, P])
        winI = sb("winI", [P, 2, WGROUPS], I32)
        keys_all = sb("keys_all", [P, BUFS * WINS * 4])
        keys_of = [keys_all[:, k * WINS * 4:(k + 1) * WINS * 4].rearrange("p (w c) -> p w c", w=WINS) for k in range(BUFS)]
        checks = sb("checks", [P, 16])
        check_max, check_bias = checks[:, 0:3], checks[:, 15:16]
        check_parts = [checks[:, 3 + 3 * k:6 + 3 * k] for k in range(BUFS)]
        flagI = sb("flagI", [P, 1], I32)
        rs_in = sb("rs_in", [P, D])
        rs_out = sb("rs_out", [P, D])
        w0 = sb("w0", [P, HEADS])
        mrun = sb("mrun", [P, HEADS, U + 1])
        logit = tri_incl[:, 0:U * HEADS].rearrange("p (j h) -> p j h", h=HEADS)
        keepn = tri_incl[:, U * HEADS:U * HEADS + U]
        logitT = shift4[:, 0:U * HEADS].rearrange("p (h j) -> p h j", h=HEADS)
        expo = keys_all[:, 0:2 * HEADS * U].rearrange("p (t h j) -> p t h j", t=2, h=HEADS)
        bnd = keys_all[:, 2 * HEADS * U:2 * HEADS * U + ROW2 + HEADS + 1]
        bmax = sb("bmax", [P, 3, HEADS])

        xe = [big[:, k * U * D:(k + 1) * U * D] for k in range(BUFS)]
        o = BUFS * U * D
        hotP, hotB = [], []
        for n in range(2):
            hotP.append(big[:, o:o + HC * P // 2].bitcast(BF16).rearrange("p (j n) -> p j n", j=HC))
            o += HC * P // 2
            hotB.append(big[:, o:o + HC * B // 2].bitcast(BF16).rearrange("p (j n) -> p j n", j=HC))
            o += HC * B // 2
        assert o <= J * HEADS and HC % 2 == 0 and HSTEPS % 2 == 0
        XZ = big[:, 0:B * 2 * D].rearrange("p (b f) -> p b f", b=B)
        query = big[:, :].rearrange("p (j h) -> p j h", h=HEADS)
        dstI = Zflat[:, 0:J].bitcast(I32)
        JH = HIST_CHUNKS * HSTEPS * HC
        dstF = Zflat[:, JH:JH + J]
        node_half = Zflat[:, 0:JH].bitcast(BF16)
        pnode, bnode = node_half[:, 0:JH], node_half[:, JH:2 * JH]
        RAW = 4 * P
        raw = [t[:, n * RAW:(n + 1) * RAW].rearrange("p (c j v) -> p c j v", c=2, j=P)
               for t, count in ((Tflat, 7), (tmpf, WGROUPS - 7)) for n in range(count)]
        raw_flat = [t[:, n * RAW:(n + 1) * RAW] for t, count in ((Tflat, 7), (tmpf, WGROUPS - 7)) for n in range(count)]
        keys = Zflat[:, 0:B * WINS * 4 // 2].bitcast(BF16)
        edge_rec = edge_logit[:, J // 2:, :].rearrange("p j (a v) -> p (j a) v", v=2)
        AB4 = B * P // 4 + 1
        ablock_space = [spare[0:P, n * AB4:(n + 1) * AB4] for n in range(BUFS)]
        ablock = [t.bitcast(F8)[:, 0:B * P].rearrange("p (b d) -> p b d", b=B) for t in ablock_space]
        junk = tmpf[:, 0:AB4].bitcast(F8)[:, 0:B * P].rearrange("p (b d) -> p b d", b=B)
        WK = WIN * B + P
        HOTS = 8
        winhot = [Tflat[:, n * WK:(n + 1) * WK].bitcast(BF16) for n in range(HOTS + 1)]
        assert BUFS * AB4 <= N and (HOTS + 1) * WK <= B * (D + 2 * HEADS) and WINS % HOTS == 1
        abuf_space = [values[:, 0:AB4], factor[:, 0:AB4], runs[:, 0:AB4], gath_all[:, 0:AB4], gath_all[:, AB4:2 * AB4]]
        abuf = [t.bitcast(F8)[:, 0:B * P].rearrange("p (b d) -> p b d", b=B) for t in abuf_space]

        def pairs_of_bytes(t):
            return t.bitcast(BF16)[:, 0:B * P // 2]

        PARTS = {D: 2, 32: 3}

        def parts(w):
            n = PARTS[w]
            return big[:, 0:B * n * w // 2].bitcast(F16).rearrange("p (b t f) -> p b t f", b=B, t=n)

        ps = ctx.enter_context(nc.psum_tensor("ps", [128, 8, BANK], F32))

        def v3(t, w, n=B):
            return t[:, 0:n * w].rearrange("p (b f) -> p b f", b=n)

        def chunk3(t, w):
            return t[:, 0:U * w].rearrange("p (j f) -> p j f", j=U)

        def run3(t, w):
            return t[:, 0:w * (U + 1)].rearrange("p (f j) -> p f j", f=w)

        def rowsof(r, i, k):
            v = sums[r].rearrange("(p j) f -> p j f", p=P)
            return v[:, bass.ds(i * (BUFS * U) + k * U, U), :]

        PASSW = (D, 32, 32, ROW2, D, D)
        GCN_NO = {1: 0, 2: 1, 4: 2, 5: 3}

        def seq(r):
            return GCN_NO[r] if r in GCN_NO else r // 3

        def PS(name, r):
            return S(name + "_gcn") if r in GCN_NO else S(name)
        CORRW = (D, 32, 32, ROW2 + HEADS + 1, D, D)

        def units(src, kind):
            if kind == "pair":
                return [src[:, 2 * u:2 * u + 2, :].rearrange("p b f -> p (b f)") for u in range(B // 2)]
            return [src[:, u, :] for u in range(B)]

        T64, T32, T72 = v3(Tflat, D), v3(Tflat, 32), v3(Tflat, D + 2 * HEADS)
        tmp64 = v3(tmpf, D)
        LINEARS = {
            "message": (units(X, "pair"), WG, 128),
            "update": (units(XZ, "one"), WU, D),
            "gcn11": (units(X, "pair"), W11, D),
            "gcn12": (units(tmp64, "pair"), W12, 128),
            "attend": (units(X, "pair"), WN, 2 * (D + 2 * HEADS)),
            "gcn31": (units(tmp64, "pair"), W31, 128),
            "gcn32": (units(tmp64, "pair"), W32, 128),
        }
        ORDER = list(LINEARS)
        group_base, g0 = {}, 0
        for name in ORDER:
            group_base[name] = g0
            g0 += -(-len(LINEARS[name][0]) // GROUP)

        def groups(name):
            us = LINEARS[name][0]
            return [us[i:i + GROUP] for i in range(0, len(us), GROUP)]

        BIASES = ("L0_gnn_M_b", "L0_gnn_U_b", "L1_gnn_b1", "L1_gnn_b2", "L2_gnn_bias", "L3_gnn_b1", "L3_gnn_gamma1",
                  "L3_gnn_beta1", "L3_gnn_b2", "L3_gnn_gamma2", "L3_gnn_beta2")
        W_LOADS = 16 + 3 + len(BIASES)

        HALVES = (range(0, 6), range(6, PAIRS))
        SIDE = ((range(0, 3), range(3, 6), range(6, HSTEPS)), (range(0, 8), range(8, 16), range(16, WINS)))
        PAIRS_W = (WINS + 1) // 2

        def pair_bank(p):
            return 7 if p == PAIRS_W - 1 else 4 + p % 3
        block = ctx.enter_context(nc.Block())

        @block.sync
        def _(sp):
            dense = [None]

            def load(dst, src, sem="loaded"):
                sp.dma_start(dst, src).then_inc(S(sem), 16)

            load(X[:, :, :], a["x"].rearrange("(b p) f -> p b f", p=P), "loaded_m")
            sp.wait_ge(S("zeroed"), 1)
            for h in range(2):
                load(srcG[D * h:D * h + D, D * h:D * h + D], a["L0_gnn_M_W"][:, 0:D], "loaded_m")
            load(bias[:, 0, :], a[BIASES[0]].rearrange("(a n) -> a n", a=1).to_broadcast([P, D]), "loaded_m")
            load(srcI[:, 0:J], a["src"].rearrange("(p j) -> p j", p=P), "loaded_src")
            load(dstI, a["dst"].rearrange("(p j) -> p j", p=P), "loaded_dst")
            dst2 = a["dst"].rearrange("(p j) -> p j", p=P)
            load(firstI[:, :], dst2[:, 0:2], "loaded_dst")
            load(nextI[0:P - 1, :], dst2[1:P, 0:2], "loaded_dst")
            n = 0
            for h in range(2):
                lo, hi = D * h, D * h + D
                for dst, src in (
                    (srcE[lo:hi, lo:hi], a["L0_gnn_M_W"][:, D:2 * D]),
                    (W11[lo:hi, 32 * h:32 * h + 32], a["L1_gnn_W1"]),
                    (W12[lo:lo + 32, lo:hi], a["L1_gnn_W2"]),
                    (WN[lo:hi, 72 * h:72 * h + D], a["L2_gnn_W_node"]),
                    (W31[lo:hi, lo:hi], a["L3_gnn_W1"]),
                    (W32[lo:hi, lo:hi], a["L3_gnn_W2"]),
                    (w_edge2[lo:hi, :], a["L2_gnn_W_edge"]),
                    (w_node2[lo:hi, :], a["L2_gnn_W_node"]),
                ):
                    load(dst, src, "loaded_w")
                    n += 1
            load(srcU[:, :], a["L0_gnn_U_W"], "loaded_w")
            for m, name in enumerate(("edge", "key", "query")):
                row = a[f"L2_gnn_attn_{name}"].rearrange("(a h) d -> a (h d)", a=1)
                load(attn[:, m, :], row.to_broadcast([128, D]), "loaded_w")
            for m, name in tuple(enumerate(BIASES))[1:]:
                v = a[name].rearrange("(a n) -> a n", a=1)
                w = v.shape[1]
                load(bias[:, m, 0:w], v.to_broadcast([P, w]), "loaded_w")
            assert n + 3 + len(BIASES) == W_LOADS

            def store_table(r, src):
                sp.wait_ge(PS("table_ready", r), seq(r) + 1)
                sp.dma_start(tables[r].rearrange("(b p) f -> p b f", p=P), src).then_inc(PS("table", r), 16)

            def gcn_loads(r, src):
                with sp.If(dense[0] == 1):
                    sp.wait_ge(S("parts_ready"), seq(r) + 1)
                    with sp.Fori(0, B // ABUFS) as i:
                        for k in range(ABUFS):
                            sp.wait_ge(S("a_used"), i * ABUFS + (seq(r) * B + k + 1))
                            sp.dma_start(pairs_of_bytes(abuf_space[k]),
                                         adjacency[bass.ds(i * ABUFS + k, 1), :, :].rearrange("a p n -> (a p) n")).then_inc(S(f"a{k}"), 16)
                with sp.Else():
                    store_table(r, src)

            store_table(0, T64)

            sp.wait_ge(S("records_ready"), 1)
            load(records[0:E, :].rearrange("(p j) v -> p j v", p=P), edge_rec, "records")
            load(records[E:E + FILLERS, :].rearrange("(p c) v -> p c v", c=SEGS),
                 keys_of[0][0:FILLERS // SEGS, 0:SEGS, 0:2], "records")
            sp.wait_ge(S("zeros_ready"), 1)
            query_flat = query_start[0:E, :].rearrange("(p j) h -> p (j h)", p=P)
            for lo, hi in ((0, N), (N, J * HEADS)):
                sp.dma_start(query_flat[:, lo:hi], spare[0:P, 0:hi - lo]).then_inc(S("query_zero"), 16)
            edges = a["edge_attr_64"].rearrange("(p j) f -> p j f", p=P)

            def load_edges(i, k):
                sp.wait_ge(S("xt_turned"), (i * BUFS + k) * 2 + 2)
                sp.dma_start(chunk3(xe[k % BUFS], D), edges[:, bass.ds(i * (BUFS * U) + k * U, U), :]).then_inc(S(f"xe{k % BUFS}"), 16)

            with sp.Fori(0, HIST_CHUNKS // BUFS) as i:
                for k in range(BUFS):
                    load_edges(i, k)
            load_edges(HIST_CHUNKS // BUFS, 0)
            sp.wait_ge(S("starts_ready"), 1)
            sp.dma_start(start_node.rearrange("(b p) a -> p b a", p=P), startnI[:, :].unsqueeze(2), allow_slow_non_contiguous=True).then_inc(S("starts_put"), 16)
            sp.wait_ge(S("starts_put"), 16)
            sp.dma_start(winI[:, 0, :].unsqueeze(2), start_node.rearrange("(g p d) a -> p g (d a)", g=WGROUPS, p=P)[:, :, 0:1],
                         allow_slow_non_contiguous=True).then_inc(S("starts_back"), 16)
            with sp.Fori(HIST_CHUNKS // BUFS, ITER - 1) as i:
                for k in range(BUFS):
                    load_edges(i, k + 1)
            for k in range(1, BUFS):
                load_edges(ITER - 1, k)
            sp.wait_ge(S("flag_ready"), 1)
            dense[0] = sp.value_load(flagI[0:1, 0:1], min_val=0, max_val=1)
            gcn_loads(1, T32)
            gcn_loads(2, T32)
            sp.wait_ge(S("table_ready"), 2)
            sp.dma_start(tables[3].rearrange("(b p) f -> p b f", p=P), T72[:, :, 0:ROW2]).then_inc(S("table"), 16)
            sp.dma_start(query_table.rearrange("(b p) f -> p b f", p=P), T72[:, :, ROW2:ROW2 + HEADS]).then_inc(S("query_table"), 16)
            sp.wait_ge(S("query_put"), 16 * B)
            sp.dma_start(big[:, :], query_start[0:E, :].rearrange("(p j) h -> p (j h)", p=P)).then_inc(S("query_back"), 16)
            gcn_loads(4, T64)
            gcn_loads(5, T64)
            sp.wait_ge(S("result"), 1)
            sp.dma_start(out.rearrange("(b p) f -> p b f", p=P), X[:, :, :]).then_inc(S("out"), 16)
            sp.wait_ge(S("out"), 16)

        @block.gpsimd
        def _(g):
            g.memset(ident[:, :], 0.0).then_inc(S("pool_const"), 1)
            g.memset(ones[:, :], 1.0).then_inc(S("pool_const"), 1)
            g.iota(iotaP[:, :], pattern=[[1, P]], base=0, channel_multiplier=0, allow_small_or_imprecise_dtypes=True).then_inc(S("pool_const"), 1)
            g.iota(iotaB[:, :], pattern=[[1, B]], base=0, channel_multiplier=0, allow_small_or_imprecise_dtypes=True).then_inc(S("pool_const"), 1)
            g.iota(node_no[:, :], pattern=[[P, B]], base=0, channel_multiplier=1, allow_small_or_imprecise_dtypes=True).then_inc(S("pool_const"), 1)
            g.iota(iotaW[:, :], pattern=[[1, WIN * B]], base=0, channel_multiplier=0, allow_small_or_imprecise_dtypes=True).then_inc(S("pool_const"), 1)
            g.iota(win_off[:, :], pattern=[[WIN * B, P]], base=0, channel_multiplier=0, allow_small_or_imprecise_dtypes=True).then_inc(S("pool_const"), 1)
            g.memset(shift4[:, :], 0.0).then_inc(S("pool_const"), 1)
            g.wait_ge(S("pool_const"), 8)
            g.affine_select(out=ident[:, :], in_=ident[:, :], compare_op=ALU.not_equal, fill=1.0, base=0,
                            pattern=[[-1, 128]], channel_multiplier=1).then_inc(S("pool_const"), 1)
            g.affine_select(out=tri[:, :], in_=ones[:, :], compare_op=ALU.is_gt, fill=0.0, base=0,
                            pattern=[[1, P]], channel_multiplier=-1).then_inc(S("pool_const"), 1)
            g.affine_select(out=tri_incl[:, :], in_=ones[:, :], compare_op=ALU.is_ge, fill=0.0, base=0,
                            pattern=[[1, P]], channel_multiplier=-1).then_inc(S("pool_const"), 1)
            g.affine_select(out=shift4[:, :], in_=shift4[:, :], compare_op=ALU.not_equal, fill=1.0, base=1 - WIN,
                            pattern=[[-1, P]], channel_multiplier=1).then_inc(S("pool_const"), 1)

            def gather(dst, table, index, sem):
                g.indirect_dma_start(out=dst, out_offset=None, in_=table,
                                     in_offset=bass.IndirectOffsetOnAxis(ap=index, axis=0)).then_inc(sem, 16)

            def edge_pass(r):
                w = PASSW[r]
                r0 = seq(r) * CHUNKS
                g.wait_ge(PS("table", r), 16 * (seq(r) + 1))
                for lo, hi in ((0, FIRST_BLOCK // BUFS), (FIRST_BLOCK // BUFS, ITER)) if r == 0 else ((0, ITER),):
                    if lo:
                        gather_windows()
                    gather_chunks(r, w, r0, lo, hi)

            def gather_chunks(r, w, r0, lo, hi):
                with g.Fori(lo, hi) as i:
                    for k in range(BUFS):
                        g.wait_ge(PS("idx_ready", r), i * BUFS + (r0 + k + 1))
                        g.sem_inc(S("gather_begun"), 1)
                        for j in range(U):
                            gather(chunk3(gath[k], w)[:, j, :], tables[r], idx[k][:, j:j + 1], PS(f"gathered{k}", r))

            def gather_windows():
                g.wait_ge(S("starts_back"), 16)
                g.tensor_scalar(winI[:, 1, :], winI[:, 0, :], SEGS, None, ALU.add).then_inc(S("win_index"), 1)
                g.wait_ge(S("win_index"), 1)
                g.wait_ge(S("wide_records"), 16 * SEGS)
                for n in range(WGROUPS):
                    for c in range(2):
                        gather(raw_flat[n][:, c * 2 * P:(c + 1) * 2 * P], wide_records, winI[:, c, n:n + 1], S("windows_gathered"))

            def node_gather(r):
                w = sums[r].shape[1]
                g.wait_ge(PS("stored", r), 16 * (CHUNKS * (seq(r) + 1) + 1))
                g.wait_ge(S("ends_ready"), 1)
                g.wait_ge(PS("z_free", r), seq(r) + 1)
                for b in range(B):
                    gather(v3(Zflat, w)[:, b, :], sums[r], endI[:, b:b + 1], PS("nodes_gathered", r))

            for r in range(6):
                if r == 3:
                    g.wait_ge(S("table_ready"), 2)
                    g.wait_ge(S("query_zero"), 32)
                    for b in range(B):
                        g.indirect_dma_start(out=query_start, out_offset=bass.IndirectOffsetOnAxis(ap=startI[:, b:b + 1], axis=0),
                                             in_=T72[:, b, ROW2:ROW2 + HEADS], in_offset=None).then_inc(S("query_put"), 16)
                    g.wait_ge(S("query_table"), 16)
                    gather(w0[:, :], query_table, firstI[:, 0:1], S("query_first"))
                if r in GCN_NO:
                    with g.If(dense == 0):
                        edge_pass(r)
                        node_gather(r)
                else:
                    edge_pass(r)
                    node_gather(r)
                if r == 0:
                    g.wait_ge(S("flag_ready"), 1)
                    dense = g.value_load(flagI[0:1, 0:1], min_val=0, max_val=1)

        @block.tensor
        def _(pe):
            def linear(name):
                _, w, ncol = LINEARS[name]
                gs, base = groups(name), group_base[name]
                pe.wait_ge(S("in_" + name), 1)

                def turn(n):
                    q = base + n
                    if q >= LIN:
                        pe.wait_ge(S("lin_copied"), q - LIN + 1)
                    for i, u in enumerate(gs[n]):
                        last = pe.transpose(ps[:, q % LIN, i * P:(i + 1) * P], u, ident[0:P, 0:P])
                    last.then_inc(S("lin_turned"), 1)

                for n in range(LIN - 1):
                    turn(n)
                for n in range(len(gs)):
                    if n + LIN - 1 < len(gs):
                        turn(n + LIN - 1)
                    q = base + n
                    pe.wait_ge(S("lin_copied"), q + 1)
                    if q >= LIN:
                        pe.wait_ge(S("lin_taken"), q - LIN + 1)
                    for i in range(len(gs[n])):
                        last = pe.matmul(ps[0:P, LIN + q % LIN, i * ncol:(i + 1) * ncol], lin_in[q % LIN][:, i, :], w[:, 0:ncol],
                                         start=True, stop=True)
                    last.then_inc(S("lin_done"), 1)

            def crossing(r, rhs):
                w = CORRW[r]
                per = min(8, BANK // w)
                pe.wait_ge(PS("cross_in", r), seq(r) + 1)
                for b in range(B):
                    last = pe.matmul(ps[0:P, b // per, (b % per) * w:(b % per + 1) * w], cross_sel[:, b * P:(b + 1) * P], rhs,
                                     start=True, stop=True)
                last.then_inc(PS("cross_out", r), 1)

            def gcn_products(r, rhs):
                w = PASSW[r]
                with pe.If(dense == 1):
                    pe.wait_ge(S("peak_in"), seq(r) + 1)
                    pe.matmul(ps[0:P, 7, 0:P], ones[:, :], tmpf[:, 0:P], start=True, stop=True).then_inc(S("peak_out"), 1)
                    pe.wait_ge(S("parts_ready"), seq(r) + 1)
                    with pe.Fori(0, B // ABUFS) as i:
                        for k in range(ABUFS):
                            pe.wait_ge(S(f"a{k}"), (i + (seq(r) * (B // ABUFS) + 1)) * 16)
                            pe.wait_ge(S("a_taken"), i * ABUFS + (seq(r) * B + k + 1))
                            pe.sem_inc(S("a_begun"), 1)
                            for b in range(B):
                                last = pe.matmul(ps[0:P, k, 0:PARTS[w] * w], abuf[k][:, b, :],
                                                 parts(w)[:, b, :, :].rearrange("p t f -> p (t f)"), start=(b == 0), stop=(b == B - 1))
                            last.then_inc(S("a_used"), 1)
                with pe.Else():
                    crossing(r, rhs)

            def column_sums(n):
                pe.wait_ge(S("colsum_in"), n + 1)
                pe.matmul(ps[0:P, 7, 0:D], ones[:, :], nt[:, 0, :], start=True, stop=True).then_inc(S("colsum_out"), 1)

            pe.wait_ge(S("loaded_m"), 16 * 4)
            pe.wait_ge(S("pool_const"), 12)
            pe.transpose(ps[:, 6, 192:320], srcG[:, :], ident[:, :]).then_inc(S("w_turned"), 1)
            linear("message")
            pe.wait_ge(S("loaded_w"), 16 * W_LOADS)
            pe.transpose(ps[:, 6, 0:128], srcE[:, :], ident[:, :])
            pe.transpose(ps[:, 6, 128:192], srcU[:, :], ident[0:D, 0:D]).then_inc(S("w_turned"), 1)

            pe.wait_ge(S("hist_zero"), 1)
            pe.matmul(ps[0:P, 7, 0:B], hotP[0][:, 0, :], hotB[0][:, 0, :], start=True, stop=False, skip_group_check=True).then_inc(S("hist_cleared"), 1)
            pe.sem_inc(S("hot_used"), 2)
            pe.sem_inc(S("xt_turned"), 2 * BUFS)
            pe.sem_inc(S("a_used"), ABUFS)

            def turn_edges(i, k, h):
                q = (i * BUFS + k) * 2 + h
                if h == 0:
                    pe.wait_ge(S(f"xe{k % BUFS}"), (i + k // BUFS) * 16 + 16)
                pe.wait_ge(S("xt_copied"), q + 1)
                for u in HALVES[h]:
                    v = u - HALVES[h][0]
                    last = pe.transpose(ps[:, v // 4, (v % 4) * P:(v % 4 + 1) * P], xe[k % BUFS][:, u * 2 * D:(u + 1) * 2 * D], ident[0:P, 0:P])
                last.then_inc(S("xt_turned"), 1)

            def edge_products(i, k, h):
                q = (i * BUFS + k) * 2 + h
                pe.wait_ge(S("xt_copied"), q + 2)
                pe.wait_ge(S("edge_taken"), q + 1)
                for u in HALVES[h]:
                    v = u - HALVES[h][0]
                    last = pe.matmul(ps[0:P, 2 + v // 3, (v % 3) * 136:(v % 3 + 1) * 136], xT[:, u, :], WE[:, :], start=True, stop=True)
                last.then_inc(S("edge_done"), 1)

            def hist(i, k, parts):
                for part in parts:
                    pe.wait_ge(S("hot_ready"), (i * BUFS + k) * HSTEPS + (part + 1))
                    for j in range(HC):
                        last = pe.matmul(ps[0:P, 7, 0:B], hotP[part % 2][:, j, :], hotB[part % 2][:, j, :], start=False, stop=False, skip_group_check=True)
                    last.then_inc(S("hot_used"), 1)

            def windows(i, k, ws):
                for w in ws:
                    at = (i * BUFS - (FIRST_BLOCK - k)) * WINS + w
                    pair = (i * BUFS - (FIRST_BLOCK - k)) * PAIRS_W + w // 2
                    pe.wait_ge(S("winhot"), at + 1)
                    if w % 2 == 0:
                        pe.wait_ge(S("win_copied"), pair + 1)
                    bank = pair_bank(w // 2)
                    hb = winhot[HOTS if w == WINS - 1 else w % HOTS]
                    for c in range(2):
                        last = pe.matmul(ps[0:P, bank, WIN * B * (w % 2):WIN * B * (w % 2 + 1)],
                                         hb[:, 2 * WIN * B + c * P:2 * WIN * B + (c + 1) * P],
                                         hb[:, c * WIN * B:(c + 1) * WIN * B], start=(c == 0), stop=(c == 1))
                    last.then_inc(S("win_done"), 1)

            def no_side(i, k, part):
                pass

            def turn_windows():
                pe.wait_ge(S("windows_gathered"), 16 * 2 * WGROUPS)
                for n in range(WGROUPS):
                    if n >= 3:
                        pe.wait_ge(S("keys_taken"), n - 2)
                    for m in range(4):
                        last = pe.transpose(ps[0:P, 4 + n % 3, m * P:(m + 1) * P], raw[n][:, m // 2, :, m % 2], ident[0:P, 0:P])
                    last.then_inc(S("windows_turned"), 1)

            def edge_chunk(i, k, side, last=False):
                edge_products(i, k, 0)
                turn_edges(i, k, 1)
                side(i, k, SIDE[side is windows][0])
                edge_products(i, k, 1)
                if not last:
                    turn_edges(i, k + 1, 0)
                side(i, k, SIDE[side is windows][1])
                side(i, k, SIDE[side is windows][2])

            turn_edges(0, 0, 0)
            for lo, hi, side in ((0, HIST_CHUNKS // BUFS, hist), (HIST_CHUNKS // BUFS, FIRST_BLOCK // BUFS, no_side), (FIRST_BLOCK // BUFS, ITER - 1, windows)):
                if side is windows:
                    turn_windows()
                with pe.Fori(lo, hi) as i:
                    for k in range(BUFS):
                        edge_chunk(i, k, side)
                if side is hist:
                    pe.wait_ge(S("cum_in"), 1)
                    pe.matmul(ps[0:P, 7, 64:64 + B], tri_incl[:, :], deg[:, :], start=True, stop=True)
                    pe.matmul(ps[0:P, 7, 128:128 + B], ones[:, :], deg[:, :], start=True, stop=True).then_inc(S("cum_out"), 1)
                    pe.wait_ge(S("cum_in"), 2)
                    pe.matmul(ps[0:P, 7, 192:192 + B], shift4[:, :], cum[:, :], start=True, stop=True).then_inc(S("cum_out"), 1)
            for k in range(BUFS):
                edge_chunk(ITER - 1, k, windows if k + 1 < BUFS else no_side, k + 1 == BUFS)
            pe.wait_ge(S("checks_in"), 1)
            pe.matmul(ps[0:P, 7, 256:257], ones[:, :], check_parts[0][:, 0:1], start=True, stop=True).then_inc(S("checks_out"), 1)
            pe.wait_ge(S("flag_ready"), 1)
            dense = pe.value_load(flagI[0:1, 0:1], min_val=0, max_val=1)
            crossing(0, chunk3(rows, D)[:, U - 1, :])
            linear("update")
            linear("gcn11")
            gcn_products(1, chunk3(rows, 32)[:, U - 1, :])
            gcn_products(2, chunk3(rows, 32)[:, U - 1, :])
            linear("gcn12")
            linear("attend")
            pe.wait_ge(S("diag_ready"), 1)
            for m in range(6):
                last = pe.matmul(ps[0:P, m // 4, (m % 4) * P:(m % 4 + 1) * P], ones[:, :], v3(tmpf, P, 6)[:, m, :],
                                 start=True, stop=True)
            last.then_inc(S("diag_out"), 1)
            crossing(3, bnd[:, :])
            gcn_products(4, chunk3(rows, D)[:, U - 1, :])
            linear("gcn31")
            column_sums(0)
            column_sums(1)
            gcn_products(5, chunk3(rows, D)[:, U - 1, :])
            linear("gcn32")
            column_sums(2)
            column_sums(3)

        @block.scalar
        def _(act):
            def linear(name):
                base = group_base[name]
                for n, us in enumerate(groups(name)):
                    q = base + n
                    act.wait_ge(S("lin_turned"), q + 1)
                    if q >= LIN:
                        act.wait_ge(S("lin_done"), q - LIN + 1)
                    w = len(us)
                    act.copy(lin_in[q % LIN][:, 0:w, :], ps[:, q % LIN, 0:w * P].rearrange("p (u n) -> p u n", u=w)).then_inc(S("lin_copied"), 1)

            root_n = [0]

            def root(w=B):
                root_n[0] += 1
                act.wait_ge(S("root_in"), root_n[0])
                act.activation(rs_out[:, 0:w], rs_in[:, 0:w], ACT.Sqrt).then_inc(S("root_out"), 1)

            def expand(r, c, w):
                act.wait_ge(PS("keepc_ready", r), c + (seq(r) * CHUNKS + 1))
                act.copy(run3(factor, w)[:, :, 1:U + 1],
                         keepc[:, :].unsqueeze(1).to_broadcast([P, w, U])).then_inc(PS("factor_ready", r), 1)

            def store_rows(r, i, k, w):
                c = i * BUFS + k
                c1 = c + (seq(r) * CHUNKS + 1)
                act.wait_ge(PS("scanned", r), c1)
                act.wait_ge(PS("stored", r), c1 * 16)
                full = sums[r].shape[1]
                v = chunk3(rows, full)
                if full > w:
                    act.copy(v[:, :, w:full], mrun[:, :, 1:U + 1].rearrange("p h j -> p j h")).then_inc(S("rows_max"), 1)
                    act.wait_ge(S("rows_max"), c + 1)
                act.copy(v[:, :, 0:w], run3(runs, w)[:, :, 1:U + 1].rearrange("p f j -> p j f")).then_inc(PS("rows_ready", r), 1)
                act.wait_ge(PS("rows_ready", r), c + (seq(r) * CHUNKS + 2))
                act.dma_start(rowsof(r, i, k), v).then_inc(PS("stored", r), 16)

            for suffix in ("", "_gcn"):
                act.sem_inc(S("stored" + suffix), 16)
                act.sem_inc(S("rows_ready" + suffix), 1)
            for k in range(BUFS):
                act.sem_inc(S(f"block_stored{k}"), 16)
            act.sem_inc(S("win_copied"), 3)
            act.sem_inc(S("xt_copied"), 1)
            linear("message")

            def copy_turned(i, k, h):
                q = (i * BUFS + k) * 2 + h
                act.wait_ge(S("xt_turned"), q + (2 * BUFS + 1))
                act.wait_ge(S("edge_done"), q + 1)
                n, at = len(HALVES[h]), HALVES[h][0]
                act.copy(xT[:, at:at + 4, :], ps[:, 0, 0:4 * P].rearrange("p (u n) -> p u n", n=P))
                act.copy(xT[:, at + 4:at + n, :], ps[:, 1, 0:(n - 4) * P].rearrange("p (u n) -> p u n", n=P)).then_inc(S("xt_copied"), 1)

            def relu(i, k):
                v = run3(values, D)[:, :, 1:U + 1]
                act.wait_ge(S("edge_taken"), (i * BUFS + k) * 2 + 3)
                act.activation(v, v, ACT.Relu).then_inc(S("messages_ready"), 1)

            def copy_windows(i, k, pairs):
                at = (i * BUFS - (FIRST_BLOCK - k)) * WINS
                if 0 in pairs:
                    act.wait_ge(S(f"block_stored{k}"), (i - (FIRST_BLOCK // BUFS - 1)) * 16)
                for p in pairs:
                    n = min(2, WINS - 2 * p)
                    act.wait_ge(S("win_done"), at + (2 * p + n + HOTS))
                    act.sem_inc(S("copy_begun"), 1)
                    act.copy(ablock[k][:, :, 2 * p * WIN:(2 * p + n) * WIN].rearrange("p b (w d) -> p w d b", w=n),
                             ps[0:P, pair_bank(p), 0:n * WIN * B].rearrange("p (w d b) -> p w d b", w=n, d=WIN),
                             saturate=False).then_inc(S("win_copied"), 1)

            def check_counts(i, k, part):
                pairs = WIN_PAIRS[part]
                lo, hi = pairs[0] * 2 * WIN, min((pairs[-1] + 1) * 2, WINS) * WIN
                act.wait_ge(S("win_copied"), (i * BUFS - (FIRST_BLOCK - k)) * PAIRS_W + (pairs[-1] + 1 + 3))
                act.sem_inc(S("copy_begun"), 1)
                return act.activation(junk[:, :, lo:hi], ablock[k][:, :, lo:hi], ACT.Relu, bias=check_bias,
                                      accum_out=check_parts[k][:, part:part + 1], saturate=False)

            WIN_PAIRS = (range(0, 4), range(4, 8), range(8, PAIRS_W))
            act.wait_ge(S("records"), 32)
            for n in range(SEGS):
                act.dma_start(wide_records.rearrange("(m s) f -> m s f", s=SEGS)[:, n, :],
                              records[n * STEP:n * STEP + WROWS // SEGS * P, :].rearrange("(m j) v -> m (j v)", j=P)).then_inc(S("wide_records"), 16)
            def plain_chunk(i, k, last=False):
                copy_turned(i, k, 1)
                expand(0, i * BUFS + k, D)
                if not last:
                    copy_turned(i, k + 1, 0)
                relu(i, k)
                store_rows(0, i, k, D)

            def block_chunk(i, k):
                copy_turned(i, k, 1)
                expand(0, i * BUFS + k, D)
                copy_windows(i, k, WIN_PAIRS[0])
                check_counts(i, k, 0)
                copy_windows(i, k, WIN_PAIRS[1])
                copy_turned(i, k + 1, 0)
                relu(i, k)
                check_counts(i, k, 1)
                copy_windows(i, k, WIN_PAIRS[2])
                check_counts(i, k, 2).then_inc(S("checked"), 1)
                act.dma_start(adjacency[bass.ds(i * BUFS - (FIRST_BLOCK - k), 1), :, :].rearrange("a p n -> (a p) n"),
                              pairs_of_bytes(ablock_space[k])).then_inc(S(f"block_stored{k}"), 16)
                store_rows(0, i, k, D)

            copy_turned(0, 0, 0)
            for lo, hi in ((0, HIST_CHUNKS // BUFS), (HIST_CHUNKS // BUFS, FIRST_BLOCK // BUFS)):
                if lo:
                    root()
                with act.Fori(lo, hi) as i:
                    for k in range(BUFS):
                        plain_chunk(i, k)
            act.wait_ge(S("query_zero"), 32)
            with act.Fori(FIRST_BLOCK // BUFS, ITER - 1) as i:
                for k in range(BUFS):
                    block_chunk(i, k)
            for k in range(BUFS - 1):
                block_chunk(ITER - 1, k)
            plain_chunk(ITER - 1, BUFS - 1, last=True)
            act.wait_ge(S("flag_ready"), 1)
            dense = act.value_load(flagI[0:1, 0:1], min_val=0, max_val=1)
            act.wait_ge(S("x_fixed"), 1)
            act.copy(XZ[:, :, 0:D], X[:, :, :]).then_inc(S("xz_x"), 1)
            linear("update")
            root()
            linear("gcn11")
            for r in (1, 2):
                with act.If(dense == 0):
                    with act.Fori(0, ITER) as i:
                        for k in range(BUFS):
                            expand(r, i * BUFS + k, 32)
                            store_rows(r, i, k, 32)
            linear("gcn12")
            root()
            linear("attend")
            with act.Fori(0, ITER) as i:
                for k in range(BUFS):
                    c = i * BUFS + k
                    act.wait_ge(S("expo_in"), c + 1)
                    act.activation(expo[:, :, :, :], expo[:, :, :, :], ACT.Exp).then_inc(S("expo_out"), 1)
                    act.wait_ge(S("expo_out"), c + 1)
                    act.copy(run3(factor, ROW2).rearrange("p (h e) j -> p h e j", h=HEADS)[:, :, :, 1:U + 1],
                             expo[:, 0, :, :].unsqueeze(2).to_broadcast([P, HEADS, AW, U])).then_inc(S("factor_ready"), 1)
                    store_rows(3, i, k, ROW2)
            act.wait_ge(S("bexp_in"), 1)
            act.activation(bmax[:, 2, :], bmax[:, 2, :], ACT.Exp).then_inc(S("bexp_out"), 1)
            act.wait_ge(S("nexp_in"), 1)
            act.activation(Tflat[:, 0:2 * B * HEADS], Tflat[:, 0:2 * B * HEADS], ACT.Exp).then_inc(S("nexp_out"), 1)
            root()
            for r in (4, 5):
                with act.If(dense == 0):
                    with act.Fori(0, ITER) as i:
                        for k in range(BUFS):
                            expand(r, i * BUFS + k, D)
                            store_rows(r, i, k, D)
                linear("gcn31" if r == 4 else "gcn32")
                root(D)
            root()

        @block.vector
        def _(dve):
            done = [0]

            def do(ins):
                done[0] += 1
                ins.then_inc(S("dve"), 1)
                dve.wait_ge(S("dve"), done[0])

            def tell(name, n=1):
                dve.sem_inc(S(name), n)

            TT, TS, STT, CP = dve.tensor_tensor, dve.tensor_scalar, dve.scalar_tensor_tensor, dve.tensor_copy

            def over(t, w):
                return t.unsqueeze(2).to_broadcast([P, t.shape[1], w])

            def row(t, n):
                return t.unsqueeze(1).to_broadcast([P, n, t.shape[1]])

            def take(name, n, us, ins):
                dve.wait_ge(S("lin_done"), group_base[name] + n + 1)
                ins(n, us).then_inc(S("lin_taken"), 1)
                dve.wait_ge(S("lin_taken"), group_base[name] + n + 1)

            def product(name, op):
                ncol = LINEARS[name][2]
                per = 2 if len(LINEARS[name][0]) < B else 1
                for n, us in enumerate(groups(name)):
                    nb = len(us) * per
                    b0 = n * GROUP * per
                    v = ps[0:P, LIN + (group_base[name] + n) % LIN, 0:len(us) * ncol].rearrange("p (b f) -> p b f", b=nb)
                    take(name, n, us, lambda n, us: op(v, b0, nb))

            def rsqrt(t, w=B):
                do(CP(rs_in[:, 0:w], t))
                tell("root_in")
                roots[0] += 1
                dve.wait_ge(S("root_out"), roots[0])
                y, z = nt[:, 2, 0:w], nt[:, 3, 0:w]
                do(dve.reciprocal(y, rs_out[:, 0:w]))
                do(TT(z, y, y, ALU.mult))
                do(TT(z, z, rs_in[:, 0:w], ALU.mult))
                do(TS(z, z, -0.5, 1.5, ALU.mult, ALU.add))
                do(TT(t, y, z, ALU.mult))

            roots = [0]

            def layer_norm():
                m, v = nt[:, 0, 0:B], nt[:, 1, 0:B]
                do(dve.tensor_reduce(m, X[:, :, :], AX, ALU.add))
                do(TS(m, m, 1.0 / D, None, ALU.mult))
                do(TT(X[:, :, :], X[:, :, :], over(m, D), ALU.subtract))
                do(TT(tmp64, X[:, :, :], X[:, :, :], ALU.mult))
                do(dve.tensor_reduce(v, tmp64, AX, ALU.add))
                do(TS(v, v, 1.0 / D, EPS, ALU.mult, ALU.add))
                rsqrt(v)
                do(TT(X[:, :, :], X[:, :, :], over(v, D), ALU.mult))

            def copy_keep(r, i, k):
                TS(keepc[:, :], keep[:, bass.ds(i * (BUFS * U) + k * U, U)], 1.0, None, ALU.mult).then_inc(PS("keepc_ready", r), 1)

            def first_indices():
                for k in range(BUFS):
                    CP(idx[k][:, :], srcI[:, k * U:(k + 1) * U]).then_inc(S("idx_ready"), 1)
                dve.wait_ge(S("idx_ready"), BUFS)

            def next_indices(r, i, k):
                TS(idx[k][:, :], srcI[:, bass.ds(i * (BUFS * U) + (BUFS + k) * U, U)], 1, None, ALU.mult).then_inc(PS("idx_ready", r), 1)

            def scan(r, c, w):
                gc = c + (seq(r) * CHUNKS + 1)
                dve.wait_ge(PS("factor_ready", r), gc)
                dve.wait_ge(PS("rows_ready", r), gc)
                dve.wait_ge(PS("carried", r), gc)
                dve.tensor_tensor_scan(runs[:, 0:w * (U + 1)], factor[:, 0:w * (U + 1)], values[:, 0:w * (U + 1)], 0.0,
                                       ALU.mult, ALU.add).then_inc(PS("scanned", r), 1)
                dve.wait_ge(PS("scanned", r), gc)
                CP(run3(values, w)[:, :, 0:1], run3(runs, w)[:, :, U:U + 1]).then_inc(PS("carried", r), 1)

            def finish_sums(r):
                w, n0 = PASSW[r], seq(r) + 1
                dve.wait_ge(PS("rows_ready", r), n0 * CHUNKS + 1)
                dve.wait_ge(PS("carried", r), n0 * CHUNKS + 1)
                tell(("cross_in_gcn" if r in GCN_NO else "cross_in"))
                dve.wait_ge(PS("nodes_gathered", r), 16 * B * n0)
                z = v3(Zflat, w)
                do(TT(z, z, over(mask[:, :], w), ALU.mult))
                dve.wait_ge(PS("cross_out", r), n0)
                for n in range(0, B, 8):
                    m = min(8, B - n)
                    do(TT(z[:, n:n + m, :], z[:, n:n + m, :], ps[0:P, n // 8, 0:m * w].rearrange("p (b f) -> p b f", b=m), ALU.add))
                return z

            def gcn_sums(r, table):
                w, z, n0 = PASSW[r], v3(Zflat, PASSW[r]), seq(r)
                tell("z_free_gcn")
                before = done[0]
                with dve.If(dense[0] == 1):
                    t2, peak, scale, back = parts(w), nt[:, 0, 0:1], nt[:, 0, 1:2], nt[:, 0, 2:3]
                    do(dve.tensor_reduce(peak, table.rearrange("p b f -> p (b f)"), AX, ALU.max, apply_absolute_value=True))
                    do(TS(tmpf[:, 0:P], ident[0:P, 0:P], peak, None, ALU.mult))
                    tell("peak_in")
                    dve.wait_ge(S("peak_out"), n0 + 1)
                    do(dve.tensor_reduce(peak, ps[0:P, 7, 0:P], AX, ALU.max))
                    do(TS(back, peak, 1.0 / BIG, 1.0 / PEAK, ALU.max, ALU.mult))
                    do(dve.reciprocal(scale, back))
                    do(TS(t2[:, :, 0, :], table, scale, None, ALU.mult))
                    if PARTS[w] == 2:
                        do(STT(t2[:, :, 1, :], table, scale, t2[:, :, 0, :], ALU.mult, ALU.subtract))
                    else:
                        left = v3(tmpf, w)
                        do(STT(left, table, scale, t2[:, :, 0, :], ALU.mult, ALU.subtract))
                        do(CP(t2[:, :, 1, :], left))
                        do(TT(t2[:, :, 2, :], left, t2[:, :, 1, :], ALU.subtract))
                    tell("parts_ready")
                    with dve.Fori(0, B // ABUFS) as i:
                        for k in range(ABUFS):
                            n = i * ABUFS + (n0 * B + k)
                            dve.wait_ge(S("a_used"), n + (ABUFS + 1))
                            dve.wait_ge(S("z_summed"), n + 1)
                            part = rows[:, k * D:k * D + w]
                            dve.tensor_reduce(part, ps[0:P, k, 0:PARTS[w] * w].rearrange("p (t f) -> p f t", t=PARTS[w]), AX, ALU.add).then_inc(S("a_taken"), 1)
                            dve.wait_ge(S("a_taken"), n + (ABUFS + 1))
                            at = bass.ds(i * ABUFS + k, 1)
                            STT(z[:, at, :].rearrange("p a f -> p (a f)"), part, back, table[:, at, :].rearrange("p a f -> p (a f)"),
                                ALU.mult, ALU.add).then_inc(S("z_summed"), 1)
                    dve.wait_ge(S("z_summed"), (n0 + 1) * B + ABUFS)
                    dve.sem_inc(S("dve"), BRANCH - (done[0] - before))
                done[0] = before
                with dve.Else():
                    tell("table_ready_gcn")
                    do(dve.memset(values[:, :], 0.0))
                    do(dve.memset(factor[:, :], 0.0))
                    with dve.Fori(0, ITER) as i:
                        for k in range(BUFS):
                            c = i * BUFS + k
                            copy_keep(r, i, k)
                            dve.wait_ge(PS(f"gathered{k}", r), (i + (n0 * ITER + 1)) * (16 * U))
                            CP(run3(values, w)[:, :, 1:U + 1], chunk3(gath[k], w).rearrange("p j f -> p f j")).then_inc(PS("values_ready", r), 1)
                            dve.wait_ge(PS("values_ready", r), c + (n0 * CHUNKS + 1))
                            next_indices(r, i, k)
                            scan(r, c, w)
                    finish_sums(r)
                    do(TT(z, z, table, ALU.add))
                    dve.sem_inc(S("dve"), BRANCH - (done[0] - before))
                done[0] = before + BRANCH
                return z

            BRANCH = 32
            dense = [None]

            for t in (srcG, srcE, W11, W12, W31, W32, WE, WN):
                do(dve.memset(t[:, :], 0.0))
            do(dve.memset(nextI[:, :], -1))
            tell("zeroed")
            dve.wait_ge(S("pool_const"), 12)
            dve.wait_ge(S("w_turned"), 1)
            do(CP(WG[:, :], ps[:, 6, 192:320]))
            dve.wait_ge(S("loaded_m"), 16 * 4)
            tell("in_message")
            product("message", lambda v, b0, nb: TT(T64[:, b0:b0 + nb, :], v, row(bias[:, 0, :], nb), ALU.add))
            tell("table_ready")
            dve.wait_ge(S("loaded_src"), 16)
            do(CP(srcI[:, J:J + BUFS * U], srcI[:, 0:BUFS * U]))
            first_indices()

            do(dve.memset(keep[:, 0:1], 0.0))
            do(dve.memset(factor[:, :], 0.0))
            do(dve.memset(hotP[0], 0.0))
            do(dve.memset(hotB[0], 0.0))
            tell("hist_zero")
            dve.wait_ge(S("loaded_dst"), 48)
            do(CP(dstF, dstI))
            do(TT(keep[:, 1:J], dstF[:, 1:J], dstF[:, 0:J - 1], ALU.is_equal))
            q, rest, off = (spare[0:P, n * J:(n + 1) * J] for n in range(3))
            qI, srcF = tmpf[:, 0:J].bitcast(I32), tmpf[:, J:2 * J]

            def divide(t, quotient, remainder, by, q, qI, rest, off):
                do(TS(qI, t, 1.0 / by, -0.5 + 0.5 / by, ALU.mult, ALU.add))
                do(CP(q, qI))
                do(STT(rest, q, -float(by), t, ALU.mult, ALU.add))
                do(TS(off, rest, 0.0, None, ALU.is_lt))
                do(TT(q, q, off, ALU.subtract))
                do(STT(rest, off, float(by), rest, ALU.mult, ALU.add))
                do(TS(off, rest, float(by), None, ALU.is_ge))
                do(TT(quotient, q, off, ALU.add))
                do(STT(remainder, off, -float(by), rest, ALU.mult, ALU.add))

            do(CP(srcF, srcI[:, 0:J]))
            divide(srcF, srcF, edge_rec[:, :, 1], P, q, qI, rest, off)
            do(STT(edge_rec[:, :, 0], dstF, float(B), srcF, ALU.mult, ALU.add))
            do(dve.memset(keys_of[0][:, :, :], -1.0))
            tell("records_ready")
            do(dve.memset(pnode[:, J:JH], -1.0))
            do(dve.memset(bnode[:, J:JH], -1.0))
            divide(dstF, bnode[:, 0:J], pnode[:, 0:J], P, q, qI, rest, off)
            do(CP(edge_ends[:, 0:1], dstF[:, J - 1:J]))
            do(CP(edge_ends[:, 1:2], nextI[:, 0:1]))
            do(TT(edge_ends[:, 2:3], edge_ends[:, 0:1], edge_ends[:, 1:2], ALU.is_equal))
            dve.wait_ge(S("w_turned"), 2)
            for h in range(2):
                lo, hi = D * h, D * h + D
                do(CP(WE[lo:hi, 68 * h:68 * h + D], ps[lo:hi, 6, lo:hi]))
            do(CP(WU[:, :], ps[:, 6, 128:192]))
            for m, (w, t, at, step) in enumerate(((w_edge2, WE, D, 68), (w_node2, WN, D, 72), (w_node2, WN, D + HEADS, 72))):
                do(TT(wtmp[:, :], w[:, :], attn[:, m, :], ALU.mult))
                for h in range(2):
                    lo, hi = D * h, D * h + D
                    do(dve.tensor_reduce(t[lo:hi, step * h + at:step * h + at + HEADS],
                                         wtmp[lo:hi, :].rearrange("p (h d) -> p h d", h=HEADS), AX, ALU.add))
            tell("z_free")
            do(dve.memset(spare[0:P, :], 0.0))
            tell("zeros_ready")
            dve.wait_ge(S("records"), 32)

            do(dve.memset(values[:, :], 0.0))
            do(dve.memset(checks[:, :], 0.0))
            do(dve.memset(check_bias, -float(MAX_COUNT)))
            tell("checked")
            tell("check_kept")
            tell("carried")
            tell("carried_gcn")
            tell("edge_taken")
            tell("edge_done", 2)
            tell("win_done", HOTS)
            tell("idx_ready_gcn", BUFS)
            tell("a_taken", ABUFS)
            tell("z_summed", ABUFS)

            def take_edges(i, k, h):
                q = (i * BUFS + k) * 2 + h
                cols = i * (BUFS * U) + k * U
                dve.wait_ge(S("edge_done"), q + 3)
                g3 = chunk3(gath[k], D)
                banks = [(2 + b, HALVES[h][0] * 2 + 6 * b, 2 * min(3, len(HALVES[h]) - 3 * b)) for b in range(2)]
                for bank, at, n in banks:
                    v = ps[0:P, bank, 0:n * 68].rearrange("p (j f) -> p j f", j=n)
                    TS(edge_logit[:, bass.ds(cols + at, n), :], v[:, :, D:D + HEADS], 1.0, None, ALU.mult)
                if h == 0:
                    dve.wait_ge(S(f"gathered{k}"), (i + 1) * (16 * U))
                for bank, at, n in banks:
                    v = ps[0:P, bank, 0:n * 68].rearrange("p (j f) -> p f j", j=n)
                    last = TT(run3(values, D)[:, :, 1 + at:1 + at + n], g3[:, at:at + n, :].rearrange("p j f -> p f j"), v[:, 0:D, :], ALU.add)
                last.then_inc(S("edge_taken"), 1)

            def hist(i, k, parts):
                for part in parts:
                    n = (i * BUFS + k) * HSTEPS + part
                    dve.wait_ge(S("hot_used"), n + 1)
                    at = bass.ds((i * BUFS + k) * (HSTEPS * HC) + part * HC, HC)
                    TT(hotP[part % 2], pnode[:, at].unsqueeze(2).to_broadcast([P, HC, P]),
                       iotaP[:, :].unsqueeze(1).to_broadcast([P, HC, P]), ALU.is_equal)
                    TT(hotB[part % 2], bnode[:, at].unsqueeze(2).to_broadcast([P, HC, B]),
                       iotaB[:, :].unsqueeze(1).to_broadcast([P, HC, B]), ALU.is_equal).then_inc(S("hot_ready"), 1)

            def take_keys():
                for n in range(WGROUPS):
                    dve.wait_ge(S("windows_turned"), n + 1)
                    turned = ps[0:P, 4 + n % 3, 0:4 * P].rearrange("p (c v w) -> p w c v", c=2, v=2)
                    k4 = keys[:, n * 4 * P:(n + 1) * 4 * P].rearrange("p (w c v) -> p w c v", c=2, v=2)
                    CP(k4[:, :, :, 1], turned[:, :, :, 1])
                    STT(k4[:, :, :, 0], turned[:, :, :, 0], -float(n * P * WIN * B), win_off[:, :].unsqueeze(2).to_broadcast([P, P, 2]),
                        ALU.add, ALU.subtract).then_inc(S("keys_taken"), 1)
                dve.wait_ge(S("keys_taken"), WGROUPS)

            def window_keys(i, k):
                n = i * BUFS - (FIRST_BLOCK - k)
                TS(keys_all[:, k % BUFS * (WINS * 4):(k % BUFS + 1) * (WINS * 4)], keys[:, bass.ds(n * (WINS * 4), WINS * 4)], 1.0, None, ALU.mult).then_inc(S("keys_ready"), 1)

            def windows(i, k, ws):
                for w in ws:
                    at = (i * BUFS - (FIRST_BLOCK - k)) * WINS + w
                    dve.wait_ge(S("win_done"), at + 1)
                    hb = winhot[HOTS if w == WINS - 1 else w % HOTS]
                    for c in range(2):
                        TS(hb[:, c * WIN * B:(c + 1) * WIN * B], iotaW[:, :], keys_of[k][:, w, 2 * c:2 * c + 1], None, ALU.is_equal)
                        last = TS(hb[:, 2 * WIN * B + c * P:2 * WIN * B + (c + 1) * P], iotaP[:, :], keys_of[k][:, w, 2 * c + 1:2 * c + 2], None, ALU.is_equal)
                    last.then_inc(S("winhot"), 1)

            def keep_checks(n, k):
                dve.wait_ge(S("checked"), n + 1)
                dve.wait_ge(S("check_kept"), n + 1)
                TT(check_max, check_max, check_parts[k], ALU.max).then_inc(S("check_kept"), 1)

            dve.wait_ge(S("hist_cleared"), 1)
            def no_side(i, k, part):
                pass

            def edge_chunk(i, k, side, more=True):
                c = i * BUFS + k
                steps = SIDE[side is windows]
                if side is windows:
                    dve.wait_ge(S("keys_ready"), c - (FIRST_BLOCK - 1))
                copy_keep(0, i, k)
                side(i, k, steps[0])
                take_edges(i, k, 0)
                side(i, k, steps[1])
                take_edges(i, k, 1)
                side(i, k, steps[2][:1])
                dve.wait_ge(S("edge_taken"), c * 2 + 3)
                next_indices(0, i, k)
                side(i, k, steps[2][1:])
                if side is windows:
                    if more:
                        window_keys(i, k + 1)
                    keep_checks(c - FIRST_BLOCK, k - 1)
                dve.wait_ge(S("messages_ready"), c + 1)
                scan(0, c, D)

            for lo, hi, side in ((0, HIST_CHUNKS // BUFS, hist), (HIST_CHUNKS // BUFS, FIRST_BLOCK // BUFS, no_side), (FIRST_BLOCK // BUFS, ITER - 1, windows)):
                if side is windows:
                    take_keys()
                    window_keys(lo, 0)
                with dve.Fori(lo, hi) as i:
                    for k in range(BUFS):
                        edge_chunk(i, k, side)
                if side is not hist:
                    continue
                dve.wait_ge(S("hot_used"), HIST_CHUNKS * HSTEPS + 2)
                do(CP(deg[:, :], ps[0:P, 7, 0:B]))
                tell("cum_in")
                dve.wait_ge(S("cum_out"), 1)
                tot, before_block, first = nt[:, 0, 0:B], nt[:, 1, 0:B], nt[:, 2, 0:B]
                do(CP(tot, ps[0:P, 7, 128:128 + B]))
                do(dve.tensor_tensor_scan(before_block, ones[:, 0:B], tot, 0.0, ALU.mult, ALU.add))
                do(TT(before_block, before_block, tot, ALU.subtract))
                do(TT(cum[:, :], ps[0:P, 7, 64:64 + B], before_block, ALU.add))
                tell("cum_in")
                do(TT(first, cum[:, :], deg[:, :], ALU.subtract))
                before = rs_in[:, 0:B]
                divide(first, tot, before, STEP, nt[:, 3, 0:B], startnI[:, :], before, rs_out[:, 0:B])
                do(CP(startnI[:, :], tot))
                tell("starts_ready")
                dve.wait_ge(S("cum_out"), 2)
                do(TT(tot, ps[0:P, 7, 192:192 + B], first, ALU.subtract))
                do(TT(tot, tot, before, ALU.add))
                do(TS(tot, tot, float(WIN_EDGES), None, ALU.is_gt))
                do(dve.tensor_reduce(checks[:, 0:1], tot, AX, ALU.max))
                do(TS(endI[:, :], cum[:, :], -1.0, 0.0, ALU.add, ALU.max))
                tell("ends_ready")
                do(TS(mask[:, :], deg[:, :], 1.0, None, ALU.min))
                do(TT(first, first, mask[:, :], ALU.mult))
                do(TS(tot, mask[:, :], -1.0, 1.0, ALU.mult, ALU.add))
                do(TS(before_block, node_no[:, :], float(E), None, ALU.add))
                do(TT(tot, tot, before_block, ALU.mult))
                do(TT(startI[:, :], first, tot, ALU.add))
                do(TS(dis[:, :], deg[:, :], 1.0, None, ALU.add))
                rsqrt(dis[:, :])
            for k in range(BUFS):
                edge_chunk(ITER - 1, k, windows if k + 1 < BUFS else no_side, k + 2 < BUFS)
            tell("x_fixed")
            dve.wait_ge(S("win_copied"), B * PAIRS_W + 3)
            for k in range(BUFS):
                dve.wait_ge(S(f"block_stored{k}"), 16 * (len(range(k, B, BUFS)) + 1))
            dve.wait_ge(S("win_done"), B * WINS + HOTS)
            keep_checks(B, (B - 1) % BUFS)
            dve.wait_ge(S("check_kept"), B + 2)
            do(dve.tensor_reduce(check_parts[0][:, 0:1], check_max, AX, ALU.max))
            tell("checks_in")
            dve.wait_ge(S("checks_out"), 1)
            do(TS(flagI[:, :], ps[0:P, 7, 256:257], FLAG_AT, None, ALU.is_le))
            tell("flag_ready")
            dense[0] = dve.value_load(flagI[0:1, 0:1], min_val=0, max_val=1)
            end_in_block = nt[:, 0, 0:B]
            do(TS(end_in_block, iotaB[:, :], -float(P), edge_ends[:, 0:1], ALU.mult, ALU.add))
            for b in range(B):
                last = TS(cross_sel[:, b * P:(b + 1) * P], iotaP[:, :], end_in_block[:, b:b + 1], edge_ends[:, 2:3], ALU.is_equal, ALU.mult)
            do(last)

            finish_sums(0)
            z = v3(Zflat, D)
            dve.wait_ge(S("xz_x"), 1)
            do(CP(XZ[:, :, D:2 * D], z))
            tell("z_free")
            tell("in_update")
            product("update", lambda v, b0, nb: TT(tmp64[:, b0:b0 + nb, :], v, row(bias[:, 1, :], nb), ALU.add))
            do(STT(X[:, :, :], tmp64, 0.0, X[:, :, :], ALU.max, ALU.add))
            layer_norm()

            tell("in_gcn11")
            product("gcn11", lambda v, b0, nb: TT(T32[:, b0:b0 + nb, :], v, over(dis[:, b0:b0 + nb], 32), ALU.mult))
            z = gcn_sums(1, T32)
            do(TT(z, z, over(dis[:, :], 32), ALU.mult))
            do(TT(z, z, row(bias[:, 2, 0:32], B), ALU.add))
            do(STT(T32, z, 0.0, over(dis[:, :], 32), ALU.max, ALU.mult))
            z = gcn_sums(2, T32)
            do(dve.memset(tmp64, 0.0))
            do(TT(tmp64[:, :, 0:32], z, over(dis[:, :], 32), ALU.mult))
            tell("in_gcn12")
            product("gcn12", lambda v, b0, nb: TT(X[:, b0:b0 + nb, :], X[:, b0:b0 + nb, :], v, ALU.add))
            do(TT(X[:, :, :], X[:, :, :], row(bias[:, 3, :], B), ALU.add))
            layer_norm()

            tell("in_attend")
            product("attend", lambda v, b0, nb: CP(T72[:, b0:b0 + nb, :], v))
            tell("table_ready")
            dve.wait_ge(S("query_back"), 16)
            dve.wait_ge(S("query_first"), 16)
            do(CP(query[:, 0, :], w0[:, :]))
            for h in range(HEADS):
                do(dve.tensor_tensor_scan(query[:, :, h], keep[:, :], query[:, :, h], 0.0, ALU.mult, ALU.add))
            do(TT(edge_logit[:, :, :], edge_logit[:, :, :], query, ALU.add))
            do(dve.memset(values[:, :], 0.0))
            do(dve.memset(factor[:, :], 0.0))
            do(dve.memset(mrun[:, :, :], -BIG))
            loop_base, STEPS = done[0], 14
            with dve.Fori(0, ITER) as i:
                for k in range(BUFS):
                    c = i * BUFS + k
                    n = [0]

                    def ldo(ins):
                        n[0] += 1
                        ins.then_inc(S("dve"), 1)
                        dve.wait_ge(S("dve"), c * STEPS + (loop_base + n[0]))

                    cols = bass.ds(i * (BUFS * U) + k * U, U)
                    dve.wait_ge(S(f"gathered{k}"), (i + (ITER + 1)) * (16 * U))
                    g3 = chunk3(gath[k], ROW2)
                    ldo(TT(logit[:, :, :], edge_logit[:, cols, :], g3[:, :, D:ROW2], ALU.add))
                    ldo(STT(logitT[:, :, :].rearrange("p h j -> p j h"), logit[:, :, :], 0.01, logit[:, :, :], ALU.mult, ALU.max))
                    ldo(TS(keepn[:, :], keep[:, cols], -1.0, BIG, ALU.add, ALU.mult))
                    dve.wait_ge(S("rows_ready"), c + (CHUNKS + 1))
                    for h in range(HEADS):
                        ldo(dve.tensor_tensor_scan(mrun[:, h, 1:U + 1], keepn[:, :], logitT[:, h, :], mrun[:, h, 0:1], ALU.add, ALU.max))
                    ldo(TT(expo[:, 0, :, :], mrun[:, :, 0:U], keepn[:, :].unsqueeze(1).to_broadcast([P, HEADS, U]), ALU.add))
                    ldo(TT(expo[:, 0, :, :], expo[:, 0, :, :], mrun[:, :, 1:U + 1], ALU.subtract))
                    TT(expo[:, 1, :, :], logitT[:, :, :], mrun[:, :, 1:U + 1], ALU.subtract).then_inc(S("expo_in"), 1)
                    dve.wait_ge(S("expo_in"), c + 1)
                    dve.wait_ge(S("expo_out"), c + 1)
                    v4 = run3(values, ROW2).rearrange("p (h e) j -> p h e j", h=HEADS)
                    for h in range(HEADS):
                        ins = TT(v4[:, h, 0:HD, 1:U + 1], g3[:, :, h * HD:(h + 1) * HD].rearrange("p j d -> p d j"),
                                 expo[:, 1, h, :].unsqueeze(1).to_broadcast([P, HD, U]), ALU.mult)
                        if h < HEADS - 1:
                            ldo(ins)
                        else:
                            ins.then_inc(S("values_ready"), 1)
                            dve.wait_ge(S("values_ready"), c + 1)
                    ldo(CP(v4[:, :, HD, 1:U + 1], expo[:, 1, :, :]))
                    next_indices(3, i, k)
                    scan(3, c, ROW2)
                    dve.wait_ge(S("rows_ready"), c + (CHUNKS + 2))
                    ldo(CP(mrun[:, :, 0:1], mrun[:, :, U:U + 1]))
                    assert n[0] == STEPS
            done[0] = loop_base + CHUNKS * STEPS
            dve.wait_ge(S("carried"), 2 * CHUNKS + 1)
            last_row = chunk3(rows, ROW2 + HEADS)[:, U - 1, :]
            dm = v3(tmpf, P, 6)
            for m in range(6):
                col = last_row[:, ROW2 + m:ROW2 + m + 1] if m < HEADS else edge_ends[:, (0, 2)[m - HEADS]:(0, 2)[m - HEADS] + 1]
                do(TS(dm[:, m, :], ident[0:P, 0:P], col, None, ALU.mult))
            tell("diag_ready")
            dve.wait_ge(S("diag_out"), 1)
            same, t2 = dm[:, 0, :], dm[:, 1, :]
            do(TS(same, ps[0:P, 1, 0:P], edge_ends[:, 0:1], None, ALU.is_equal))
            do(TT(same, same, ps[0:P, 1, P:2 * P], ALU.mult))
            for h in range(HEADS):
                do(TT(t2, same, ps[0:P, 0, h * P:(h + 1) * P], ALU.mult))
                do(TS(dm[:, 2, :], same, -1.0, BIG, ALU.add, ALU.mult))
                do(TT(t2, t2, dm[:, 2, :], ALU.add))
                do(dve.tensor_reduce(bmax[:, 0, h:h + 1], t2, AX, ALU.max))
            do(TT(t2, same, tri[:, :], ALU.mult))
            do(dve.tensor_reduce(edge_ends[:, 3:4], t2, AX, ALU.max))
            do(TS(edge_ends[:, 3:4], edge_ends[:, 3:4], -1.0, 1.0, ALU.mult, ALU.add))
            do(TT(edge_ends[:, 3:4], edge_ends[:, 3:4], edge_ends[:, 2:3], ALU.mult))
            do(TT(bmax[:, 2, :], last_row[:, ROW2:ROW2 + HEADS], bmax[:, 0, :], ALU.subtract))
            do(TS(bmax[:, 2, :], bmax[:, 2, :], 0.0, None, ALU.min))
            tell("bexp_in")
            dve.wait_ge(S("bexp_out"), 1)
            do(TT(bnd[:, 0:ROW2].rearrange("p (h e) -> p h e", h=HEADS), last_row[:, 0:ROW2].rearrange("p (h e) -> p h e", h=HEADS),
                  bmax[:, 2, :].unsqueeze(2).to_broadcast([P, HEADS, AW]), ALU.mult))
            do(TS(bnd[:, ROW2:ROW2 + HEADS], bmax[:, 0, :], edge_ends[:, 3:4], None, ALU.mult))
            do(CP(bnd[:, ROW2 + HEADS:ROW2 + HEADS + 1], edge_ends[:, 3:4]))
            tell("cross_in")
            dve.wait_ge(S("cross_out"), 2)
            CW = CORRW[3]
            cr = v3(tmpf, CW)
            per = BANK // CW
            for n in range(0, B, per):
                m = min(per, B - n)
                do(CP(cr[:, n:n + m, :], ps[0:P, n // per, 0:m * CW].rearrange("p (b f) -> p b f", b=m)))
            dve.wait_ge(S("nodes_gathered"), 16 * B * 2)
            z = v3(Zflat, ROW2 + HEADS)
            e1, e2 = v3(Tflat, HEADS), Tflat[:, B * HEADS:2 * B * HEADS].rearrange("p (b h) -> p b h", b=B)
            mx = Tflat[:, 2 * B * HEADS:3 * B * HEADS].rearrange("p (b h) -> p b h", b=B)
            has = nt[:, 0, 0:B]
            do(TS(has, cr[:, :, ROW2 + HEADS], -1.0, BIG, ALU.add, ALU.mult))
            do(TT(e2, cr[:, :, ROW2:ROW2 + HEADS], over(has, HEADS), ALU.add))
            do(TT(mx, z[:, :, ROW2:ROW2 + HEADS], e2, ALU.max))
            do(TT(e1, z[:, :, ROW2:ROW2 + HEADS], mx, ALU.subtract))
            do(TT(e2, e2, mx, ALU.subtract))
            tell("nexp_in")
            dve.wait_ge(S("nexp_out"), 1)
            for h in range(HEADS):
                zh, ch = z[:, :, h * AW:(h + 1) * AW], cr[:, :, h * AW:(h + 1) * AW]
                do(TT(zh, zh, over(e1[:, :, h], AW), ALU.mult))
                do(TT(ch, ch, over(e2[:, :, h], AW), ALU.mult))
                do(TT(zh, zh, ch, ALU.add))
                rd = nt[:, 1, 0:B]
                do(dve.reciprocal(rd, zh[:, :, HD]))
                do(TT(rd, rd, mask[:, :], ALU.mult))
                do(TT(zh[:, :, 0:HD], zh[:, :, 0:HD], over(rd, HD), ALU.mult))
                xh = X[:, :, h * HD:(h + 1) * HD]
                do(STT(xh, xh, 2.0, zh[:, :, 0:HD], ALU.mult, ALU.add))
            do(TT(X[:, :, :], X[:, :, :], row(bias[:, 4, :], B), ALU.add))
            layer_norm()

            for n in range(2):
                r = 4 + n
                b_, gamma, beta = bias[:, 5 + 3 * n, :], bias[:, 6 + 3 * n, :], bias[:, 7 + 3 * n, :]
                do(TT(T64, X[:, :, :] if n == 0 else T64, over(dis[:, :], D), ALU.mult))
                z = gcn_sums(r, T64)
                do(TT(tmp64, z, over(dis[:, :], D), ALU.mult))
                name = ("gcn31", "gcn32")[n]
                tell("in_" + name)
                product(name, lambda v, b0, nb: TT(T64[:, b0:b0 + nb, :], v, row(b_, nb), ALU.add))
                s0, s1 = nt[:, 0, :], nt[:, 1, :]
                for m in range(2):
                    if m == 0:
                        do(dve.tensor_reduce(s0, T64.rearrange("p b f -> p f b"), AX, ALU.add))
                    else:
                        do(TT(tmp64, T64, T64, ALU.mult))
                        do(dve.tensor_reduce(s0, tmp64.rearrange("p b f -> p f b"), AX, ALU.add))
                    tell("colsum_in")
                    dve.wait_ge(S("colsum_out"), 2 * n + m + 1)
                    do(TS(s1, ps[0:P, 7, 0:D], 1.0 / N, EPS * m, ALU.mult, ALU.add))
                    if m == 0:
                        do(TT(T64, T64, row(s1, B), ALU.subtract))
                rsqrt(s1, D)
                do(TT(s1, s1, gamma, ALU.mult))
                do(TT(T64, T64, row(s1, B), ALU.mult))
                do(TT(T64, T64, row(beta, B), ALU.add))
                do(STT(T64, T64, 0.01, T64, ALU.mult, ALU.max))
            do(TT(X[:, :, :], X[:, :, :], T64, ALU.add))
            layer_norm()
            tell("result")


def kernel(**inputs):
    import numpy as np
    import concourse.bacc as bacc
    from concourse.bass_utils import run_bass_kernel_spmd as run

    nc = bacc.Bacc("TRN2", target_bir_lowering=False, num_devices=1)
    arrays, args = {}, {}
    for name, value in inputs.items():
        v = np.ascontiguousarray(value)
        arrays[name] = v
        args[name] = nc.dram_tensor(name, v.shape, mybir.dt.from_np(v.dtype), kind="ExternalInput").ap()
    out = nc.dram_tensor("out", inputs["x"].shape, F32, kind="ExternalOutput").ap()
    gnn_kernel(nc, args, out)
    r = run(nc, [arrays], core_ids=[0])
    return r.results[0]["out"]
```
